# Optimizing a Trainium2 kernel written in Bass

```python
import numpy as np
import jax
import jax.numpy as jnp

def _softmax(x, axis=-1):
    return jax.nn.softmax(x, axis=axis)

def _gelu(x):
    return jax.nn.gelu(x, approximate=True)

def _silu(x):
    return jax.nn.silu(x)

def _sigmoid(x):
    return jax.nn.sigmoid(x)

def _layernorm(x, axis=-1, eps=1e-05):
    m = jnp.mean(x, axis=axis, keepdims=True)
    v = jnp.var(x, axis=axis, keepdims=True)
    return (x - m) / jnp.sqrt(v + eps)

def _scatter_add(tgt, idx, src, axis=0):
    return tgt.at[idx].add(src)

def _segment_sum(src, seg, n):
    return jax.ops.segment_sum(src, seg, n)
kernel_name = 'mk_xattn_ffn_d4_seqx_r8_d430e4'

def setup_inputs(seed: int=0):
    np.random.seed(seed)
    _w = jnp.asarray

    def _rec_inputs():
        import jax
        import jax.numpy as jnp
        _rk = jax.random.key(seed)
        x = -0.0003929 + 0.9999 * jax.random.normal(jax.random.fold_in(_rk, 1), (2, 256, 512), jnp.float32)
        _lenS = 256 - jax.random.randint(jax.random.fold_in(_rk, 7), (2,), 0, max(1, 256 // 4) + 1, jnp.int32)
        _lenS2 = 512 - jax.random.randint(jax.random.fold_in(_rk, 8), (2,), 0, max(1, 512 // 4) + 1, jnp.int32)
        pos_BxS = jnp.broadcast_to(jnp.arange(256, dtype=jnp.int32), (2, 256))
        _ctx_1024P = jax.random.normal(jax.random.fold_in(_rk, 12), (2, 16, 128), jnp.float32)
        _ctx_1024c = jax.random.dirichlet(jax.random.fold_in(_rk, 512), 0.3 * jnp.ones((16,), jnp.float32), (2, 512))
        _ctx_1024t = jnp.einsum('bsk,bkd->bsd', _ctx_1024c, _ctx_1024P)
        _ctx_1024t = _ctx_1024t * jax.lax.rsqrt(jnp.mean(jnp.square(_ctx_1024t)) + 1e-12) * 0.953939
        ctx_1024 = 6.77073e-06 + 0.0199965 * (_ctx_1024t + 0.3 * jax.random.normal(jax.random.fold_in(_rk, 612), (2, 512, 128), jnp.float32))
        _validS = jnp.arange(256)[None, :] < _lenS[:, None]
        _validS2 = jnp.arange(512)[None, :] < _lenS2[:, None]
        _causal = jnp.tril(jnp.ones((256, 256), dtype=bool))
        mask_SxS2_ff0 = jnp.where(jnp.ones((256, 512), dtype=bool), 0.0, -1000000000.0).astype(jnp.float32)
        return (x, pos_BxS, ctx_1024, mask_SxS2_ff0)
    x, pos_BxS, ctx_1024, mask_SxS2_ff0 = _rec_inputs()

    def _L0_xattn_setup():
        import jax, jax.numpy as jnp
        import numpy as np
        H = 128
        C = 4
        RH = 16
        HS = H // RH
        DR = 8
        M = 512
        NH = 16
        HD = H // NH
        A_SIZE = (C - 1) * RH
        B_SIZE = C * RH
        EPS = 1e-05
        SSM_EPS = 1e-05

        def rat_read(res, W, gamma, beta, num_outputs):
            b, l, _ = res.shape
            x = res.reshape(b, l, H, C)
            y = jnp.einsum('blhc,hoc->bloh', x, W)
            mu = y.mean(-1, keepdims=True)
            var = y.var(-1, keepdims=True)
            yn = (y - mu) * jax.lax.rsqrt(var + EPS)
            yn = yn * gamma.reshape(num_outputs, H) + beta.reshape(num_outputs, H)
            return yn.reshape(b, l, num_outputs * H)

        def rope(x, pos):
            half = HD // 2
            inv = 1.0 / 10000.0 ** (jnp.arange(half, dtype=jnp.float32) / half)
            ang = pos.astype(jnp.float32)[..., None] * inv
            cos = jnp.cos(ang)[:, :, None, :]
            sin = jnp.sin(ang)[:, :, None, :]
            x1, x2 = (x[..., :half], x[..., half:])
            return jnp.concatenate([x1 * cos - x2 * sin, x2 * cos + x1 * sin], axis=-1)

        def attention(qkv_in, qkv_w, pos):
            b, l, _ = qkv_in.shape
            q, k, v = jnp.split(qkv_in, 3, axis=-1)
            q = jnp.einsum('bli,oi->blo', q, qkv_w[0]).reshape(b, l, NH, HD)
            k = jnp.einsum('bli,oi->blo', k, qkv_w[1]).reshape(b, l, NH, HD)
            v = jnp.einsum('bli,oi->blo', v, qkv_w[2]).reshape(b, l, NH, HD)
            q = rope(q, pos)
            k = rope(k, pos)
            scores = jnp.einsum('bqhd,bkhd->bhqk', q, k) / np.sqrt(HD).astype(np.float32)
            mask = jnp.tril(jnp.ones((l, l), dtype=bool))
            scores = jnp.where(mask, scores, jnp.float32(-1e+30))
            p = jax.nn.softmax(scores, axis=-1)
            o = jnp.einsum('bhqk,bkhd->bqhd', p, v)
            return o.reshape(b, l, H)

        def rat_write(res, y, wod_w, wab_w, wab_b, du_w, du_b):
            b, l, _ = res.shape
            o_d = y @ wod_w.T
            A_B = y @ wab_w.T + wab_b
            out = o_d[..., :H]
            delta_low = o_d[..., H:]
            A_logit = A_B[..., :A_SIZE]
            B_proj = A_B[..., A_SIZE:2 * A_SIZE]
            B_skip = A_B[..., 2 * A_SIZE:]
            delta = jax.nn.softplus(delta_low @ du_w.T + du_b)
            hs = res.reshape(b, l, HS, RH, C)
            out = out.reshape(b, l, HS, RH, 1)
            delta = delta.reshape(b, l, HS, RH, 1)
            A_logit = A_logit.reshape(b, l, 1, RH, C - 1)
            B_proj = B_proj.reshape(b, l, 1, RH, C - 1)
            B_skip = B_skip.reshape(b, l, 1, RH, 1)
            A_neg = -jax.nn.softplus(A_logit)
            A_bar = jnp.exp(delta * A_neg)
            B_bar = (A_bar - 1.0) / (A_neg - SSM_EPS) * B_proj
            B_bar_skip = delta * B_skip
            A_full = jnp.concatenate([A_bar, jnp.ones_like(A_bar[..., :1])], axis=-1)
            B_full = jnp.concatenate([B_bar, B_bar_skip], axis=-1)
            return (hs * A_full + out * B_full).reshape(b, l, H * C)

        def layer_forward(hidden_states, position_ids, attn_read_w, attn_read_g, attn_read_b, qkv_w, attn_wod_w, attn_wab_w, attn_wab_b, attn_du_w, attn_du_b, mlp_read_w, mlp_read_g, mlp_read_b, mlp_in_w, mlp_wod_w, mlp_wab_w, mlp_wab_b, mlp_du_w, mlp_du_b):
            qkv_in = rat_read(hidden_states, attn_read_w, attn_read_g, attn_read_b, 3)
            attn_out = attention(qkv_in, qkv_w, position_ids)
            hidden_states = rat_write(hidden_states, attn_out, attn_wod_w, attn_wab_w, attn_wab_b, attn_du_w, attn_du_b)
            mlp_in = rat_read(hidden_states, mlp_read_w, mlp_read_g, mlp_read_b, 2)
            g_in, u_in = (mlp_in[..., :H], mlp_in[..., H:])
            gate = jnp.einsum('bli,oi->blo', g_in, mlp_in_w[0])
            up = jnp.einsum('bli,oi->blo', u_in, mlp_in_w[1])
            mlp_out = jax.nn.silu(gate) * up
            hidden_states = rat_write(hidden_states, mlp_out, mlp_wod_w, mlp_wab_w, mlp_wab_b, mlp_du_w, mlp_du_b)
            return hidden_states
        key = jax.random.key(seed)
        ks = jax.random.split(key, 20)
        B, L = (2, 256)
        s = 0.02
        return {'hidden_states': jax.random.normal(ks[0], (B, L, H * C), jnp.float32), 'position_ids': jnp.tile(jnp.arange(L, dtype=jnp.int64), (B, 1)), 'attn_read_w': jax.random.normal(ks[1], (H, 3, C), jnp.float32) / np.sqrt(C).astype(np.float32), 'attn_read_g': jnp.ones((3 * H,), jnp.float32), 'attn_read_b': jnp.zeros((3 * H,), jnp.float32), 'qkv_w': jax.random.normal(ks[2], (3, H, H), jnp.float32) * s, 'attn_wod_w': jax.random.normal(ks[3], (H + DR, H), jnp.float32) * s, 'attn_wab_w': jax.random.normal(ks[4], (A_SIZE + B_SIZE, H), jnp.float32) * s, 'attn_wab_b': jax.random.normal(ks[5], (A_SIZE + B_SIZE,), jnp.float32) * s, 'attn_du_w': jax.random.normal(ks[6], (H, DR), jnp.float32) * s, 'attn_du_b': jax.random.normal(ks[7], (H,), jnp.float32) * s, 'mlp_read_w': jax.random.normal(ks[8], (H, 2, C), jnp.float32) / np.sqrt(C).astype(np.float32), 'mlp_read_g': jnp.ones((2 * H,), jnp.float32), 'mlp_read_b': jnp.zeros((2 * H,), jnp.float32), 'mlp_in_w': jax.random.normal(ks[9], (2, M, H), jnp.float32) * s, 'mlp_wod_w': jax.random.normal(ks[10], (H + DR, M), jnp.float32) * s, 'mlp_wab_w': jax.random.normal(ks[11], (A_SIZE + B_SIZE, M), jnp.float32) * s, 'mlp_wab_b': jax.random.normal(ks[12], (A_SIZE + B_SIZE,), jnp.float32) * s, 'mlp_du_w': jax.random.normal(ks[13], (H, DR), jnp.float32) * s, 'mlp_du_b': jax.random.normal(ks[14], (H,), jnp.float32) * s}
    _L0_xattn_all = _L0_xattn_setup()
    _L0_xattn_in = {k: v for k, v in _L0_xattn_all.items() if k in ('attn_read_w', 'attn_read_g', 'attn_read_b', 'qkv_w', 'attn_wod_w', 'attn_wab_w', 'attn_wab_b', 'attn_du_w', 'attn_du_b', 'mlp_read_w', 'mlp_read_g', 'mlp_read_b', 'mlp_wod_w', 'mlp_wab_w', 'mlp_wab_b', 'mlp_du_w', 'mlp_du_b')}
    del _L0_xattn_all

    def _L0_ffn_setup():
        import jax, jax.numpy as jnp
        import numpy as np
        H = 512
        I = 1376
        R = 32
        NLEV = 16
        Q_ZERO = 7.5
        Q_STEP = 0.005
        LR_SCALE = 0.02

        def _qlinear(x, q, scale, A, Bm):
            w = (q.astype(jnp.float32) - Q_ZERO) * (scale * Q_STEP)[:, None]
            y = jnp.einsum('bsh,oh->bso', x, w)
            return y + LR_SCALE * (x @ A @ Bm)
        key = jax.random.key(seed)
        ks = jax.random.split(key, 13)
        B, S = (2, 256)
        inp = {'x': jax.random.normal(ks[0], (B, S, H), jnp.float32), 'gate_q': jax.random.randint(ks[1], (I, H), 0, NLEV, jnp.int32), 'gate_scale': jax.random.uniform(ks[2], (I,), jnp.float32), 'gate_A': jax.random.normal(ks[3], (H, R), jnp.float32), 'gate_B': jax.random.normal(ks[4], (R, I), jnp.float32), 'up_q': jax.random.randint(ks[5], (I, H), 0, NLEV, jnp.int32), 'up_scale': jax.random.uniform(ks[6], (I,), jnp.float32), 'up_A': jax.random.normal(ks[7], (H, R), jnp.float32), 'up_B': jax.random.normal(ks[8], (R, I), jnp.float32), 'down_q': jax.random.randint(ks[9], (H, I), 0, NLEV, jnp.int32), 'down_scale': jax.random.uniform(ks[10], (H,), jnp.float32), 'down_A': jax.random.normal(ks[11], (I, R), jnp.float32), 'down_B': jax.random.normal(ks[12], (R, H), jnp.float32)}
        return inp
    _L0_ffn_all = _L0_ffn_setup()
    _L0_ffn_in = {k: v for k, v in _L0_ffn_all.items() if k in ('gate_q', 'gate_scale', 'gate_A', 'gate_B', 'up_q', 'up_scale', 'up_A', 'up_B', 'down_q', 'down_scale', 'down_A', 'down_B')}
    del _L0_ffn_all

    def _L1_xattn_setup():
        import math
        import jax, jax.numpy as jnp
        import numpy as np
        N_HEADS = 32
        N_KV_HEADS = 8
        N_REP = N_HEADS // N_KV_HEADS
        HEAD_DIM = 512 // N_HEADS
        key = jax.random.key(seed)
        kq, kk, kv = jax.random.split(key, 3)
        B, S, T = (2, 256, 256)
        q = jax.random.normal(kq, (B, S, N_HEADS * HEAD_DIM), dtype=jnp.float32)
        k = jax.random.normal(kk, (B, T, N_KV_HEADS * HEAD_DIM), dtype=jnp.float32)
        v = jax.random.normal(kv, (B, T, N_KV_HEADS * HEAD_DIM), dtype=jnp.float32)
        mask = jnp.zeros((S, T), dtype=jnp.float32)
        return {'q': q, 'k': k, 'v': v, 'start_pos': 0, 'mask': mask}
    _L1_xattn_all = _L1_xattn_setup()
    _L1_xattn_in = {k: v for k, v in _L1_xattn_all.items() if k in ()}
    del _L1_xattn_all

    def _L1_ffn_setup():
        import jax, jax.numpy as jnp
        import numpy as np
        BATCH, TOK, DIM, OUT = (4, 256, 512, 512)
        E, R, TOP_K = (8, 16, 2)
        SCALING = 16.0 / R
        key = jax.random.key(seed)
        ks = jax.random.split(key, 6)
        return {'x': jax.random.normal(ks[0], (BATCH, TOK, DIM), dtype=jnp.float32), 'W_base': jax.random.normal(ks[1], (OUT, DIM), dtype=jnp.float32) / np.sqrt(DIM), 'b_base': jax.random.normal(ks[2], (OUT,), dtype=jnp.float32) * 0.01, 'W_gate': jax.random.normal(ks[3], (E, DIM), dtype=jnp.float32) * 0.01, 'A': jax.random.normal(ks[4], (E, R, DIM), dtype=jnp.float32) / np.sqrt(DIM), 'B': jax.random.normal(ks[5], (OUT, OUT // OUT * R * 0 + R), dtype=jnp.float32)[None].repeat(E, 0) * 0.0 + jax.random.normal(ks[5], (E, OUT, R), dtype=jnp.float32) * 0.02}
    _L1_ffn_all = _L1_ffn_setup()
    _L1_ffn_in = {k: v for k, v in _L1_ffn_all.items() if k in ('W_base', 'b_base', 'W_gate', 'A', 'B')}
    del _L1_ffn_all

    def _L2_xattn_setup():
        import jax, jax.numpy as jnp
        import numpy as np
        H = 128
        C = 4
        RH = 16
        HS = H // RH
        DR = 8
        M = 512
        NH = 16
        HD = H // NH
        A_SIZE = (C - 1) * RH
        B_SIZE = C * RH
        EPS = 1e-05
        SSM_EPS = 1e-05

        def rat_read(res, W, gamma, beta, num_outputs):
            b, l, _ = res.shape
            x = res.reshape(b, l, H, C)
            y = jnp.einsum('blhc,hoc->bloh', x, W)
            mu = y.mean(-1, keepdims=True)
            var = y.var(-1, keepdims=True)
            yn = (y - mu) * jax.lax.rsqrt(var + EPS)
            yn = yn * gamma.reshape(num_outputs, H) + beta.reshape(num_outputs, H)
            return yn.reshape(b, l, num_outputs * H)

        def rope(x, pos):
            half = HD // 2
            inv = 1.0 / 10000.0 ** (jnp.arange(half, dtype=jnp.float32) / half)
            ang = pos.astype(jnp.float32)[..., None] * inv
            cos = jnp.cos(ang)[:, :, None, :]
            sin = jnp.sin(ang)[:, :, None, :]
            x1, x2 = (x[..., :half], x[..., half:])
            return jnp.concatenate([x1 * cos - x2 * sin, x2 * cos + x1 * sin], axis=-1)

        def attention(qkv_in, qkv_w, pos):
            b, l, _ = qkv_in.shape
            q, k, v = jnp.split(qkv_in, 3, axis=-1)
            q = jnp.einsum('bli,oi->blo', q, qkv_w[0]).reshape(b, l, NH, HD)
            k = jnp.einsum('bli,oi->blo', k, qkv_w[1]).reshape(b, l, NH, HD)
            v = jnp.einsum('bli,oi->blo', v, qkv_w[2]).reshape(b, l, NH, HD)
            q = rope(q, pos)
            k = rope(k, pos)
            scores = jnp.einsum('bqhd,bkhd->bhqk', q, k) / np.sqrt(HD).astype(np.float32)
            mask = jnp.tril(jnp.ones((l, l), dtype=bool))
            scores = jnp.where(mask, scores, jnp.float32(-1e+30))
            p = jax.nn.softmax(scores, axis=-1)
            o = jnp.einsum('bhqk,bkhd->bqhd', p, v)
            return o.reshape(b, l, H)

        def rat_write(res, y, wod_w, wab_w, wab_b, du_w, du_b):
            b, l, _ = res.shape
            o_d = y @ wod_w.T
            A_B = y @ wab_w.T + wab_b
            out = o_d[..., :H]
            delta_low = o_d[..., H:]
            A_logit = A_B[..., :A_SIZE]
            B_proj = A_B[..., A_SIZE:2 * A_SIZE]
            B_skip = A_B[..., 2 * A_SIZE:]
            delta = jax.nn.softplus(delta_low @ du_w.T + du_b)
            hs = res.reshape(b, l, HS, RH, C)
            out = out.reshape(b, l, HS, RH, 1)
            delta = delta.reshape(b, l, HS, RH, 1)
            A_logit = A_logit.reshape(b, l, 1, RH, C - 1)
            B_proj = B_proj.reshape(b, l, 1, RH, C - 1)
            B_skip = B_skip.reshape(b, l, 1, RH, 1)
            A_neg = -jax.nn.softplus(A_logit)
            A_bar = jnp.exp(delta * A_neg)
            B_bar = (A_bar - 1.0) / (A_neg - SSM_EPS) * B_proj
            B_bar_skip = delta * B_skip
            A_full = jnp.concatenate([A_bar, jnp.ones_like(A_bar[..., :1])], axis=-1)
            B_full = jnp.concatenate([B_bar, B_bar_skip], axis=-1)
            return (hs * A_full + out * B_full).reshape(b, l, H * C)

        def layer_forward(hidden_states, position_ids, attn_read_w, attn_read_g, attn_read_b, qkv_w, attn_wod_w, attn_wab_w, attn_wab_b, attn_du_w, attn_du_b, mlp_read_w, mlp_read_g, mlp_read_b, mlp_in_w, mlp_wod_w, mlp_wab_w, mlp_wab_b, mlp_du_w, mlp_du_b):
            qkv_in = rat_read(hidden_states, attn_read_w, attn_read_g, attn_read_b, 3)
            attn_out = attention(qkv_in, qkv_w, position_ids)
            hidden_states = rat_write(hidden_states, attn_out, attn_wod_w, attn_wab_w, attn_wab_b, attn_du_w, attn_du_b)
            mlp_in = rat_read(hidden_states, mlp_read_w, mlp_read_g, mlp_read_b, 2)
            g_in, u_in = (mlp_in[..., :H], mlp_in[..., H:])
            gate = jnp.einsum('bli,oi->blo', g_in, mlp_in_w[0])
            up = jnp.einsum('bli,oi->blo', u_in, mlp_in_w[1])
            mlp_out = jax.nn.silu(gate) * up
            hidden_states = rat_write(hidden_states, mlp_out, mlp_wod_w, mlp_wab_w, mlp_wab_b, mlp_du_w, mlp_du_b)
            return hidden_states
        key = jax.random.key(seed)
        ks = jax.random.split(key, 20)
        B, L = (2, 256)
        s = 0.02
        return {'hidden_states': jax.random.normal(ks[0], (B, L, H * C), jnp.float32), 'position_ids': jnp.tile(jnp.arange(L, dtype=jnp.int64), (B, 1)), 'attn_read_w': jax.random.normal(ks[1], (H, 3, C), jnp.float32) / np.sqrt(C).astype(np.float32), 'attn_read_g': jnp.ones((3 * H,), jnp.float32), 'attn_read_b': jnp.zeros((3 * H,), jnp.float32), 'qkv_w': jax.random.normal(ks[2], (3, H, H), jnp.float32) * s, 'attn_wod_w': jax.random.normal(ks[3], (H + DR, H), jnp.float32) * s, 'attn_wab_w': jax.random.normal(ks[4], (A_SIZE + B_SIZE, H), jnp.float32) * s, 'attn_wab_b': jax.random.normal(ks[5], (A_SIZE + B_SIZE,), jnp.float32) * s, 'attn_du_w': jax.random.normal(ks[6], (H, DR), jnp.float32) * s, 'attn_du_b': jax.random.normal(ks[7], (H,), jnp.float32) * s, 'mlp_read_w': jax.random.normal(ks[8], (H, 2, C), jnp.float32) / np.sqrt(C).astype(np.float32), 'mlp_read_g': jnp.ones((2 * H,), jnp.float32), 'mlp_read_b': jnp.zeros((2 * H,), jnp.float32), 'mlp_in_w': jax.random.normal(ks[9], (2, M, H), jnp.float32) * s, 'mlp_wod_w': jax.random.normal(ks[10], (H + DR, M), jnp.float32) * s, 'mlp_wab_w': jax.random.normal(ks[11], (A_SIZE + B_SIZE, M), jnp.float32) * s, 'mlp_wab_b': jax.random.normal(ks[12], (A_SIZE + B_SIZE,), jnp.float32) * s, 'mlp_du_w': jax.random.normal(ks[13], (H, DR), jnp.float32) * s, 'mlp_du_b': jax.random.normal(ks[14], (H,), jnp.float32) * s}
    _L2_xattn_all = _L2_xattn_setup()
    _L2_xattn_in = {k: v for k, v in _L2_xattn_all.items() if k in ('attn_read_w', 'attn_read_g', 'attn_read_b', 'qkv_w', 'attn_wod_w', 'attn_wab_w', 'attn_wab_b', 'attn_du_w', 'attn_du_b', 'mlp_read_w', 'mlp_read_g', 'mlp_read_b', 'mlp_wod_w', 'mlp_wab_w', 'mlp_wab_b', 'mlp_du_w', 'mlp_du_b')}
    del _L2_xattn_all

    def _L2_ffn_setup():
        import jax, jax.numpy as jnp
        import numpy as np
        B, S, D, O, E, R = (2, 512, 512, 512, 8, 16)
        TOP_K = 2
        SCALING = 32.0 / 16.0
        key = jax.random.key(seed)
        k = jax.random.split(key, 6)
        x = jax.random.normal(k[0], (B, S, D), dtype=jnp.float32)
        W_base = jax.random.normal(k[1], (O, D), dtype=jnp.float32) * 0.02
        b_base = jax.random.normal(k[2], (O,), dtype=jnp.float32) * 0.02
        W_router = jax.random.normal(k[3], (E, D), dtype=jnp.float32) * 0.01
        lora_A = jax.random.normal(k[4], (E, R, D), dtype=jnp.float32) * (1.0 / np.sqrt(D))
        lora_B = jax.random.normal(k[5], (E, O, R), dtype=jnp.float32) * 0.02
        return {'x': x, 'W_base': W_base, 'b_base': b_base, 'W_router': W_router, 'lora_A': lora_A, 'lora_B': lora_B}
    _L2_ffn_all = _L2_ffn_setup()
    _L2_ffn_in = {k: v for k, v in _L2_ffn_all.items() if k in ('W_base', 'b_base', 'W_router', 'lora_A', 'lora_B')}
    del _L2_ffn_all

    def _L3_xattn_setup():
        import math
        import jax, jax.numpy as jnp
        import numpy as np
        N_HEADS = 32
        N_KV_HEADS = 8
        N_REP = N_HEADS // N_KV_HEADS
        HEAD_DIM = 512 // N_HEADS
        key = jax.random.key(seed)
        kq, kk, kv = jax.random.split(key, 3)
        B, S, T = (2, 256, 256)
        q = jax.random.normal(kq, (B, S, N_HEADS * HEAD_DIM), dtype=jnp.float32)
        k = jax.random.normal(kk, (B, T, N_KV_HEADS * HEAD_DIM), dtype=jnp.float32)
        v = jax.random.normal(kv, (B, T, N_KV_HEADS * HEAD_DIM), dtype=jnp.float32)
        mask = jnp.zeros((S, T), dtype=jnp.float32)
        return {'q': q, 'k': k, 'v': v, 'start_pos': 0, 'mask': mask}
    _L3_xattn_all = _L3_xattn_setup()
    _L3_xattn_in = {k: v for k, v in _L3_xattn_all.items() if k in ()}
    del _L3_xattn_all

    def _L3_ffn_setup():
        import jax, jax.numpy as jnp
        import numpy as np
        N_BITS = 8
        QMAX = 2 ** (N_BITS - 1) - 1
        EPS = 1e-08

        def fake_quant(x):
            scale = jnp.max(jnp.abs(x), axis=-1, keepdims=True) / QMAX
            scale = jnp.maximum(scale, EPS)
            q = jnp.clip(jnp.round(x / scale), -QMAX - 1, QMAX)
            return q * scale
        key = jax.random.key(seed)
        k1, k2, k3, k4 = jax.random.split(key, 4)
        B, S, H, I = (2, 256, 512, 1792)
        hidden_states = jax.random.normal(k1, (B, S, H), dtype=jnp.float32)
        w_gate = jax.random.normal(k2, (I, H), dtype=jnp.float32) * 0.02
        w_up = jax.random.normal(k3, (I, H), dtype=jnp.float32) * 0.02
        w_down = jax.random.normal(k4, (H, I), dtype=jnp.float32) * 0.02
        return {'hidden_states': hidden_states, 'w_gate': w_gate, 'w_up': w_up, 'w_down': w_down}
    _L3_ffn_all = _L3_ffn_setup()
    _L3_ffn_in = {k: v for k, v in _L3_ffn_all.items() if k in ('w_gate', 'w_up', 'w_down')}
    del _L3_ffn_all
    return {'x': x, 'pos_BxS': pos_BxS, 'ctx_1024': ctx_1024, 'mask_SxS2_ff0': mask_SxS2_ff0, 'L0_xattn_attn_read_w': _L0_xattn_in['attn_read_w'], 'L0_xattn_attn_read_g': _L0_xattn_in['attn_read_g'], 'L0_xattn_attn_read_b': _L0_xattn_in['attn_read_b'], 'L0_xattn_qkv_w': _L0_xattn_in['qkv_w'], 'L0_xattn_attn_wod_w': _L0_xattn_in['attn_wod_w'], 'L0_xattn_attn_wab_w': _L0_xattn_in['attn_wab_w'], 'L0_xattn_attn_wab_b': _L0_xattn_in['attn_wab_b'], 'L0_xattn_attn_du_w': _L0_xattn_in['attn_du_w'], 'L0_xattn_attn_du_b': _L0_xattn_in['attn_du_b'], 'L0_xattn_mlp_read_w': _L0_xattn_in['mlp_read_w'], 'L0_xattn_mlp_read_g': _L0_xattn_in['mlp_read_g'], 'L0_xattn_mlp_read_b': _L0_xattn_in['mlp_read_b'], 'L0_xattn_mlp_wod_w': _L0_xattn_in['mlp_wod_w'], 'L0_xattn_mlp_wab_w': _L0_xattn_in['mlp_wab_w'], 'L0_xattn_mlp_wab_b': _L0_xattn_in['mlp_wab_b'], 'L0_xattn_mlp_du_w': _L0_xattn_in['mlp_du_w'], 'L0_xattn_mlp_du_b': _L0_xattn_in['mlp_du_b'], 'L0_ffn_gate_q': _L0_ffn_in['gate_q'], 'L0_ffn_gate_scale': _L0_ffn_in['gate_scale'], 'L0_ffn_gate_A': _L0_ffn_in['gate_A'], 'L0_ffn_gate_B': _L0_ffn_in['gate_B'], 'L0_ffn_up_q': _L0_ffn_in['up_q'], 'L0_ffn_up_scale': _L0_ffn_in['up_scale'], 'L0_ffn_up_A': _L0_ffn_in['up_A'], 'L0_ffn_up_B': _L0_ffn_in['up_B'], 'L0_ffn_down_q': _L0_ffn_in['down_q'], 'L0_ffn_down_scale': _L0_ffn_in['down_scale'], 'L0_ffn_down_A': _L0_ffn_in['down_A'], 'L0_ffn_down_B': _L0_ffn_in['down_B'], 'L1_ffn_W_base': _L1_ffn_in['W_base'], 'L1_ffn_b_base': _L1_ffn_in['b_base'], 'L1_ffn_W_gate': _L1_ffn_in['W_gate'], 'L1_ffn_A': _L1_ffn_in['A'], 'L1_ffn_B': _L1_ffn_in['B'], 'L2_xattn_attn_read_w': _L2_xattn_in['attn_read_w'], 'L2_xattn_attn_read_g': _L2_xattn_in['attn_read_g'], 'L2_xattn_attn_read_b': _L2_xattn_in['attn_read_b'], 'L2_xattn_qkv_w': _L2_xattn_in['qkv_w'], 'L2_xattn_attn_wod_w': _L2_xattn_in['attn_wod_w'], 'L2_xattn_attn_wab_w': _L2_xattn_in['attn_wab_w'], 'L2_xattn_attn_wab_b': _L2_xattn_in['attn_wab_b'], 'L2_xattn_attn_du_w': _L2_xattn_in['attn_du_w'], 'L2_xattn_attn_du_b': _L2_xattn_in['attn_du_b'], 'L2_xattn_mlp_read_w': _L2_xattn_in['mlp_read_w'], 'L2_xattn_mlp_read_g': _L2_xattn_in['mlp_read_g'], 'L2_xattn_mlp_read_b': _L2_xattn_in['mlp_read_b'], 'L2_xattn_mlp_wod_w': _L2_xattn_in['mlp_wod_w'], 'L2_xattn_mlp_wab_w': _L2_xattn_in['mlp_wab_w'], 'L2_xattn_mlp_wab_b': _L2_xattn_in['mlp_wab_b'], 'L2_xattn_mlp_du_w': _L2_xattn_in['mlp_du_w'], 'L2_xattn_mlp_du_b': _L2_xattn_in['mlp_du_b'], 'L2_ffn_W_base': _L2_ffn_in['W_base'], 'L2_ffn_b_base': _L2_ffn_in['b_base'], 'L2_ffn_W_router': _L2_ffn_in['W_router'], 'L2_ffn_lora_A': _L2_ffn_in['lora_A'], 'L2_ffn_lora_B': _L2_ffn_in['lora_B'], 'L3_ffn_w_gate': _L3_ffn_in['w_gate'], 'L3_ffn_w_up': _L3_ffn_in['w_up'], 'L3_ffn_w_down': _L3_ffn_in['w_down']}

def reference(x, pos_BxS, ctx_1024, mask_SxS2_ff0, L0_xattn_attn_read_w, L0_xattn_attn_read_g, L0_xattn_attn_read_b, L0_xattn_qkv_w, L0_xattn_attn_wod_w, L0_xattn_attn_wab_w, L0_xattn_attn_wab_b, L0_xattn_attn_du_w, L0_xattn_attn_du_b, L0_xattn_mlp_read_w, L0_xattn_mlp_read_g, L0_xattn_mlp_read_b, L0_xattn_mlp_wod_w, L0_xattn_mlp_wab_w, L0_xattn_mlp_wab_b, L0_xattn_mlp_du_w, L0_xattn_mlp_du_b, L0_ffn_gate_q, L0_ffn_gate_scale, L0_ffn_gate_A, L0_ffn_gate_B, L0_ffn_up_q, L0_ffn_up_scale, L0_ffn_up_A, L0_ffn_up_B, L0_ffn_down_q, L0_ffn_down_scale, L0_ffn_down_A, L0_ffn_down_B, L1_ffn_W_base, L1_ffn_b_base, L1_ffn_W_gate, L1_ffn_A, L1_ffn_B, L2_xattn_attn_read_w, L2_xattn_attn_read_g, L2_xattn_attn_read_b, L2_xattn_qkv_w, L2_xattn_attn_wod_w, L2_xattn_attn_wab_w, L2_xattn_attn_wab_b, L2_xattn_attn_du_w, L2_xattn_attn_du_b, L2_xattn_mlp_read_w, L2_xattn_mlp_read_g, L2_xattn_mlp_read_b, L2_xattn_mlp_wod_w, L2_xattn_mlp_wab_w, L2_xattn_mlp_wab_b, L2_xattn_mlp_du_w, L2_xattn_mlp_du_b, L2_ffn_W_base, L2_ffn_b_base, L2_ffn_W_router, L2_ffn_lora_A, L2_ffn_lora_B, L3_ffn_w_gate, L3_ffn_w_up, L3_ffn_w_down):
    import jax
    import jax.numpy as jnp

    def _L0_xattn_ref(hidden_states, position_ids, attn_read_w, attn_read_g, attn_read_b, qkv_w, attn_wod_w, attn_wab_w, attn_wab_b, attn_du_w, attn_du_b, mlp_read_w, mlp_read_g, mlp_read_b, mlp_in_w, mlp_wod_w, mlp_wab_w, mlp_wab_b, mlp_du_w, mlp_du_b):
        import jax, jax.numpy as jnp
        import numpy as np
        H = 128
        C = 4
        RH = 16
        HS = H // RH
        DR = 8
        M = 512
        NH = 16
        HD = H // NH
        A_SIZE = (C - 1) * RH
        B_SIZE = C * RH
        EPS = 1e-05
        SSM_EPS = 1e-05

        def rat_read(res, W, gamma, beta, num_outputs):
            b, l, _ = res.shape
            x = res.reshape(b, l, H, C)
            y = jnp.einsum('blhc,hoc->bloh', x, W)
            mu = y.mean(-1, keepdims=True)
            var = y.var(-1, keepdims=True)
            yn = (y - mu) * jax.lax.rsqrt(var + EPS)
            yn = yn * gamma.reshape(num_outputs, H) + beta.reshape(num_outputs, H)
            return yn.reshape(b, l, num_outputs * H)

        def rope(x, pos):
            half = HD // 2
            inv = 1.0 / 10000.0 ** (jnp.arange(half, dtype=jnp.float32) / half)
            ang = pos.astype(jnp.float32)[..., None] * inv
            cos = jnp.cos(ang)[:, :, None, :]
            sin = jnp.sin(ang)[:, :, None, :]
            x1, x2 = (x[..., :half], x[..., half:])
            return jnp.concatenate([x1 * cos - x2 * sin, x2 * cos + x1 * sin], axis=-1)

        def attention(qkv_in, qkv_w, pos):
            b, l, _ = qkv_in.shape
            q, k, v = jnp.split(qkv_in, 3, axis=-1)
            q = jnp.einsum('bli,oi->blo', q, qkv_w[0]).reshape(b, l, NH, HD)
            k = jnp.einsum('bli,oi->blo', k, qkv_w[1]).reshape(b, l, NH, HD)
            v = jnp.einsum('bli,oi->blo', v, qkv_w[2]).reshape(b, l, NH, HD)
            q = rope(q, pos)
            k = rope(k, pos)
            scores = jnp.einsum('bqhd,bkhd->bhqk', q, k) / np.sqrt(HD).astype(np.float32)
            mask = jnp.tril(jnp.ones((l, l), dtype=bool))
            scores = jnp.where(mask, scores, jnp.float32(-1e+30))
            p = jax.nn.softmax(scores, axis=-1)
            o = jnp.einsum('bhqk,bkhd->bqhd', p, v)
            return o.reshape(b, l, H)

        def rat_write(res, y, wod_w, wab_w, wab_b, du_w, du_b):
            b, l, _ = res.shape
            o_d = y @ wod_w.T
            A_B = y @ wab_w.T + wab_b
            out = o_d[..., :H]
            delta_low = o_d[..., H:]
            A_logit = A_B[..., :A_SIZE]
            B_proj = A_B[..., A_SIZE:2 * A_SIZE]
            B_skip = A_B[..., 2 * A_SIZE:]
            delta = jax.nn.softplus(delta_low @ du_w.T + du_b)
            hs = res.reshape(b, l, HS, RH, C)
            out = out.reshape(b, l, HS, RH, 1)
            delta = delta.reshape(b, l, HS, RH, 1)
            A_logit = A_logit.reshape(b, l, 1, RH, C - 1)
            B_proj = B_proj.reshape(b, l, 1, RH, C - 1)
            B_skip = B_skip.reshape(b, l, 1, RH, 1)
            A_neg = -jax.nn.softplus(A_logit)
            A_bar = jnp.exp(delta * A_neg)
            B_bar = (A_bar - 1.0) / (A_neg - SSM_EPS) * B_proj
            B_bar_skip = delta * B_skip
            A_full = jnp.concatenate([A_bar, jnp.ones_like(A_bar[..., :1])], axis=-1)
            B_full = jnp.concatenate([B_bar, B_bar_skip], axis=-1)
            return (hs * A_full + out * B_full).reshape(b, l, H * C)

        def layer_forward(hidden_states, position_ids, attn_read_w, attn_read_g, attn_read_b, qkv_w, attn_wod_w, attn_wab_w, attn_wab_b, attn_du_w, attn_du_b, mlp_read_w, mlp_read_g, mlp_read_b, mlp_in_w, mlp_wod_w, mlp_wab_w, mlp_wab_b, mlp_du_w, mlp_du_b):
            qkv_in = rat_read(hidden_states, attn_read_w, attn_read_g, attn_read_b, 3)
            attn_out = attention(qkv_in, qkv_w, position_ids)
            hidden_states = rat_write(hidden_states, attn_out, attn_wod_w, attn_wab_w, attn_wab_b, attn_du_w, attn_du_b)
            mlp_in = rat_read(hidden_states, mlp_read_w, mlp_read_g, mlp_read_b, 2)
            g_in, u_in = (mlp_in[..., :H], mlp_in[..., H:])
            gate = jnp.einsum('bli,oi->blo', g_in, mlp_in_w[0])
            up = jnp.einsum('bli,oi->blo', u_in, mlp_in_w[1])
            mlp_out = jax.nn.silu(gate) * up
            hidden_states = rat_write(hidden_states, mlp_out, mlp_wod_w, mlp_wab_w, mlp_wab_b, mlp_du_w, mlp_du_b)
            return hidden_states
        return layer_forward(hidden_states, position_ids, attn_read_w, attn_read_g, attn_read_b, qkv_w, attn_wod_w, attn_wab_w, attn_wab_b, attn_du_w, attn_du_b, mlp_read_w, mlp_read_g, mlp_read_b, mlp_in_w, mlp_wod_w, mlp_wab_w, mlp_wab_b, mlp_du_w, mlp_du_b)

    def _L0_ffn_ref(x, gate_q, gate_scale, gate_A, gate_B, up_q, up_scale, up_A, up_B, down_q, down_scale, down_A, down_B):
        import jax, jax.numpy as jnp
        import numpy as np
        H = 512
        I = 1376
        R = 32
        NLEV = 16
        Q_ZERO = 7.5
        Q_STEP = 0.005
        LR_SCALE = 0.02

        def _qlinear(x, q, scale, A, Bm):
            w = (q.astype(jnp.float32) - Q_ZERO) * (scale * Q_STEP)[:, None]
            y = jnp.einsum('bsh,oh->bso', x, w)
            return y + LR_SCALE * (x @ A @ Bm)
        g = _qlinear(x, gate_q, gate_scale, gate_A, gate_B)
        u = _qlinear(x, up_q, up_scale, up_A, up_B)
        h = jax.nn.silu(g) * u
        return _qlinear(h, down_q, down_scale, down_A, down_B)

    def _L1_xattn_ref(q, k, v, start_pos, mask):
        import math
        import jax, jax.numpy as jnp
        import numpy as np
        N_HEADS = 32
        N_KV_HEADS = 8
        N_REP = N_HEADS // N_KV_HEADS
        HEAD_DIM = 512 // N_HEADS
        b, s, _ = q.shape
        t = k.shape[1]
        xq = q.reshape(b, s, N_KV_HEADS, N_REP, HEAD_DIM)
        xk = k.reshape(b, t, N_KV_HEADS, HEAD_DIM)
        xv = v.reshape(b, t, N_KV_HEADS, HEAD_DIM)
        scores = jnp.einsum('bsgrd,btgd->bgrst', xq, xk) / math.sqrt(HEAD_DIM)
        scores = scores + mask
        probs = jax.nn.softmax(scores.astype(jnp.float32), axis=-1).astype(q.dtype)
        out = jnp.einsum('bgrst,btgd->bsgrd', probs, xv)
        return out.reshape(b, s, N_HEADS * HEAD_DIM)

    def _L1_ffn_ref(x, W_base, b_base, W_gate, A, B):
        import jax, jax.numpy as jnp
        import numpy as np
        BATCH, TOK, DIM, OUT = (4, 256, 512, 512)
        E, R, TOP_K = (8, 16, 2)
        SCALING = 16.0 / R
        result = jnp.einsum('bnd,od->bno', x, W_base) + b_base
        logits = jnp.einsum('bnd,ed->bne', x, W_gate)
        probs = jax.nn.softmax(logits.astype(jnp.float32), axis=-1)
        top_p, top_i = jax.lax.top_k(probs, TOP_K)
        top_p = top_p / jnp.sum(top_p, axis=-1, keepdims=True)
        top_p = top_p.astype(x.dtype)
        route_w = jnp.sum(jax.nn.one_hot(top_i, E, dtype=x.dtype) * top_p[..., None], axis=-2)
        h = jnp.einsum('bnd,erd->bner', x, A)
        hw = h * route_w[..., None]
        delta = jnp.einsum('bner,eor->bno', hw, B)
        return result + delta * SCALING

    def _L2_xattn_ref(hidden_states, position_ids, attn_read_w, attn_read_g, attn_read_b, qkv_w, attn_wod_w, attn_wab_w, attn_wab_b, attn_du_w, attn_du_b, mlp_read_w, mlp_read_g, mlp_read_b, mlp_in_w, mlp_wod_w, mlp_wab_w, mlp_wab_b, mlp_du_w, mlp_du_b):
        import jax, jax.numpy as jnp
        import numpy as np
        H = 128
        C = 4
        RH = 16
        HS = H // RH
        DR = 8
        M = 512
        NH = 16
        HD = H // NH
        A_SIZE = (C - 1) * RH
        B_SIZE = C * RH
        EPS = 1e-05
        SSM_EPS = 1e-05

        def rat_read(res, W, gamma, beta, num_outputs):
            b, l, _ = res.shape
            x = res.reshape(b, l, H, C)
            y = jnp.einsum('blhc,hoc->bloh', x, W)
            mu = y.mean(-1, keepdims=True)
            var = y.var(-1, keepdims=True)
            yn = (y - mu) * jax.lax.rsqrt(var + EPS)
            yn = yn * gamma.reshape(num_outputs, H) + beta.reshape(num_outputs, H)
            return yn.reshape(b, l, num_outputs * H)

        def rope(x, pos):
            half = HD // 2
            inv = 1.0 / 10000.0 ** (jnp.arange(half, dtype=jnp.float32) / half)
            ang = pos.astype(jnp.float32)[..., None] * inv
            cos = jnp.cos(ang)[:, :, None, :]
            sin = jnp.sin(ang)[:, :, None, :]
            x1, x2 = (x[..., :half], x[..., half:])
            return jnp.concatenate([x1 * cos - x2 * sin, x2 * cos + x1 * sin], axis=-1)

        def attention(qkv_in, qkv_w, pos):
            b, l, _ = qkv_in.shape
            q, k, v = jnp.split(qkv_in, 3, axis=-1)
            q = jnp.einsum('bli,oi->blo', q, qkv_w[0]).reshape(b, l, NH, HD)
            k = jnp.einsum('bli,oi->blo', k, qkv_w[1]).reshape(b, l, NH, HD)
            v = jnp.einsum('bli,oi->blo', v, qkv_w[2]).reshape(b, l, NH, HD)
            q = rope(q, pos)
            k = rope(k, pos)
            scores = jnp.einsum('bqhd,bkhd->bhqk', q, k) / np.sqrt(HD).astype(np.float32)
            mask = jnp.tril(jnp.ones((l, l), dtype=bool))
            scores = jnp.where(mask, scores, jnp.float32(-1e+30))
            p = jax.nn.softmax(scores, axis=-1)
            o = jnp.einsum('bhqk,bkhd->bqhd', p, v)
            return o.reshape(b, l, H)

        def rat_write(res, y, wod_w, wab_w, wab_b, du_w, du_b):
            b, l, _ = res.shape
            o_d = y @ wod_w.T
            A_B = y @ wab_w.T + wab_b
            out = o_d[..., :H]
            delta_low = o_d[..., H:]
            A_logit = A_B[..., :A_SIZE]
            B_proj = A_B[..., A_SIZE:2 * A_SIZE]
            B_skip = A_B[..., 2 * A_SIZE:]
            delta = jax.nn.softplus(delta_low @ du_w.T + du_b)
            hs = res.reshape(b, l, HS, RH, C)
            out = out.reshape(b, l, HS, RH, 1)
            delta = delta.reshape(b, l, HS, RH, 1)
            A_logit = A_logit.reshape(b, l, 1, RH, C - 1)
            B_proj = B_proj.reshape(b, l, 1, RH, C - 1)
            B_skip = B_skip.reshape(b, l, 1, RH, 1)
            A_neg = -jax.nn.softplus(A_logit)
            A_bar = jnp.exp(delta * A_neg)
            B_bar = (A_bar - 1.0) / (A_neg - SSM_EPS) * B_proj
            B_bar_skip = delta * B_skip
            A_full = jnp.concatenate([A_bar, jnp.ones_like(A_bar[..., :1])], axis=-1)
            B_full = jnp.concatenate([B_bar, B_bar_skip], axis=-1)
            return (hs * A_full + out * B_full).reshape(b, l, H * C)

        def layer_forward(hidden_states, position_ids, attn_read_w, attn_read_g, attn_read_b, qkv_w, attn_wod_w, attn_wab_w, attn_wab_b, attn_du_w, attn_du_b, mlp_read_w, mlp_read_g, mlp_read_b, mlp_in_w, mlp_wod_w, mlp_wab_w, mlp_wab_b, mlp_du_w, mlp_du_b):
            qkv_in = rat_read(hidden_states, attn_read_w, attn_read_g, attn_read_b, 3)
            attn_out = attention(qkv_in, qkv_w, position_ids)
            hidden_states = rat_write(hidden_states, attn_out, attn_wod_w, attn_wab_w, attn_wab_b, attn_du_w, attn_du_b)
            mlp_in = rat_read(hidden_states, mlp_read_w, mlp_read_g, mlp_read_b, 2)
            g_in, u_in = (mlp_in[..., :H], mlp_in[..., H:])
            gate = jnp.einsum('bli,oi->blo', g_in, mlp_in_w[0])
            up = jnp.einsum('bli,oi->blo', u_in, mlp_in_w[1])
            mlp_out = jax.nn.silu(gate) * up
            hidden_states = rat_write(hidden_states, mlp_out, mlp_wod_w, mlp_wab_w, mlp_wab_b, mlp_du_w, mlp_du_b)
            return hidden_states
        return layer_forward(hidden_states, position_ids, attn_read_w, attn_read_g, attn_read_b, qkv_w, attn_wod_w, attn_wab_w, attn_wab_b, attn_du_w, attn_du_b, mlp_read_w, mlp_read_g, mlp_read_b, mlp_in_w, mlp_wod_w, mlp_wab_w, mlp_wab_b, mlp_du_w, mlp_du_b)

    def _L2_ffn_ref(x, W_base, b_base, W_router, lora_A, lora_B):
        import jax, jax.numpy as jnp
        import numpy as np
        B, S, D, O, E, R = (2, 512, 512, 512, 8, 16)
        TOP_K = 2
        SCALING = 32.0 / 16.0
        d = x.shape[-1]
        n_experts = W_router.shape[0]
        xf = x.reshape(-1, d)
        logits = xf @ W_router.T
        probs = jax.nn.softmax(logits, axis=-1)
        topk_p, topk_i = jax.lax.top_k(probs, TOP_K)
        topk_p = topk_p / jnp.sum(topk_p, axis=-1, keepdims=True)
        w = jnp.sum(jax.nn.one_hot(topk_i, n_experts, dtype=xf.dtype) * topk_p[..., None], axis=1)
        h = jnp.einsum('td,erd->ter', xf, lora_A)
        lora_out = jnp.einsum('ter,eor,te->to', h, lora_B, w) * SCALING
        base = x @ W_base.T + b_base
        return base + lora_out.reshape(x.shape[:-1] + (W_base.shape[0],))

    def _L3_xattn_ref(q, k, v, start_pos, mask):
        import math
        import jax, jax.numpy as jnp
        import numpy as np
        N_HEADS = 32
        N_KV_HEADS = 8
        N_REP = N_HEADS // N_KV_HEADS
        HEAD_DIM = 512 // N_HEADS
        b, s, _ = q.shape
        t = k.shape[1]
        xq = q.reshape(b, s, N_KV_HEADS, N_REP, HEAD_DIM)
        xk = k.reshape(b, t, N_KV_HEADS, HEAD_DIM)
        xv = v.reshape(b, t, N_KV_HEADS, HEAD_DIM)
        scores = jnp.einsum('bsgrd,btgd->bgrst', xq, xk) / math.sqrt(HEAD_DIM)
        scores = scores + mask
        probs = jax.nn.softmax(scores.astype(jnp.float32), axis=-1).astype(q.dtype)
        out = jnp.einsum('bgrst,btgd->bsgrd', probs, xv)
        return out.reshape(b, s, N_HEADS * HEAD_DIM)

    def _L3_ffn_ref(hidden_states, w_gate, w_up, w_down):
        import jax, jax.numpy as jnp
        import numpy as np
        N_BITS = 8
        QMAX = 2 ** (N_BITS - 1) - 1
        EPS = 1e-08

        def fake_quant(x):
            scale = jnp.max(jnp.abs(x), axis=-1, keepdims=True) / QMAX
            scale = jnp.maximum(scale, EPS)
            q = jnp.clip(jnp.round(x / scale), -QMAX - 1, QMAX)
            return q * scale
        xq = fake_quant(hidden_states)
        gate = jnp.einsum('bsh,ih->bsi', xq, w_gate)
        up = jnp.einsum('bsh,ih->bsi', xq, w_up)
        inter = jax.nn.silu(gate) * up
        interq = fake_quant(inter)
        return jnp.einsum('bsi,hi->bsh', interq, w_down)
    x = x + _L0_xattn_ref(_layernorm(x, axis=-1), pos_BxS, L0_xattn_attn_read_w, L0_xattn_attn_read_g, L0_xattn_attn_read_b, L0_xattn_qkv_w, L0_xattn_attn_wod_w, L0_xattn_attn_wab_w, L0_xattn_attn_wab_b, L0_xattn_attn_du_w, L0_xattn_attn_du_b, L0_xattn_mlp_read_w, L0_xattn_mlp_read_g, L0_xattn_mlp_read_b, ctx_1024, L0_xattn_mlp_wod_w, L0_xattn_mlp_wab_w, L0_xattn_mlp_wab_b, L0_xattn_mlp_du_w, L0_xattn_mlp_du_b)
    x = x + _L0_ffn_ref(_layernorm(x, axis=-1), L0_ffn_gate_q, L0_ffn_gate_scale, L0_ffn_gate_A, L0_ffn_gate_B, L0_ffn_up_q, L0_ffn_up_scale, L0_ffn_up_A, L0_ffn_up_B, L0_ffn_down_q, L0_ffn_down_scale, L0_ffn_down_A, L0_ffn_down_B)
    x = x + _L1_xattn_ref(_layernorm(x, axis=-1), ctx_1024, ctx_1024, 0, mask_SxS2_ff0)
    x = x + _L1_ffn_ref(_layernorm(x, axis=-1), L1_ffn_W_base, L1_ffn_b_base, L1_ffn_W_gate, L1_ffn_A, L1_ffn_B)
    x = x + _L2_xattn_ref(_layernorm(x, axis=-1), pos_BxS, L2_xattn_attn_read_w, L2_xattn_attn_read_g, L2_xattn_attn_read_b, L2_xattn_qkv_w, L2_xattn_attn_wod_w, L2_xattn_attn_wab_w, L2_xattn_attn_wab_b, L2_xattn_attn_du_w, L2_xattn_attn_du_b, L2_xattn_mlp_read_w, L2_xattn_mlp_read_g, L2_xattn_mlp_read_b, ctx_1024, L2_xattn_mlp_wod_w, L2_xattn_mlp_wab_w, L2_xattn_mlp_wab_b, L2_xattn_mlp_du_w, L2_xattn_mlp_du_b)
    x = x + _L2_ffn_ref(_layernorm(x, axis=-1), L2_ffn_W_base, L2_ffn_b_base, L2_ffn_W_router, L2_ffn_lora_A, L2_ffn_lora_B)
    x = x + _L3_xattn_ref(_layernorm(x, axis=-1), ctx_1024, ctx_1024, 0, mask_SxS2_ff0)
    x = x + _L3_ffn_ref(_layernorm(x, axis=-1), L3_ffn_w_gate, L3_ffn_w_up, L3_ffn_w_down)
    return x

_drawn_inputs = setup_inputs


def setup_inputs(seed=0):
    import zlib

    import numpy as np

    out = dict(_drawn_inputs(seed))
    spreads = {'mask_SxS2_ff0': (0.0, 2.0),
     'L0_xattn_attn_read_g': (1.0, 0.6),
     'L0_xattn_attn_read_b': (0.0, 0.8),
     'L0_xattn_mlp_read_g': (1.0, 0.6),
     'L0_xattn_mlp_read_b': (0.0, 0.8),
     'L2_xattn_attn_read_g': (1.0, 0.6),
     'L2_xattn_attn_read_b': (0.0, 0.8),
     'L2_xattn_mlp_read_g': (1.0, 0.6),
     'L2_xattn_mlp_read_b': (0.0, 0.8)}
    factors = {'ctx_1024': 8.0,
     'L0_xattn_attn_read_w': 8.0,
     'L0_xattn_qkv_w': 8.0,
     'L0_xattn_attn_wod_w': 8.0,
     'L0_xattn_attn_wab_w': 8.0,
     'L0_xattn_attn_wab_b': 8.0,
     'L0_xattn_attn_du_w': 8.0,
     'L0_xattn_attn_du_b': 8.0,
     'L0_xattn_mlp_read_w': 8.0,
     'L0_xattn_mlp_wod_w': 8.0,
     'L0_xattn_mlp_wab_w': 8.0,
     'L0_xattn_mlp_wab_b': 8.0,
     'L0_xattn_mlp_du_w': 8.0,
     'L0_xattn_mlp_du_b': 8.0,
     'L1_ffn_b_base': 23.635,
     'L1_ffn_W_gate': 8.0,
     'L1_ffn_A': 8.0,
     'L1_ffn_B': 8.0,
     'L2_xattn_attn_read_w': 8.0,
     'L2_xattn_qkv_w': 8.0,
     'L2_xattn_attn_wod_w': 8.0,
     'L2_xattn_attn_wab_w': 8.0,
     'L2_xattn_attn_wab_b': 8.0,
     'L2_xattn_attn_du_w': 8.0,
     'L2_xattn_attn_du_b': 8.0,
     'L2_xattn_mlp_read_w': 8.0,
     'L2_xattn_mlp_wod_w': 8.0,
     'L2_xattn_mlp_wab_w': 8.0,
     'L2_xattn_mlp_wab_b': 29.731,
     'L2_xattn_mlp_du_w': 8.0,
     'L2_xattn_mlp_du_b': 48.636,
     'L2_ffn_b_base': 64.0,
     'L2_ffn_W_router': 64.0,
     'L2_ffn_lora_A': 64.0,
     'L2_ffn_lora_B': 64.0,
     'L3_ffn_w_gate': 23.386,
     'L3_ffn_w_up': 8.0,
     'L3_ffn_w_down': 8.0,
     'L2_ffn_W_base': 8.0}
    for name, (base, spread) in spreads.items():
        noise = np.random.default_rng([zlib.crc32(name.encode()), seed]).standard_normal(out[name].shape)
        drawn = base * np.exp(spread * noise) if base else spread * noise
        out[name] = jnp.asarray(drawn.astype(out[name].dtype))
    for name, factor in factors.items():
        out[name] = (out[name] * factor).astype(out[name].dtype)
    return out
```

```python
from contextlib import ExitStack

import concourse.bass as bass
from concourse import mybir
import numpy as np

ALU = mybir.AluOpType
ACT = mybir.ActivationFunctionType
F32 = mybir.dt.float32
F32R = mybir.dt.float32r
I32 = mybir.dt.int32
AX = mybir.AxisListType

P = 128
B, S, D = 2, 256, 512
NT = B * S // P
QT = S // P
DC = D // P
T = B * S
S2, CD = 512, 128
KT = S2 // P
EPS = 1e-5

H, C, RH, DR, NH, HD = 128, 4, 16, 8, 16, 8
HS = H // RH
C3 = C - 1
AS = C3 * RH
NAB = 2 * AS + RH
NW = H + DR + NAB
MC = S2 // P
SLOT = 32
GH = P // SLOT
NG = NH // GH

XH, XG, XD = 32, 8, 16
XSLOT = 64
NPAIR = XH // 2
XK = 3 * XD + 2
XV = XD + 1
XR = XH // XG

I0, R0, QZERO, QSTEP, LRS = 1376, 32, 7.5, 0.005, 0.02
F0 = (I0 + P - 1) // P
F0W = [min(P, I0 - P * f) for f in range(F0)]

E, R = 8, 16
ER = E * R

I3 = 1792
NB3 = 4
W3 = I3 // NB3
F3 = I3 // P
QMAX, QEPS = 127.0, 1e-8
MAGIC = 1.5 * 2.0 ** 23

RP = {}
_at = 0
for _name, _n in (("rw", DC * 3), ("rg", 3), ("rb", 3), ("qkv", 3 * H), ("wcat", NW),
                  ("mw", DC * 2), ("mg", 2), ("mb", 2), ("mcat", MC * NW)):
    RP[_name] = (_at, _at + _n)
    _at += _n
RPN = _at
MP = {"base": (0, DC * D), "ag": (DC * D, DC * D + DC * (ER + E)), "b": (DC * D + DC * (ER + E), DC * D + DC * (ER + E) + D)}
MPN = MP["b"][1]


class Signal:

    def __init__(self, sem, per):
        self.sem, self.per = sem, per

    def __call__(self, k, n):
        assert 0 < n <= self.per, (self.sem, k, n)
        return self.sem, k * self.per + n


def sbuf_map(nc, first):
    buf, at = {}, {}

    def lay(end, *items):
        for name, shape, dt in items:
            buf[name] = nc.alloc_sbuf_tensor_at(name, shape, dt, offset=end)
            at[name] = end
            end += (int(np.prod(shape[1:])) * 4 + 31) // 32 * 32
        return end

    mix = lay(first,
              ("ident", [P, P], F32), ("identr", [P, P], F32R),
              ("causal0", [P, 3 * P], F32), ("causal", [P, 3 * P], F32R),
              ("sel", [P, SLOT], F32),
              ("iota8", [P, E], F32), ("powc", [P, 16], F32),
              ("mask_q", [P, QT, S2], F32), ("mask_k", [P, KT, S], F32),
              ("x", [P, NT, D], F32), ("xn", [P, NT, D], F32), ("xnT", [P, DC, T], F32),
              ("ctx", [P, B * KT, CD], F32), ("ctxT", [P, B, S2], F32),
              ("rw", [P, RPN], F32), ("rrow", [P, 2, NAB], F32), ("du", [DR + 1, 2, H], F32),
              ("dl", [DR + 1, T], F32), ("wd", [P, DC, 3, SLOT], F32),
              ("pos", [P, NT], I32), ("ang", [P, NT, HD // 2], F32), ("turn", [P, NT, HD // 2], F32),
              ("cos", [P, NT, HD // 2], F32), ("sin", [P, NT, HD // 2], F32),
              ("stats", [P, 12, 6], F32), ("mv", [P, 12, 2], F32), ("ve", [P, 12], F32), ("rstd", [P, 12], F32),
              ("sc3", [P, 2, NT], F32), ("isc3", [P, 2, NT], F32), ("route", [P, 12, NT, E], F32))
    low = max(lay(mix, ("gA", [P, DC, 3 * R0], F32), ("uA", [P, DC, 3 * R0], F32),
                  ("gB", [3 * R0, I0], F32R), ("uB", [3 * R0, I0], F32R),
                  ("dA", [P, F0, 2 * R0], F32R), ("gsc", [P, 2, F0], F32), ("dsc", [P, D], F32),
                  ("dB", [3 * R0, D], F32R)),
              lay(mix, ("mw", [P, MPN], F32), ("mB", [P, D], F32), ("hs", [P, NT, ER], F32),
                  ("hsT", [P, T], F32)))

    def rat(k, start):
        qk = [P, NT, 2, H]
        a = lay(start, ("qks%d" % k, [P, NT, 2, NH, SLOT], F32))
        b = lay(a, ("vs%d" % k, [P, NT, NH, SLOT], F32), ("kT%d" % k, [P, NG, T], F32R))
        c = lay(b, ("yn%d" % k, [P, NT, 3, H], F32), ("ynT%d" % k, [P, 3, T], F32))
        lay(b, ("p%d0" % k, [P, GH, 3 * P], F32), ("p%d1" % k, [P, GH, 3 * P], F32))
        d = lay(c, ("qk%d" % k, qk, F32), ("qkr%d" % k, qk, F32))
        lay(c, ("qT%d" % k, [P, NG, T], F32R))
        e = lay(d, ("qkh%d" % k, qk, F32R))
        end = lay(e, ("oT%d0" % k, [P, S], F32), ("oT%d1" % k, [P, S], F32),
                  ("y%d" % k, [P, NT, H], F32), ("yT%d" % k, [P, 1, T], F32))
        assert lay(start, ("u%d" % k, [P, NT, H, C3], F32), ("t%d" % k, [P, NT, H, C3], F32),
                   ("os%d" % k, [P, NT, H], F32), ("ab%d" % k, [P, NT, NAB], F32)) <= a
        assert lay(a, ("sp%d" % k, [P, NT, AS + H], F32), ("gg%d" % k, [P, NT, AS], F32)) <= a + 8192
        lay(a + 8192, ("gT%d" % k, [P, MC, T], F32))
        lay(c, ("az%d" % k, [P, NT, AS + H], F32), ("ln%d" % k, [P, NT, AS + H], F32))
        lay(d, ("silu%d0" % k, [P, T], F32), ("silu%d1" % k, [P, T], F32))
        return end

    high = rat(0, low)
    high = max(high, lay(low, ("hh", [P, F0, T], F32R), ("hl", [P, F0, T], F32R),
                         ("xh", [P, DC, T], F32R), ("xl", [P, DC, T], F32R)))
    lay(low, ("gBraw", [3 * R0, I0], F32), ("uBraw", [3 * R0, I0], F32), ("dAraw", [P, F0, R0], F32),
        ("dBraw", [3 * R0, D], F32))
    lay(at["xn"], ("us", [3 * R0, 2, T], F32R), ("ug", [3 * R0, 2, T], F32))
    lay(at["xnT"], ("lg", [P, 2, T], F32), ("lu", [P, 2, T], F32))
    assert lay(at["rw"], ("gp", [P, 2, T], F32), ("up", [P, T], F32)) <= at["rrow"]
    lay(at["xn"], ("udh", [3 * R0, T], F32R), ("udf", [3 * R0, T], F32), ("ud2", [P, NT, 2 * R0], F32),
        ("ud3", [P, NT, 3, R0], F32))
    lay(low, ("dsum", [P, NT, D], F32))
    kv = lay(low, ("kx", [P, XG // 2, B * S2], F32R), ("vx", [P, B * KT, XG, SLOT], F32))
    lay(kv, ("kst", [P, B * KT, XG, XSLOT], F32), ("ch", [P, B * KT, CD], F32R))
    assert lay(kv, ("qt0", [P, S], F32R), ("qt1", [P, S], F32R), ("qm0", [P, S], F32R), ("qm1", [P, S], F32R),
               ("ox0", [P, 2, S], F32), ("ox1", [P, 2, S], F32), ("on", [P, QT * 2 * XR, XD], F32), ("rden", [P, QT * 2 * XR], F32)) <= high
    assert lay(high, ("qst", [P, NT, XH, XSLOT], F32), *[("px%d" % i, [P, 2, 2, S], F32) for i in range(4)],
               ("junk", [P, 2, S2], mybir.dt.bfloat16), ("mkh", [P, 2, S], F32R), ("mkl", [P, 2, S], F32R),
               ("mh", [P, QT, 2], F32R)) <= nc.sbuf_usable_end
    lay(at["xnT"], ("qh", [P, NT, D], F32R))
    assert lay(low, ("inter", [P, NT, I3], F32), ("iqT", [P, F3, T], F32R)) <= high
    lay(at["xnT"], ("xqT", [P, DC, T], F32R))
    lay(high, *[("w%s%d" % (n, i), [P, DC * W3], dt) for n, dt, c in
        (("raw", F32, 3), ("hi", F32R, 3), ("lo", F32R, 3)) for i in range(c)],
        ("sil0", [P, W3], F32), ("sil1", [P, W3], F32))
    ends = [lay(high, ("gi", [P, DC, I0], F32R), ("ui", [P, DC, I0], F32R), ("di", [P, F0, D], F32R)),
            lay(high, ("gq", [P, DC, I0], I32), ("uq", [P, DC, I0], I32), ("dq", [P, F0, D], I32)),
            rat(1, high)]
    assert max(ends) <= nc.sbuf_usable_end
    return buf


def program(nc, a, out):
    with ExitStack() as ctx:
        buf = sbuf_map(nc, (nc.sbuf_base + 31) // 32 * 32)
        ps = ctx.enter_context(nc.psum_tensor("ps", [P, 8, 512], F32))

        def v(name):
            return buf[name]

        def signal(name, per):
            return Signal(ctx.enter_context(nc.semaphore(name)), per)

        x, xn, xnT = v("x"), v("xn"), v("xnT")
        ident, identr = v("ident"), v("identr")
        stats, mv, ve, rstd = v("stats"), v("mv"), v("ve"), v("rstd")
        RATJ, RATN = [0, 4], [0, 4]

        x_in = signal("x_in", 16)
        pos_in = signal("pos_in", 16)
        small_in = signal("small_in", 16 * 3)
        rat_in = signal("rat_in", 16 * 3)
        ff_in = signal("ff_in", 16 * 8)
        q_in = [signal("q_in%d" % i, 16 * DC) for i in range(3)]
        mix_in = signal("mix_in", 16 * 2)
        bias_in = signal("bias_in", 16)
        w_in = [signal("w_in%d" % i, 16) for i in range(3)]
        stored = signal("stored", 16 * NT)
        ident_ok = signal("ident_ok", 1)
        const_ok = signal("const_ok", 1)
        constr = signal("constr", 2)
        rope_ok = signal("rope_ok", 1)
        ang_ok = signal("ang_ok", 1)
        ctxt_ok = signal("ctxt_ok", 1)
        ctxT_ok = signal("ctxT_ok", 1)
        mv_ok = signal("mv_ok", 1)
        rstd_ok = signal("rstd_ok", 1)
        xn_ok = signal("xn_ok", NT)
        x_ok = signal("x_ok", 1)
        tr_ok = signal("tr_ok", NT)
        xnT_ok = signal("xnT_ok", NT)
        wd_ok = signal("wd_ok", 1)
        y_ok = signal("y_ok", NT)
        ymv_ok = signal("ymv_ok", 1)
        yrstd_ok = signal("yrstd_ok", 1)
        yn_ok = signal("yn_ok", NT)
        ynt_ok = signal("ynt_ok", 5)
        ynT_ok = signal("ynT_ok", 5)
        qkv_ok = signal("qkv_ok", NT)
        qk_sb = signal("qk_sb", 2 * NT)
        pads = signal("pads", 1)
        qkh_ok = signal("qkh_ok", 1)
        qks_ok = signal("qks_ok", 2)
        st_ok = signal("st_ok", 3 * NG)
        sT_ok = signal("sT_ok", 3 * NG)
        s_ok = signal("s_ok", B * NG)
        max_ok = signal("max_ok", B * NG)
        sk_ok = signal("sk_ok", B * NG)
        p_ok = signal("p_ok", B * NG)
        pm_ok = signal("pm_ok", B * NG)
        o_ok = signal("o_ok", B * NG)
        oT_ok = signal("oT_ok", B * NG)
        ot_ok = signal("ot_ok", B * NG)
        yy_ok = signal("yy_ok", B * NG)
        yt_ok = signal("yt_ok", 1)
        yT_ok = signal("yT_ok", 1)
        gate_ok = signal("gate_ok", MC)
        silu_ok = signal("silu_ok", MC)
        g_ok = signal("g_ok", MC)
        w1_ok = signal("w1_ok", 1)
        w2_ok = signal("w2_ok", 1)
        dl_ok = signal("dl_ok", 1)
        w3_ok = signal("w3_ok", 1)
        os_ok = signal("os_ok", 1)
        ab_ok = signal("ab_ok", 1)
        e_ok = signal("e_ok", 1)
        ln_ok = signal("ln_ok", 1)
        sp_ok = signal("sp_ok", 1)
        an_ok = signal("an_ok", 1)
        u_ok = signal("u_ok", NT)
        abar_ok = signal("abar_ok", NT)
        ah_ok = signal("ah_ok", NT)
        hid_ok = signal("hid_ok", 2 * NT)
        qi_ok = signal("qi_ok", 3)
        fb_ok = signal("fb_ok", 1)
        xhl_ok = signal("xhl_ok", 1)
        la_ok = signal("la_ok", 1)
        ug_ok = signal("ug_ok", 1)
        us_ok = signal("us_ok", 1)
        f_ok = signal("f_ok", F0)
        lc_ok = signal("lc_ok", F0)
        gp_ok = signal("gp_ok", F0)
        sg_ok = signal("sg_ok", F0)
        hp_ok = signal("hp_ok", F0)
        hh_ok = signal("hh_ok", F0)
        hl_ok = signal("hl_ok", F0)
        d_ok = signal("d_ok", 1)
        ud_ok = signal("ud_ok", 1)
        ud3_ok = signal("ud3_ok", 1)
        udt_ok = signal("udt_ok", 1)
        udf_ok = signal("udf_ok", 1)
        uds_ok = signal("uds_ok", 1)
        dlo_ok = signal("dlo_ok", 1)
        kst_ok = signal("kst_ok", 1)
        vx_ok = signal("vx_ok", 1)
        kt_ok = signal("kt_ok", XG)
        kx_ok = signal("kx_ok", XG)
        qh_ok = signal("qh_ok", 1)
        qst_ok = signal("qst_ok", 3)
        qt_ok = signal("qt_ok", B * NPAIR)
        qT_ok = signal("qT_ok", B * NPAIR)
        xs_ok = signal("xs_ok", 4 * B * NPAIR)
        xm_ok = signal("xm_ok", 4 * B * NPAIR)
        qm_ok = signal("qm_ok", B * NPAIR)
        qM_ok = signal("qM_ok", B * NPAIR)
        xk_ok = signal("xk_ok", 2 * B * NPAIR)
        ms_ok = signal("ms_ok", B * NPAIR)
        mk_ok = signal("mk_ok", 1)
        mh_ok = signal("mh_ok", B * NPAIR)
        ml_ok = signal("ml_ok", B * NPAIR)
        px_ok = signal("px_ok", 2 * B * NPAIR)
        pv_ok = signal("pv_ok", 2 * B * NPAIR)
        ox_ok = signal("ox_ok", B * NPAIR // 2)
        ot2_ok = signal("ot2_ok", B * NPAIR // XR)
        on_ok = signal("on_ok", B * NPAIR // XR)
        xo_ok = signal("xo_ok", B * NPAIR // XR)
        hl_ps = signal("hl_ps", 1)
        le_ok = signal("le_ok", 1)
        ee_ok = signal("ee_ok", 1)
        hw_ok = signal("hw_ok", 1)
        ht_ok = signal("ht_ok", 1)
        hT_ok = signal("hT_ok", 1)
        base_ok = signal("base_ok", NT)
        xb_ok = signal("xb_ok", 1)
        xq_ok = signal("xq_ok", NT)
        wc_ok = signal("wc_ok", 13)
        wl_ok = signal("wl_ok", 13)
        gu_ok = signal("gu_ok", NB3 * NT)
        si_ok = signal("si_ok", NB3 * NT)
        in_ok = signal("in_ok", NB3 * NT)
        iq_ok = signal("iq_ok", NT)
        it_ok = signal("it_ok", 4 * NT)
        iT_ok = signal("iT_ok", 4 * NT)
        dn_ok = signal("dn_ok", 5 * NT)
        step_done = {n: signal(n + "_step", 1 << 20) for n in ("dve", "pool", "act")}
        steps = {"dve": 0, "pool": 0, "act": 0}

        def link(e, name, ins):
            steps[name] += 1
            ins.then_inc(step_done[name].sem, 1)
            e.wait_ge(step_done[name].sem, steps[name])

        block = ctx.enter_context(nc.Block())

        ITEMS = [(m, blk, DC * W3) for blk in range(NB3) for m in ("wg", "wu")]
        DOWN = [(0, 3), (3, 3), (6, 3), (9, 3), (12, 2)]
        ITEMS += [("wd", f, n * D) for f, n in DOWN]

        @block.sync
        def _(sp):
            sp.dma_start(x[:, :, :], a["x"].rearrange("(t p) d -> p t d", p=P)).then_inc(x_in.sem, 16)
            sp.dma_start(v("pos")[:, :], a["pos"]).then_inc(pos_in.sem, 16)

            def rat_weights(k):
                sp.dma_start(v("rw")[:, :], a["rw%d" % k]).then_inc(rat_in.sem, 16)
                sp.dma_start(v("rrow")[:, :, :], a["rrow%d" % k].partition_broadcast(P)).then_inc(rat_in.sem, 16)
                sp.dma_start(v("du")[:, :, :], a["du%d" % k]).then_inc(rat_in.sem, 16)

            rat_weights(0)
            sp.dma_start(v("ctx")[:, :, :], a["ctx"].rearrange("(j p) d -> p j d", p=P)).then_inc(small_in.sem, 16)
            sp.dma_start(v("mask_q")[:, :, :], a["mask"].rearrange("(t p) s -> p t s", p=P)).then_inc(small_in.sem, 16)
            sp.dma_start(v("mask_k")[:, :, :], a["maskT"].rearrange("(t p) s -> p t s", p=P)).then_inc(small_in.sem, 16)
            for m, name in enumerate(("gq", "uq")):
                for c in range(DC):
                    sp.dma_start(v(name)[:, c, :], a[name][c * P:(c + 1) * P, :]).then_inc(q_in[m].sem, 16)
            for c in range(DC):
                f0, f1 = 3 * c, min(F0, 3 * c + 3)
                sp.dma_start(v("dq")[:, f0:f1, :], a["dq"][f0 * P:f1 * P, :].rearrange("(f p) d -> p f d", p=P))\
                  .then_inc(q_in[2].sem, 16)
            for n in ("gA", "uA", "gsc"):
                sp.dma_start(v(n)[:, :, :], a[n]).then_inc(ff_in.sem, 16)
            sp.dma_start(v("dsc")[:, :], a["dsc"].partition_broadcast(P)).then_inc(ff_in.sem, 16)
            sp.wait_ge(*x_ok(0, 1))
            for n in ("gBraw", "uBraw", "dBraw"):
                sp.dma_start(v(n)[:, :], a[n]).then_inc(ff_in.sem, 16)
            sp.dma_start(v("dAraw")[:, :, :], a["dAraw"]).then_inc(ff_in.sem, 16)

            def mix_weights(k):
                sp.dma_start(v("mw")[:, :], a["mw%d" % k]).then_inc(mix_in.sem, 16)
                sp.dma_start(v("mB")[:, :], a["mB%d" % k]).then_inc(mix_in.sem, 16)

            sp.wait_ge(*x_ok(1, 1))
            mix_weights(0)
            rat_weights(1)
            sp.wait_ge(*x_ok(3, 1))
            mix_weights(1)
            sp.wait_ge(*x_ok(6, 1))
            for i, (m, at, n) in enumerate(ITEMS):
                if i >= 3:
                    sp.wait_ge(*wl_ok(0, i - 2))
                dst = v("wraw%d" % (i % 3))[:, 0:n]
                if m == "wd":
                    f, c = at, n // D
                    sp.dma_start(dst.rearrange("p (f d) -> p f d", d=D),
                                 a["wd"][f * P:(f + c) * P, :].rearrange("(f p) d -> p f d", p=P))\
                      .then_inc(w_in[i % 3].sem, 16)
                else:
                    sp.dma_start(dst.rearrange("p (c i) -> p c i", c=DC),
                                 a[m][:, at * W3:(at + 1) * W3].rearrange("(c p) i -> p c i", p=P))\
                      .then_inc(w_in[i % 3].sem, 16)
            sp.wait_ge(*x_ok(7, 1))
            sp.dma_start(out.rearrange("(t p) d -> p t d", p=P), x[:, :, :]).then_inc(stored.sem, 16)
            sp.wait_ge(stored.sem, 16)

        @block.tensor
        def _(pe):
            def transposes(j, src, ready, rk, off=0):
                for t in range(NT):
                    pe.wait_ge(*ready(rk, off + t + 1))
                    for c in range(DC):
                        mm = pe.transpose(ps[:, 4 + t, c * P:(c + 1) * P], src[:, t, c * P:(c + 1) * P], ident[:, :])
                    mm.then_inc(tr_ok.sem, 1)

            def rat_read(k, half, nout):
                i, j = 2 * k + half, [[0, 1], [4, 5]][k][half]
                pe.wait_ge(*wd_ok(i, 1))
                for t in range(NT):
                    pe.wait_ge(*xnT_ok(j, t + 1))
                    for c in range(DC):
                        o = ps[:, t, 0:nout * H].rearrange("p (o h) -> p o h", o=nout)[:, :, c * SLOT:(c + 1) * SLOT]
                        mm = pe.matmul(o, xnT[:, c, t * P:(t + 1) * P], v("wd")[:, c, 0:nout, :],
                                       start=True, stop=True)
                    mm.then_inc(y_ok.sem, 1)
                for o in range(nout):
                    for t in range(NT):
                        if o == 0:
                            pe.wait_ge(*yn_ok(i, t + 1))
                        mm = pe.transpose(ps[:, 4 + o, t * P:(t + 1) * P], v("yn%d" % k)[:, t, o, :], ident[:, :])
                    mm.then_inc(ynt_ok.sem, 1)

            def rat_attention(k):
                W0 = RP["qkv"][0]
                pe.wait_ge(*ynT_ok(k, 3))
                for t in range(NT):
                    for o in range(3):
                        mm = pe.matmul(ps[:, t, o * H:(o + 1) * H], v("ynT%d" % k)[:, o, t * P:(t + 1) * P],
                                       v("rw")[:, W0 + o * H:W0 + (o + 1) * H], start=True, stop=True)
                    mm.then_inc(qkv_ok.sem, 1)

                def turn(which, g, bank):
                    for t in range(NT):
                        src = v("qks%d" % k)[:, t, which, g * GH:(g + 1) * GH, :].rearrange("p h s -> p (h s)")
                        mm = pe.transpose(ps[:, bank, t * P:(t + 1) * P], src, ident[:, :])
                    mm.then_inc(st_ok.sem, 1)

                pe.wait_ge(*qks_ok(k, 2))
                for g in range(NG):
                    turn(1, g, 4 + g)
                for g in range(NG):
                    turn(0, g, g)
                kT, qT = v("kT%d" % k), v("qT%d" % k)
                pe.wait_ge(*sT_ok(k, 2 * NG))
                for i in range(B * NG):
                    b, g = i // NG, i % NG
                    bank = 4 * (i % 2)
                    if i >= 2:
                        pe.wait_ge(*max_ok(k, i - 1))
                    for r in range(GH):
                        pe.matmul(ps[:, bank + r, 0:3 * P], identr[:, :], v("causal")[:, :], start=True, stop=True)
                    for qt in range(QT):
                        for r in range(GH):
                            row = slice(SLOT * r, SLOT * r + 3 * HD + 1)
                            n = P * (qt + 1)
                            o = ps[:, bank + r, qt * P:qt * P + n]
                            mm = pe.matmul(o, qT[row, g, (b * QT + qt) * P:(b * QT + qt + 1) * P],
                                           kT[row, g, b * S:b * S + n], start=False, stop=True,
                                           skip_group_check=True)
                    mm.then_inc(s_ok.sem, 1)
                pe.wait_ge(*max_ok(k, B * NG))
                for g in range(NG):
                    turn(0, g, g)
                pe.wait_ge(*sT_ok(k, 3 * NG))

                def values(i):
                    b, g = i // NG, i % NG
                    pe.wait_ge(*pm_ok(k, i + 1))
                    if i >= 2:
                        pe.wait_ge(*oT_ok(k, i - 1))
                    for kt in range(QT):
                        for r in range(GH):
                            n = S - kt * P
                            pt = v("p%d%d" % (k, i % 2))[:, r, kt * S:kt * S + n]
                            mm = pe.matmul(ps[SLOT * r:SLOT * r + SLOT, 4 + i % 2, kt * P:S],
                                           v("vs%d" % k)[:, b * QT + kt, g * GH + r, :], pt,
                                           start=(kt == 0), stop=True, skip_group_check=True)
                    mm.then_inc(o_ok.sem, 1)

                def outputs(i):
                    pe.wait_ge(*oT_ok(k, i + 1))
                    if i >= 2:
                        pe.wait_ge(*yy_ok(k, i - 1))
                    for qt in range(QT):
                        mm = pe.transpose(ps[:, 6 + i % 2, qt * P:(qt + 1) * P],
                                          v("oT%d%d" % (k, i % 2))[:, qt * P:(qt + 1) * P], ident[:, :])
                    mm.then_inc(ot_ok.sem, 1)

                for i in range(B * NG):
                    b, g = i // NG, i % NG
                    if i >= 1:
                        pe.wait_ge(*p_ok(k, i))
                    for kt in range(QT):
                        for r in range(GH):
                            row = slice(SLOT * r, SLOT * r + 3 * HD + 1)
                            n = S - kt * P
                            mm = pe.matmul(ps[:, r, kt * S:kt * S + n],
                                           kT[row, g, b * S + kt * P:b * S + (kt + 1) * P],
                                           qT[row, g, b * S + kt * P:(b + 1) * S], start=True, stop=True)
                    mm.then_inc(sk_ok.sem, 1)
                    if i >= 1:
                        values(i - 1)
                    if i >= 2:
                        outputs(i - 2)
                values(B * NG - 1)
                outputs(B * NG - 2)
                outputs(B * NG - 1)
                pe.wait_ge(*yy_ok(k, B * NG))
                for t in range(NT):
                    mm = pe.transpose(ps[:, 0, t * P:(t + 1) * P], v("y%d" % k)[:, t, :], ident[:, :])
                mm.then_inc(yt_ok.sem, 1)

            def rat_hidden(k):
                pe.wait_ge(*ynT_ok(k, 5))
                for m in range(MC):
                    if m >= 2:
                        pe.wait_ge(*g_ok(k, m - 1))
                    for o in range(2):
                        mm = pe.matmul(ps[:, 2 * (m % 2) + o, :], v("ctxT")[:, o, m * P:(m + 1) * P],
                                       v("ynT%d" % k)[:, o, :], start=True, stop=True)
                    mm.then_inc(gate_ok.sem, 1)

            def rat_write(k, half):
                i = 2 * k + half
                n = MC if half else 1
                w0 = RP["mcat" if half else "wcat"][0]
                yt = v(("gT%d" if half else "yT%d") % k)
                pe.wait_ge(*(g_ok(k, MC) if half else yT_ok(k, 1)))
                for c in range(n):
                    mm = pe.matmul(ps[0:DR, 4, :], v("rw")[:, w0 + c * NW + H:w0 + c * NW + H + DR], yt[:, c, :],
                                   start=(c == 0), stop=(c == n - 1))
                mm.then_inc(w2_ok.sem, 1)
                for t in range(NT):
                    for c in range(n):
                        mm = pe.matmul(ps[:, t, 0:NW], yt[:, c, t * P:(t + 1) * P],
                                       v("rw")[:, w0 + c * NW:w0 + (c + 1) * NW], start=(c == 0), stop=(c == n - 1))
                mm.then_inc(w1_ok.sem, 1)
                pe.wait_ge(*dl_ok(i, 1))
                for t in range(NT):
                    mm = pe.matmul(ps[:, 5, t * P:(t + 1) * P], v("dl")[:, t * P:(t + 1) * P],
                                   v("du")[:, half, :], start=True, stop=True)
                mm.then_inc(w3_ok.sem, 1)

            def rat(k):
                transposes(RATJ[k], xn, xn_ok, RATN[k])
                rat_read(k, 0, 3)
                rat_attention(k)
                rat_write(k, 0)
                transposes([1, 5][k], xn, hid_ok, k)
                rat_read(k, 1, 2)
                rat_hidden(k)
                rat_write(k, 1)

            def feed0():
                transposes(2, xn, xn_ok, 1)
                pe.wait_ge(*xnT_ok(2, NT))
                pe.wait_ge(*ff_in(0, 16 * 8))
                for m, n in enumerate(("gA", "uA")):
                    for c in range(DC):
                        mm = pe.matmul(ps[0:3 * R0, m, :], v(n)[:, c, :], xnT[:, c, :], start=(c == 0),
                                       stop=(c == DC - 1))
                mm.then_inc(la_ok.sem, 1)
                pe.wait_ge(*xhl_ok(0, 1))
                pe.wait_ge(*us_ok(0, 1))
                pe.wait_ge(*fb_ok(0, 1))
                for f in range(F0):
                    w = F0W[f]
                    fs = slice(f * P, f * P + w)
                    if f >= 2:
                        pe.wait_ge(*hp_ok(0, f - 1))
                    for m, n in enumerate(("gi", "ui")):
                        if f == 0:
                            pe.wait_ge(*qi_ok(0, m + 1))
                        for c in range(DC):
                            for p, part in enumerate(("xh", "xl")):
                                pe.matmul(ps[0:w, 2 * m + f % 2, :], v(n)[:, c, fs], v(part)[:, c, :],
                                          start=(c == 0 and p == 0), stop=(c == DC - 1 and p == 1))
                    for m, n in enumerate(("gB", "uB")):
                        mm = pe.matmul(ps[0:w, 4 + 2 * m + f % 2, :], v(n)[:, fs], v("us")[:, m, :],
                                       start=True, stop=True)
                    mm.then_inc(f_ok.sem, 1)
                pe.wait_ge(*qi_ok(0, 3))
                pe.wait_ge(*hp_ok(0, F0))
                for f in range(F0):
                    w = F0W[f]
                    pe.wait_ge(*hl_ok(0, f + 1))
                    for t in range(NT):
                        for p, part in enumerate(("hh", "hl")):
                            lhsT = v(part)[0:w, f, t * P:(t + 1) * P]
                            end = f == F0 - 1 and p == 1
                            pe.matmul(ps[:, t, :], lhsT, v("di")[0:w, f, :], start=(f == 0 and p == 0), stop=end)
                            mm = pe.matmul(ps[:, 4, t * P:t * P + 2 * R0], lhsT, v("dA")[0:w, f, :],
                                           start=(f == 0 and p == 0 and t == 0), stop=end,
                                           skip_group_check=True)
                mm.then_inc(d_ok.sem, 1)
                pe.wait_ge(*ud3_ok(0, 1))
                for t in range(NT):
                    mm = pe.transpose(ps[0:3 * R0, 5, t * P:(t + 1) * P],
                                      v("ud3")[:, t, :, :].rearrange("p c r -> p (c r)"), ident[:, :])
                mm.then_inc(udt_ok.sem, 1)
                pe.wait_ge(*uds_ok(0, 1))
                for t in range(NT):
                    mm = pe.matmul(ps[:, 4 + t, :], v("udh")[:, t * P:(t + 1) * P], v("dB")[:, :],
                                   start=True, stop=True)
                mm.then_inc(dlo_ok.sem, 1)

            def context():
                pe.wait_ge(*kst_ok(0, 1))
                pe.wait_ge(*x_ok(1, 1))
                for i in range(XG):
                    g, b = i // 2, i % 2
                    if i >= 2:
                        pe.wait_ge(*kx_ok(0, i - 1))
                    for kt in range(KT):
                        src = v("kst")[:, b * KT + kt, 2 * g:2 * g + 2, :].rearrange("p g s -> p (g s)")
                        mm = pe.transpose(ps[:, 4 + i % 2, kt * P:(kt + 1) * P], src, ident[:, :])
                    mm.then_inc(kt_ok.sem, 1)
                pe.wait_ge(*kx_ok(0, XG))
                pe.wait_ge(*vx_ok(0, 1))

            def cross(k):
                N = B * NPAIR
                kx, vx, qst = v("kx"), v("vx"), v("qst")

                def rows(i):
                    return slice(XSLOT * i, XSLOT * i + XK)

                def turn(n, col, done):
                    b, pr = n // NPAIR, n % NPAIR
                    for qt in range(QT):
                        src = qst[:, b * QT + qt, 2 * pr:2 * pr + 2, :].rearrange("p h s -> p (h s)")
                        mm = pe.transpose(ps[:, 7, col + qt * P:col + (qt + 1) * P], src, ident[:, :])
                    mm.then_inc(done.sem, 1)

                def turn_q(n):
                    if n >= 2:
                        pe.wait_ge(*qM_ok(k, n - 1))
                    elif n == 1:
                        pe.wait_ge(*qT_ok(k, 1))
                    turn(n, 0, qt_ok)

                def scores(n, qt):
                    b, g = n // NPAIR, n % NPAIR // 4
                    i = 4 * n + 2 * qt
                    pe.wait_ge(*qT_ok(k, n + 1))
                    for h in range(2):
                        if i >= 2:
                            pe.wait_ge(*xm_ok(k, i + h - 1))
                        pe.matmul(ps[:, 4 + h, :], v("qt%d" % (n % 2))[rows(h), qt * P:(qt + 1) * P],
                                  kx[rows(h), g, b * S2:(b + 1) * S2], start=True, stop=True)\
                          .then_inc(xs_ok.sem, 1)

                def keys(n, u):
                    b, g = n // NPAIR, n % NPAIR // 4
                    if n >= 1:
                        pe.wait_ge(*(px_ok(k, 2 * n) if u else ms_ok(k, n)))
                    if u:
                        for h in range(2):
                            for m, part in enumerate(("mkh", "mkl")):
                                pe.matmul(ps[:, 2 * u + h, :], identr[:, :],
                                          v(part)[:, :, :].rearrange("p k q -> p (k q)"), start=(m == 0), stop=False,
                                          skip_group_check=True)
                    for kk in range(2):
                        c = b * S2 + (2 * u + kk) * P
                        for h in range(2):
                            mm = pe.matmul(ps[:, 2 * u + h, kk * S:(kk + 1) * S], kx[rows(h), g, c:c + P],
                                           v("qm%d" % (n % 2))[rows(h), :], start=(u == 0), stop=True,
                                           skip_group_check=True)
                    mm.then_inc(xk_ok.sem, 1)

                def values(n, u):
                    b, gp = n // NPAIR, n % NPAIR // XR
                    i = 2 * n + u
                    if n % 2 == 0 and u == 0 and n:
                        pe.wait_ge(*ox_ok(k, n // 2))
                    pe.wait_ge(*px_ok(k, i + 1))
                    for kk in range(2):
                        for h in range(2):
                            s0 = SLOT * (2 * h + n % 2)
                            mm = pe.matmul(ps[s0:s0 + SLOT, 6, 0:S], vx[:, b * KT + 2 * u + kk, 2 * gp + h, :],
                                           v("px%d" % (i % 4))[:, h, kk, :], start=(u + kk == 0),
                                           stop=(u + kk == 2), skip_group_check=True)
                    mm.then_inc(pv_ok.sem, 1)

                def outputs(g):
                    pe.wait_ge(*ox_ok(k, 2 * g + 2))
                    for dd in range(2):
                        for qt in range(QT):
                            c = (dd * QT + qt) * P
                            mm = pe.transpose(ps[:, 4, c:c + P], v("ox%d" % (g % 2))[:, dd, qt * P:(qt + 1) * P],
                                              ident[:, :])
                    mm.then_inc(ot2_ok.sem, 1)

                pe.wait_ge(*qst_ok(k, 3))
                pe.wait_ge(*mk_ok(k, 1))
                turn_q(0)
                scores(0, 0)
                scores(0, 1)
                turn_q(1)
                scores(1, 0)
                for n in range(N):
                    pe.wait_ge(*ml_ok(k, n + 1))
                    if n + 2 <= N:
                        pe.wait_ge(*qT_ok(k, n + 2))
                    turn(n, 2 * P, qm_ok)
                    if n + 1 < N:
                        scores(n + 1, 1)
                    if n >= 1:
                        values(n - 1, 0)
                    pe.wait_ge(*qM_ok(k, n + 1))
                    keys(n, 0)
                    if n + 2 < N:
                        turn_q(n + 2)
                    keys(n, 1)
                    if n >= XR and n % XR == 1:
                        pe.wait_ge(*xm_ok(k, 4 * min(n + 2, N)))
                        outputs(n // XR - 1)
                        values(n - 1, 1)
                        pe.wait_ge(*on_ok(k, n // XR))
                        scores(n + 2, 0)
                    else:
                        if n + 2 < N:
                            scores(n + 2, 0)
                        if n >= 1:
                            values(n - 1, 1)
                values(N - 1, 0)
                values(N - 1, 1)
                outputs(N // XR - 1)

            def mixture(k):
                mw = v("mw")
                ag = mw[:, MP["ag"][0]:MP["ag"][1]].rearrange("p (c n) -> p c n", c=DC)
                base = mw[:, 0:DC * D].rearrange("p (c n) -> p c n", c=DC)
                j = [3, 6][k]
                transposes(j, xn, xn_ok, [3, 5][k])
                pe.wait_ge(*mix_in(k, 32))
                pe.wait_ge(*xnT_ok(j, NT))
                for t in range(NT):
                    for c in range(DC):
                        lhsT = xnT[:, c, t * P:(t + 1) * P]
                        mm = pe.matmul(ps[:, 5, t * E:(t + 1) * E], lhsT, ag[:, c, ER:ER + E], start=(c == 0),
                                       stop=(c == DC - 1))
                for t in range(NT):
                    for c in range(DC):
                        mm = pe.matmul(ps[:, 4, t * ER:(t + 1) * ER], xnT[:, c, t * P:(t + 1) * P], ag[:, c, 0:ER],
                                       start=(c == 0), stop=(c == DC - 1))
                mm.then_inc(hl_ps.sem, 1)
                for t in range(NT):
                    for c in range(DC):
                        pe.matmul(ps[:, t, :], xnT[:, c, t * P:(t + 1) * P], base[:, c, :], start=(c == 0), stop=False)
                pe.wait_ge(*hw_ok(k, 1))
                for t in range(NT):
                    mm = pe.transpose(ps[:, 6, t * P:(t + 1) * P], v("hs")[:, t, :], ident[:, :])
                mm.then_inc(ht_ok.sem, 1)
                pe.wait_ge(*hT_ok(k, 1))
                for t in range(NT):
                    pe.matmul(ps[:, t, :], v("hsT")[:, t * P:(t + 1) * P], v("mB")[:, :], start=False, stop=True)\
                      .then_inc(base_ok.sem, 1)

            def feed3():
                xqT, iqT = v("xqT"), v("iqT")
                transposes(7, xn, xq_ok, 0)
                pe.wait_ge(*xnT_ok(7, NT))

                def parts(i):
                    pe.wait_ge(*wl_ok(0, i + 1))
                    return [v("whi%d" % (i % 3)), v("wlo%d" % (i % 3))]

                for blk in range(NB3):
                    for t in range(NT):
                        i = blk * NT + t
                        if i >= 2:
                            pe.wait_ge(*in_ok(0, i - 1))
                        for m in range(2):
                            hi_lo = parts(2 * blk + m)
                            for c in range(DC):
                                for p, w in enumerate(hi_lo):
                                    mm = pe.matmul(ps[:, 2 * m + i % 2, 0:W3], xqT[:, c, t * P:(t + 1) * P],
                                                   w[:, c * W3:(c + 1) * W3], start=(c == 0 and p == 0),
                                                   stop=(c == DC - 1 and p == 1))
                        mm.then_inc(gu_ok.sem, 1)
                for t in range(NT):
                    pe.wait_ge(*iq_ok(0, t + 1))
                    for q in range(4):
                        i = 4 * t + q
                        if i >= 4:
                            pe.wait_ge(*iT_ok(0, i - 3))
                        fs = range(4 * q, min(F3, 4 * q + 4))
                        for f in fs:
                            mm = pe.transpose(ps[:, 4 + q, (f % 4) * P:(f % 4 + 1) * P],
                                              v("inter")[:, t, f * P:(f + 1) * P], ident[:, :])
                        mm.then_inc(it_ok.sem, 1)
                pe.wait_ge(*iT_ok(0, 4 * NT))
                for n, (f0, cnt) in enumerate(DOWN):
                    hi_lo = parts(2 * NB3 + n)
                    for t in range(NT):
                        for f in range(cnt):
                            for p, w in enumerate(hi_lo):
                                mm = pe.matmul(ps[:, t, :], iqT[:, f0 + f, t * P:(t + 1) * P],
                                               w[:, f * D:(f + 1) * D], start=(f0 + f == 0 and p == 0),
                                               stop=(f0 + f == F3 - 1 and p == 1))
                        mm.then_inc(dn_ok.sem, 1)

            pe.wait_ge(*ident_ok(0, 1))
            pe.wait_ge(*constr(0, 2))
            pe.wait_ge(*small_in(0, 16 * 3))
            for j in range(B * KT):
                mm = pe.transpose(ps[:, j // 4, (j % 4) * P:(j % 4 + 1) * P], v("ctx")[:, j, :], ident[:, :])
            mm.then_inc(ctxt_ok.sem, 1)
            pe.wait_ge(*const_ok(0, 1))
            pe.wait_ge(*ctxT_ok(0, 1))
            rat(0)
            feed0()
            context()
            cross(0)
            mixture(0)
            rat(1)
            mixture(1)
            cross(1)
            feed3()

        def query_heads(m, h):
            return m[:, :, :].rearrange("p t (g h r d) -> p (t g) h r d", h=2, r=4, d=XD)[:, :, h, :, :]

        def query_slots(m, h):
            return m[:, :, :, :].rearrange("p t (g r h) s -> p (t g) r h s", r=4, h=2)[:, :, :, h, :]

        @block.scalar
        def _(act):
            def act_copy(dst, src, scale=1.0, bias=0.0):
                return act.activation(dst, src, ACT.Copy, bias=bias, scale=scale)

            def turned(j):
                for t in range(NT):
                    act.wait_ge(*tr_ok(j, t + 1))
                    act_copy(xnT[:, :, t * P:(t + 1) * P],
                             ps[:, 4 + t, :].rearrange("p (c q) -> p c q", c=DC)).then_inc(xnT_ok.sem, 1)

            def rat_read(k, half, nout):
                turned([[0, 1], [4, 5]][k][half])
                g0, b0 = RP["mg" if half else "rg"][0], RP["mb" if half else "rb"][0]
                for o in range(nout):
                    act.wait_ge(*ynt_ok(k, 3 * half + o + 1))
                    act.activation(v("ynT%d" % k)[:, o, :], ps[:, 4 + o, :], ACT.Identity,
                                   bias=v("rw")[:, b0 + o:b0 + o + 1], scale=v("rw")[:, g0 + o:g0 + o + 1])\
                       .then_inc(ynT_ok.sem, 1)

            def rat_attention(k):
                qk, qks, qkh = v("qk%d" % k), v("qks%d" % k), v("qkh%d" % k)
                act.wait_ge(*pads(k, 1))
                for t in range(NT):
                    act.wait_ge(*qkv_ok(k, t + 1))
                    act_copy(qk[:, t, :, :], ps[:, t, 0:2 * H].rearrange("p (w h) -> p w h", w=2))\
                        .then_inc(qk_sb.sem, 1)
                    act_copy(v("vs%d" % k)[:, t, :, 0:HD],
                             ps[:, t, 2 * H:3 * H].rearrange("p (h d) -> p h d", d=HD)).then_inc(qk_sb.sem, 1)
                act.wait_ge(*qkh_ok(k, 1))
                hi = [qkh[:, :, w, :].rearrange("p t (h d) -> p t h d", d=HD) for w in range(2)]
                for w, c in ((0, 0), (0, HD), (1, 0)):
                    act_copy(qks[:, :, w, :, c:c + HD], hi[w])
                act_copy(qks[:, :, 1, :, 2 * HD:3 * HD], hi[1]).then_inc(qks_ok.sem, 1)

                def turn(n, dst, g, bank):
                    act.wait_ge(*st_ok(k, n + 1))
                    act_copy(dst[:, g, :], ps[:, bank, :]).then_inc(sT_ok.sem, 1)

                for g in range(NG):
                    turn(g, v("kT%d" % k), g, 4 + g)
                for g in range(NG):
                    turn(NG + g, v("qT%d" % k), g, g)
                for g in range(NG):
                    turn(2 * NG + g, v("qT%d" % k), g, g)

                def output(i):
                    act.wait_ge(*o_ok(k, i + 1))
                    if i >= 2:
                        act.wait_ge(*ot_ok(k, i - 1))
                    act_copy(v("oT%d%d" % (k, i % 2))[:, :], ps[:, 4 + i % 2, 0:S]).then_inc(oT_ok.sem, 1)

                for i in range(B * NG):
                    act.wait_ge(*sk_ok(k, i + 1))
                    if i >= 2:
                        act.wait_ge(*o_ok(k, i - 1))
                    act.activation(v("p%d%d" % (k, i % 2))[:, :, :], ps[:, 0:GH, 0:3 * P], ACT.Exp,
                                   scale=float(1.0 / np.sqrt(np.float32(HD)))).then_inc(p_ok.sem, 1)
                    if i >= 1:
                        output(i - 1)
                output(B * NG - 1)
                act.wait_ge(*yt_ok(k, 1))
                act_copy(v("yT%d" % k)[:, 0, :], ps[:, 0, :]).then_inc(yT_ok.sem, 1)

            def rat_hidden(k):
                for m in range(MC):
                    act.wait_ge(*gate_ok(k, m + 1))
                    if m >= 2:
                        act.wait_ge(*g_ok(k, m - 1))
                    act.activation(v("silu%d%d" % (k, m % 2))[:, :], ps[:, 2 * (m % 2), :], ACT.Silu)\
                       .then_inc(silu_ok.sem, 1)

            def rat_write(k, half):
                i = 2 * k + half
                az = v("az%d" % k)
                act.wait_ge(*w1_ok(i, 1))
                act_copy(v("os%d" % k)[:, :, :], ps[:, 0:NT, 0:H]).then_inc(os_ok.sem, 1)
                act.wait_ge(*ab_ok(i, 1))
                act.activation(az[:, :, 0:AS], v("ab%d" % k)[:, :, 0:AS], ACT.Abs)
                act.wait_ge(*w3_ok(i, 1))
                link(act, "act", act.activation(az[:, :, AS:AS + H], ps[:, 5, :].rearrange("p (t h) -> p t h", t=NT),
                                                ACT.Abs))
                act.activation(az[:, :, :], az[:, :, :], ACT.Exp, scale=-1.0).then_inc(e_ok.sem, 1)
                act.wait_ge(*e_ok(i, 1))
                act.activation(v("ln%d" % k)[:, :, :], az[:, :, :], ACT.Ln, bias=1.0).then_inc(ln_ok.sem, 1)
                for t in range(NT):
                    act.wait_ge(*u_ok(i, t + 1))
                    u = v("u%d" % k)[:, t, :, :]
                    act.activation(u, u, ACT.Exp, scale=-1.0).then_inc(abar_ok.sem, 1)

            def rat(k):
                rat_read(k, 0, 3)
                rat_attention(k)
                rat_write(k, 0)
                rat_read(k, 1, 2)
                rat_hidden(k)
                rat_write(k, 1)

            def feed0():
                turned(2)
                act.wait_ge(*la_ok(0, 1))
                act_copy(v("ug")[:, :, :], ps[0:3 * R0, 0:2, :], scale=LRS).then_inc(ug_ok.sem, 1)

                def high(f):
                    act.wait_ge(*hp_ok(0, f + 1))
                    act_copy(v("hh")[0:F0W[f], f, :], v("gp")[0:F0W[f], f % 2, :]).then_inc(hh_ok.sem, 1)

                act.wait_ge(*fb_ok(0, 1))
                for f in range(F0):
                    w = F0W[f]
                    act.wait_ge(*f_ok(0, f + 1))
                    if f >= 2:
                        act.wait_ge(*hp_ok(0, f - 1))
                    act_copy(v("lg")[0:w, f % 2, :], ps[0:w, 4 + f % 2, :])
                    act_copy(v("lu")[0:w, f % 2, :], ps[0:w, 6 + f % 2, :]).then_inc(lc_ok.sem, 1)
                    if f >= 1:
                        high(f - 1)
                    act.wait_ge(*gp_ok(0, f + 1))
                    act.activation(v("gp")[0:w, f % 2, :], v("gp")[0:w, f % 2, :], ACT.Silu).then_inc(sg_ok.sem, 1)
                high(F0 - 1)
                act.wait_ge(*d_ok(0, 1))
                act_copy(v("ud2")[:, :, :], ps[:, 4, :].rearrange("p (t r) -> p t r", t=NT)[:, :, 0:2 * R0])\
                    .then_inc(ud_ok.sem, 1)
                act.wait_ge(*udt_ok(0, 1))
                act_copy(v("udf")[:, :], ps[0:3 * R0, 5, :], scale=LRS).then_inc(udf_ok.sem, 1)

            def context():
                act.wait_ge(*x_ok(1, 1))
                for i in range(XG):
                    act.wait_ge(*kt_ok(0, i + 1))
                    act_copy(v("kx")[:, i // 2, (i % 2) * S2:(i % 2 + 1) * S2], ps[:, 4 + i % 2, :])\
                        .then_inc(kx_ok.sem, 1)

            def cross(k):
                N = B * NPAIR
                act.wait_ge(*qh_ok(k, 1))
                for h in range(2):
                    ins = act_copy(query_slots(v("qst"), h)[:, :, :, 0:XD], query_heads(v("qh"), h))
                ins.then_inc(qst_ok.sem, 1)

                def turn_q(n):
                    act.wait_ge(*qt_ok(k, n + 1))
                    if n >= 2:
                        act.wait_ge(*xs_ok(k, 4 * n - 4))
                    act_copy(v("qt%d" % (n % 2))[:, :], ps[:, 7, 0:S]).then_inc(qT_ok.sem, 1)

                def exps(n, u):
                    i = 2 * n + u
                    px = v("px%d" % (i % 4))[:, :, :, :]
                    if u == 0:
                        act.wait_ge(*ms_ok(k, n + 1))
                        act.activation(px, px, ACT.Exp).then_inc(px_ok.sem, 1)
                        return
                    act.wait_ge(*xk_ok(k, i + 1))
                    if i >= 4:
                        act.wait_ge(*pv_ok(k, i - 3))
                    act.activation(px.rearrange("p h k q -> p h (k q)"), ps[:, 2:4, :], ACT.Exp)\
                       .then_inc(px_ok.sem, 1)

                def output(m):
                    act.wait_ge(*pv_ok(k, 4 * m + 4))
                    if m >= 4 and m % 2 == 0:
                        act.wait_ge(*ot2_ok(k, m // 2 - 1))
                    act_copy(v("ox%d" % (m // 2 % 2))[:, m % 2, :], ps[:, 6, 0:S]).then_inc(ox_ok.sem, 1)

                turn_q(0)
                turn_q(1)
                for n in range(N):
                    if n >= 1:
                        exps(n - 1, 1)
                    act.wait_ge(*qm_ok(k, n + 1))
                    if n >= 2:
                        act.wait_ge(*xk_ok(k, 2 * n - 2))
                    act_copy(v("qm%d" % (n % 2))[:, :], ps[:, 7, 2 * P:4 * P]).then_inc(qM_ok.sem, 1)
                    if n + 2 < N:
                        turn_q(n + 2)
                    exps(n, 0)
                    if n >= 2 and n % 2 == 0:
                        output(n // 2 - 1)
                exps(N - 1, 1)
                output(N // 2 - 1)

            def mixture(k):
                turned([3, 6][k])
                act.wait_ge(*le_ok(k, 1))
                act.activation(v("route")[:, 1, :, :], v("route")[:, 0, :, :], ACT.Exp).then_inc(ee_ok.sem, 1)
                act.wait_ge(*ht_ok(k, 1))
                act_copy(v("hsT")[:, :], ps[:, 6, :]).then_inc(hT_ok.sem, 1)

            def feed3():
                for t in range(NT):
                    act.wait_ge(*tr_ok(7, t + 1))
                    act_copy(v("xqT")[:, :, t * P:(t + 1) * P],
                             ps[:, 4 + t, :].rearrange("p (c q) -> p c q", c=DC), bias=-MAGIC)\
                        .then_inc(xnT_ok.sem, 1)

                def split(i):
                    n = ITEMS[i][2]
                    act.wait_ge(*w_in[i % 3](i // 3, 16))
                    if 3 <= i < 2 * NB3 + 3:
                        act.wait_ge(*gu_ok(0, NT * ((i - 3) // 2 + 1)))
                    elif i >= 2 * NB3 + 3:
                        act.wait_ge(*dn_ok(0, NT * (i - 3 - 2 * NB3 + 1)))
                    act_copy(v("whi%d" % (i % 3))[:, 0:n], v("wraw%d" % (i % 3))[:, 0:n]).then_inc(wc_ok.sem, 1)

                for i in range(3):
                    split(i)
                for blk in range(NB3):
                    for t in range(NT):
                        i = blk * NT + t
                        act.wait_ge(*gu_ok(0, i + 1))
                        if i >= 2:
                            act.wait_ge(*in_ok(0, i - 1))
                        act.activation(v("sil%d" % (i % 2))[:, :], ps[:, i % 2, 0:W3], ACT.Silu,
                                       scale=v("sc3")[:, 0, t:t + 1]).then_inc(si_ok.sem, 1)
                    split(2 * blk + 3)
                    split(2 * blk + 4)
                for t in range(NT):
                    for q in range(4):
                        n = min(4, F3 - 4 * q)
                        act.wait_ge(*it_ok(0, 4 * t + q + 1))
                        act_copy(v("iqT")[:, 4 * q:4 * q + n, t * P:(t + 1) * P],
                                 ps[:, 4 + q, 0:n * P].rearrange("p (f q) -> p f q", f=n), bias=-MAGIC)\
                            .then_inc(iT_ok.sem, 1)
                split(11)
                split(12)

            act.wait_ge(*ctxt_ok(0, 1))
            act_copy(v("ctxT")[:, :, :], ps[:, 0:B, :]).then_inc(ctxT_ok.sem, 1)
            act.wait_ge(*ang_ok(0, 1))
            act.activation(v("sin")[:, :, :], v("ang")[:, :, :], ACT.Sin)
            act.activation(v("cos")[:, :, :], v("turn")[:, :, :], ACT.Sin).then_inc(rope_ok.sem, 1)
            rat(0)
            feed0()
            context()
            cross(0)
            mixture(0)
            rat(1)
            mixture(1)
            cross(1)
            feed3()

        @block.vector
        def _(dve):
            def step(ins):
                link(dve, "dve", ins)

            def norm(n):
                if n:
                    dve.wait_ge(*x_ok(n - 1, 1))
                else:
                    dve.wait_ge(*x_in(0, 16))
                for t in range(NT):
                    ins = dve.bn_stats(stats[:, t, :], x[:, t, :])
                step(ins)
                for t in range(NT):
                    ins = dve.bn_aggr(mv[:, t, :], stats[:, t, :])
                ins.then_inc(mv_ok.sem, 1)
                dve.wait_ge(*rstd_ok(n, 1))
                for t in range(NT):
                    dve.tensor_scalar(xn[:, t, :], x[:, t, :], mv[:, t, 0:1], rstd[:, t:t + 1],
                                      ALU.subtract, ALU.mult).then_inc(xn_ok.sem, 1)

            def rat_read(k, half, nout):
                i = 2 * k + half
                c0, c1 = RP["mw" if half else "rw"]
                dve.wait_ge(*rat_in(k, 48))
                col = v("rw")[:, c0:c1].rearrange("p (c o) -> p c o", o=nout)
                for c in range(DC):
                    ins = dve.tensor_tensor(v("wd")[:, c, 0:nout, :],
                                            v("sel")[:, :].unsqueeze(1).broadcast_to([P, nout, SLOT]),
                                            col[:, c, :].unsqueeze(2).broadcast_to([P, nout, SLOT]), ALU.mult)
                ins.then_inc(wd_ok.sem, 1)
                for t in range(NT):
                    dve.wait_ge(*y_ok(i, t + 1))
                    for o in range(nout):
                        ins = dve.bn_stats(stats[:, t * nout + o, :], ps[:, t, o * H:(o + 1) * H])
                step(ins)
                for t in range(NT * nout):
                    ins = dve.bn_aggr(mv[:, t, :], stats[:, t, :])
                ins.then_inc(ymv_ok.sem, 1)
                dve.wait_ge(*yrstd_ok(i, 1))
                for t in range(NT):
                    for o in range(nout):
                        n = t * nout + o
                        ins = dve.tensor_scalar(v("yn%d" % k)[:, t, o, :], ps[:, t, o * H:(o + 1) * H],
                                                mv[:, n, 0:1], rstd[:, n:n + 1], ALU.subtract, ALU.mult)
                    ins.then_inc(yn_ok.sem, 1)

            def rat_attention(k):
                dve.wait_ge(*qk_sb(k, 2 * NT))
                dve.wait_ge(*rope_ok(0, 1))
                h2 = HD // 2
                view = [v("%s%d" % (n, k))[:, :, :, :].rearrange("p t w (h d) -> p t (w h) d", d=HD)
                        for n in ("qk", "qkr")]
                tmp = v("p%d0" % k)[:, :, :].rearrange("p h s -> p (h s)")[:, 0:NT * 2 * NH * h2]\
                    .rearrange("p (t h d) -> p t h d", t=NT, d=h2)
                cos, sin = [v(n)[:, :, :].unsqueeze(2).broadcast_to([P, NT, 2 * NH, h2]) for n in ("cos", "sin")]
                lo, hi = [w[:, :, :, 0:h2] for w in view], [w[:, :, :, h2:HD] for w in view]
                dve.tensor_tensor(lo[1], lo[0], cos, ALU.mult)
                dve.tensor_tensor(hi[1], hi[0], cos, ALU.mult)
                step(dve.tensor_tensor(tmp, hi[0], sin, ALU.mult))
                step(dve.tensor_tensor(lo[1], lo[1], tmp, ALU.subtract))
                step(dve.tensor_tensor(tmp, lo[0], sin, ALU.mult))
                step(dve.tensor_tensor(hi[1], hi[1], tmp, ALU.add))
                qkr, qkh, qks = v("qkr%d" % k), v("qkh%d" % k), v("qks%d" % k)
                dve.tensor_copy(qkh[:, :, :, :], qkr[:, :, :, :]).then_inc(qkh_ok.sem, 1)
                dve.wait_ge(*qkh_ok(k, 1))
                dve.wait_ge(*pads(k, 1))
                for w, c in ((0, 2 * HD), (1, HD)):
                    a3, b3 = [m[:, :, w, :].rearrange("p t (h d) -> p t h d", d=HD)
                              for m in (qkr, qkh[:, :, :, :].bitcast(F32))]
                    ins = dve.tensor_tensor(qks[:, :, w, :, c:c + HD], a3, b3, ALU.subtract)
                ins.then_inc(qks_ok.sem, 1)
                for i in range(B * NG):
                    b, g = i // NG, i % NG
                    bank = 4 * (i % 2)
                    dve.wait_ge(*s_ok(k, i + 1))
                    for qt in range(QT):
                        m = qks[:, b * QT + qt, 0, g * GH:(g + 1) * GH, 3 * HD:3 * HD + 1]
                        ins = dve.tensor_reduce(m, ps[:, bank:bank + GH, qt * P:P + 2 * qt * P], AX.X, ALU.max)
                    ins.then_inc(max_ok.sem, 1)
                for i in range(B * NG):
                    b, g = i // NG, i % NG
                    rc = v("route")[:, i % 2, 0:QT, 0:GH]
                    dve.wait_ge(*ot_ok(k, i + 1))
                    o = ps[:, 6 + i % 2, 0:S].rearrange("p (q h s) -> p q h s", q=QT, s=SLOT)
                    step(dve.reciprocal(rc, o[:, :, :, HD]))
                    y = v("y%d" % k)[:, b * QT:(b + 1) * QT, g * SLOT:(g + 1) * SLOT]\
                        .rearrange("p q (h d) -> p q h d", d=HD)
                    dve.tensor_tensor(y, o[:, :, :, 0:HD], rc.unsqueeze(3).broadcast_to([P, QT, GH, HD]), ALU.mult)\
                       .then_inc(yy_ok.sem, 1)

            def rat_hidden(k):
                for m in range(MC):
                    dve.wait_ge(*silu_ok(k, m + 1))
                    dve.tensor_tensor(v("gT%d" % k)[:, m, :], v("silu%d%d" % (k, m % 2))[:, :],
                                      ps[:, 2 * (m % 2) + 1, :], ALU.mult).then_inc(g_ok.sem, 1)

            def rat_write(k, half):
                i = 2 * k + half
                ab, sp, gg, az, tt = [v(n % k) for n in ("ab%d", "sp%d", "gg%d", "az%d", "t%d")]
                dve.wait_ge(*w2_ok(i, 1))
                dve.tensor_copy(v("dl")[0:DR, :], ps[0:DR, 4, :]).then_inc(dl_ok.sem, 1)
                dve.wait_ge(*w1_ok(i, 1))
                dve.wait_ge(*os_ok(i, 1))
                dve.tensor_tensor(ab[:, :, :], ps[:, 0:NT, H + DR:NW],
                                  v("rrow")[:, half:half + 1, :].broadcast_to([P, NT, NAB]), ALU.add)\
                   .then_inc(ab_ok.sem, 1)
                dve.wait_ge(*ab_ok(i, 1))
                dve.wait_ge(*e_ok(i, 1))
                step(dve.tensor_scalar(sp[:, :, :], az[:, :, :], 1.0, None, ALU.add))
                step(dve.scalar_tensor_tensor(sp[:, :, :], sp[:, :, :], -1.0, az[:, :, :], ALU.add, ALU.subtract))
                dve.wait_ge(*ln_ok(i, 1))
                step(dve.tensor_tensor(sp[:, :, :], v("ln%d" % k)[:, :, :], sp[:, :, :], ALU.subtract))
                dve.scalar_tensor_tensor(sp[:, :, 0:AS], ab[:, :, 0:AS], 0.0, sp[:, :, 0:AS], ALU.max, ALU.add)
                dve.scalar_tensor_tensor(sp[:, :, AS:AS + H], ps[:, 5, :].rearrange("p (t h) -> p t h", t=NT), 0.0,
                                         sp[:, :, AS:AS + H], ALU.max, ALU.add).then_inc(sp_ok.sem, 1)
                dve.wait_ge(*sp_ok(i, 1))
                step(dve.tensor_scalar(gg[:, :, :], sp[:, :, 0:AS], -1.0, -EPS, ALU.mult, ALU.add))
                step(dve.reciprocal(gg[:, :, :], gg[:, :, :]))
                step(dve.tensor_tensor(gg[:, :, :], gg[:, :, :], ab[:, :, AS:2 * AS], ALU.mult))
                for t in range(NT):
                    dve.wait_ge(*abar_ok(i, t + 1))
                    u3 = v("u%d" % k)[:, t, :, :].rearrange("p (s r) c -> p s (r c)", s=HS)
                    t3 = tt[:, t, :, :].rearrange("p (s r) c -> p s (r c)", s=HS)
                    g3 = gg[:, t:t + 1, :].broadcast_to([P, HS, AS])
                    step(dve.scalar_tensor_tensor(t3, u3, -1.0, g3, ALU.add, ALU.mult))
                    step(dve.tensor_tensor(tt[:, t, :, :], tt[:, t, :, :],
                                           v("os%d" % k)[:, t, :].unsqueeze(2).broadcast_to([P, H, C3]), ALU.mult))
                    dve.wait_ge(*ah_ok(i, t + 1))
                    h3 = xn[:, t, :].rearrange("p (h c) -> p h c", c=C)[:, :, 0:C3]
                    dve.tensor_tensor(h3, h3, tt[:, t, :, :], ALU.add).then_inc(hid_ok.sem, 1)
                if half:
                    dve.wait_ge(*hid_ok(k, 2 * NT))
                    for t in range(NT):
                        ins = dve.tensor_tensor(x[:, t, :], x[:, t, :], xn[:, t, :], ALU.add)
                    ins.then_inc(x_ok.sem, 1)

            def rat(k):
                norm(RATN[k])
                rat_read(k, 0, 3)
                rat_attention(k)
                rat_write(k, 0)
                rat_read(k, 1, 2)
                rat_hidden(k)
                rat_write(k, 1)

            def feed0():
                norm(1)
                dve.wait_ge(*xnT_ok(2, NT))
                step(dve.tensor_copy(v("xh")[:, :, :], xnT[:, :, :]))
                dve.tensor_tensor(v("xl")[:, :, :], xnT[:, :, :], v("xh")[:, :, :].bitcast(F32), ALU.subtract)\
                   .then_inc(xhl_ok.sem, 1)
                dve.wait_ge(*ug_ok(0, 1))
                us, ug = v("us"), v("ug")
                mid = slice(R0, 2 * R0)
                step(dve.tensor_copy(us[:, :, :], ug[:, :, :]))
                dve.tensor_tensor(us[mid, :, :], ug[mid, :, :], us[mid, :, :].bitcast(F32), ALU.subtract)\
                   .then_inc(us_ok.sem, 1)
                for f in range(F0):
                    w = F0W[f]
                    gp, up = v("gp")[0:w, f % 2, :], v("up")[0:w, :]
                    dve.wait_ge(*lc_ok(0, f + 1))
                    if f >= 2:
                        dve.wait_ge(*hl_ok(0, f - 1))
                    dve.scalar_tensor_tensor(gp, ps[0:w, f % 2, :], v("gsc")[0:w, 0, f:f + 1],
                                             v("lg")[0:w, f % 2, :], ALU.mult, ALU.add).then_inc(gp_ok.sem, 1)
                    if f >= 1:
                        dve.wait_ge(*hp_ok(0, f))
                    step(dve.scalar_tensor_tensor(up, ps[0:w, 2 + f % 2, :], v("gsc")[0:w, 1, f:f + 1],
                                                  v("lu")[0:w, f % 2, :], ALU.mult, ALU.add))
                    dve.wait_ge(*sg_ok(0, f + 1))
                    dve.tensor_tensor(gp, gp, up, ALU.mult).then_inc(hp_ok.sem, 1)
                dve.wait_ge(*ud_ok(0, 1))
                ud2 = v("ud2")
                lo, hi = [ud2[:, :, n * R0:(n + 1) * R0].unsqueeze(2).broadcast_to([P, NT, 3, R0]) for n in range(2)]
                dve.tensor_tensor(v("ud3")[:, :, :, :], lo, hi, ALU.add).then_inc(ud3_ok.sem, 1)
                dsum = v("dsum")
                for t in range(NT):
                    ins = dve.tensor_tensor(dsum[:, t, :], ps[:, t, :], v("dsc")[:, :], ALU.mult)
                dve.wait_ge(*udf_ok(0, 1))
                step(dve.tensor_copy(v("udh")[:, :], v("udf")[:, :]))
                dve.tensor_tensor(v("udh")[mid, :], v("udf")[mid, :], v("udh")[mid, :].bitcast(F32), ALU.subtract)\
                   .then_inc(uds_ok.sem, 1)
                for t in range(NT):
                    ins = dve.tensor_tensor(x[:, t, :], x[:, t, :], dsum[:, t, :], ALU.add)
                step(ins)
                dve.wait_ge(*dlo_ok(0, 1))
                for t in range(NT):
                    ins = dve.tensor_tensor(x[:, t, :], x[:, t, :], ps[:, 4 + t, :], ALU.add)
                ins.then_inc(x_ok.sem, 1)

            def cross(k):
                N = B * NPAIR
                norm([2, 6][k])
                dve.wait_ge(*xn_ok([2, 6][k], NT))
                qh, qst = v("qh"), v("qst")
                dve.tensor_copy(qh[:, :, :], xn[:, :, :]).then_inc(qh_ok.sem, 1)
                dve.wait_ge(*qh_ok(k, 1))
                for h in range(2):
                    ins = dve.tensor_tensor(query_slots(qst, h)[:, :, :, 2 * XD:3 * XD], query_heads(xn, h),
                                            query_heads(qh, h).bitcast(F32), ALU.subtract)
                ins.then_inc(qst_ok.sem, 1)

                def maxima(n, qt):
                    b, pr = n // NPAIR, n % NPAIR
                    i = 4 * n + 2 * qt
                    for h in range(2):
                        dve.wait_ge(*xs_ok(k, i + h + 1))
                        if i:
                            dve.wait_ge(*xm_ok(k, i + h - 1))
                        dve.tensor_tensor_reduce(v("junk")[:, h, :], ps[:, 4 + h, :], v("mask_q")[:, qt, :], 1.0,
                                                       -3.0e38, ALU.add, ALU.max,
                                                       qst[:, b * QT + qt, 2 * pr + h, 3 * XD:3 * XD + 1])\
                           .then_inc(xm_ok.sem, 1)

                def masked(n):
                    i, u = 2 * n, 0
                    dve.wait_ge(*xk_ok(k, i + 1))
                    if i >= 4:
                        dve.wait_ge(*pv_ok(k, i - 3))
                    dve.tensor_tensor(v("px%d" % (i % 4))[:, :, :, :].rearrange("p h k q -> p h (k q)"),
                                      ps[:, 2 * u:2 * u + 2, :],
                                      v("mask_k")[:, 2 * u:2 * u + 2, :].rearrange("p k q -> p (k q)").unsqueeze(1)
                                      .broadcast_to([P, 2, 2 * S]), ALU.add).then_inc(ms_ok.sem, 1)

                def divided(g):
                    dve.wait_ge(*ot2_ok(k, g + 1))
                    o = ps[:, 4, :].rearrange("p (n v) -> p n v", v=SLOT)
                    if g:
                        dve.wait_ge(*xo_ok(k, g))
                    step(dve.reciprocal(v("rden")[:, :], o[:, :, XD]))
                    dve.tensor_tensor(v("on")[:, :, :], o[:, :, 0:XD],
                                      v("rden")[:, :].unsqueeze(2).broadcast_to([P, QT * 2 * XR, XD]),
                                      ALU.mult).then_inc(on_ok.sem, 1)

                maxima(0, 0)
                maxima(0, 1)
                maxima(1, 0)
                for n in range(N):
                    if n + 1 < N:
                        maxima(n + 1, 1)
                    masked(n)
                    if n >= XR and n % XR == 1:
                        divided(n // XR - 1)
                    if n + 2 < N:
                        maxima(n + 2, 0)
                divided(N // XR - 1)

            def mixture(k):
                rt = [v("route")[:, i, :, :] for i in range(12)]
                small = v("ve")

                def spread(ap):
                    return ap.unsqueeze(2).broadcast_to([P, NT, E])

                norm([3, 5][k])
                logits = ps[:, 5, 0:NT * E].rearrange("p (t e) -> p t e", t=NT)
                iota = v("iota8")[:, :].unsqueeze(1).broadcast_to([P, NT, E])
                m0, m1, m2 = small[:, 0:4], small[:, 4:8], small[:, 8:12]
                dve.wait_ge(*hl_ps(k, 1))
                step(dve.tensor_reduce(m0, logits, AX.X, ALU.max))
                dve.tensor_tensor(rt[0], logits, spread(m0), ALU.subtract).then_inc(le_ok.sem, 1)
                dve.wait_ge(*ee_ok(k, 1))
                step(dve.tensor_reduce(m0, rt[1], AX.X, ALU.add))
                step(dve.reciprocal(m0, m0))
                step(dve.tensor_tensor(rt[2], rt[1], spread(m0), ALU.mult))

                def first_max(p, m, eq, cand, one):
                    step(dve.tensor_reduce(m, p, AX.X, ALU.max))
                    step(dve.tensor_tensor(eq, p, spread(m), ALU.is_equal))
                    step(dve.scalar_tensor_tensor(cand, eq, -float(E), iota, ALU.mult, ALU.add))
                    step(dve.tensor_reduce(m0, cand, AX.X, ALU.min))
                    step(dve.tensor_scalar(m0, m0, float(E), None, ALU.add))
                    step(dve.tensor_tensor(one, iota, spread(m0), ALU.is_equal))

                first_max(rt[2], m1, rt[3], rt[4], rt[5])
                step(dve.scalar_tensor_tensor(rt[6], rt[5], -4.0, rt[2], ALU.mult, ALU.add))
                first_max(rt[6], m2, rt[7], rt[8], rt[9])
                step(dve.tensor_tensor(rt[10], rt[5], rt[9], ALU.add))
                step(dve.tensor_tensor(rt[10], rt[10], rt[2], ALU.mult))
                step(dve.tensor_tensor(m1, m1, m2, ALU.add))
                step(dve.reciprocal(m1, m1))
                step(dve.tensor_scalar(m1, m1, float(k + 1), None, ALU.mult))
                step(dve.tensor_tensor(rt[11], rt[10], spread(m1), ALU.mult))
                w = rt[11].rearrange("p t e -> p (t e)").unsqueeze(2).broadcast_to([P, NT * E, R])
                dve.tensor_tensor(v("hs")[:, :, :].rearrange("p t (e r) -> p (t e) r", r=R),
                                  ps[:, 4, :].rearrange("p (n r) -> p n r", r=R), w, ALU.mult).then_inc(hw_ok.sem, 1)
                dve.wait_ge(*xb_ok(k, 1))
                for t in range(NT):
                    dve.wait_ge(*base_ok(k, t + 1))
                    ins = dve.tensor_tensor(x[:, t, :], x[:, t, :], ps[:, t, :], ALU.add)
                ins.then_inc(x_ok.sem, 1)

            def feed3():
                sc, inv = v("sc3"), v("isc3")
                inter = v("inter")

                def quantise(m, t, src, done):
                    step(dve.tensor_reduce(sc[:, m, t:t + 1], src, AX.X, ALU.max, apply_absolute_value=True))
                    step(dve.tensor_scalar(sc[:, m, t:t + 1], sc[:, m, t:t + 1], 1.0 / QMAX, QEPS,
                                           ALU.mult, ALU.max))
                    step(dve.reciprocal(inv[:, m, t:t + 1], sc[:, m, t:t + 1]))
                    step(dve.tensor_scalar(src, src, inv[:, m, t:t + 1], MAGIC, ALU.mult, ALU.add))
                    dve.tensor_scalar(src, src, MAGIC + QMAX, MAGIC - QMAX - 1, ALU.min, ALU.max)\
                       .then_inc(done.sem, 1)

                norm(7)
                for t in range(NT):
                    dve.wait_ge(*xn_ok(7, t + 1))
                    quantise(0, t, xn[:, t, :], xq_ok)
                for blk in range(NB3):
                    for t in range(NT):
                        i = blk * NT + t
                        dve.wait_ge(*si_ok(0, i + 1))
                        dve.scalar_tensor_tensor(inter[:, t, blk * W3:(blk + 1) * W3], ps[:, 2 + i % 2, 0:W3],
                                                 sc[:, 0, t:t + 1], v("sil%d" % (i % 2))[:, :], ALU.mult, ALU.mult)\
                           .then_inc(in_ok.sem, 1)
                        if blk == NB3 - 1:
                            dve.wait_ge(*in_ok(0, i + 1))
                            quantise(1, t, inter[:, t, :], iq_ok)
                for t in range(NT):
                    dve.wait_ge(*dn_ok(0, 4 * NT + t + 1))
                    ins = dve.scalar_tensor_tensor(x[:, t, :], ps[:, t, :], sc[:, 1, t:t + 1], x[:, t, :],
                                                   ALU.mult, ALU.add)
                ins.then_inc(x_ok.sem, 1)

            dve.wait_ge(*ident_ok(0, 1))
            dve.tensor_copy(identr[:, :], ident[:, :]).then_inc(constr.sem, 1)
            dve.tensor_copy(v("causal")[:, :], v("causal0")[:, :]).then_inc(constr.sem, 1)
            dve.wait_ge(*pos_in(0, 16))
            ang, turn, cos = v("ang"), v("turn"), v("cos")
            for d in range(HD // 2):
                inv = float(np.float32(1.0) / np.float32(10000.0) ** np.float32(d / (HD // 2)))
                ins = dve.tensor_scalar(ang[:, :, d], v("pos")[:, :], inv, None, ALU.mult)
            step(ins)
            step(dve.tensor_scalar(turn[:, :, :], ang[:, :, :], 1.0 / (2.0 * np.pi), MAGIC, ALU.mult, ALU.add))
            step(dve.tensor_scalar(turn[:, :, :], turn[:, :, :], MAGIC, None, ALU.subtract))
            c1 = 6.28125
            c2 = float(np.round((2.0 * np.pi - c1) * 2 ** 20) / 2 ** 20)
            for c in (c1, c2, 2.0 * np.pi - c1 - c2):
                step(dve.scalar_tensor_tensor(ang[:, :, :], turn[:, :, :], -c, ang[:, :, :], ALU.mult, ALU.add))
            step(dve.tensor_scalar(ang[:, :, :], ang[:, :, :], 3.1415925, -3.1415925, ALU.min, ALU.max))
            step(dve.scalar_tensor_tensor(turn[:, :, :], ang[:, :, :], -1.0, ang[:, :, :], ALU.mult, ALU.max))
            dve.tensor_scalar(turn[:, :, :], turn[:, :, :], -1.0, float(np.pi / 2), ALU.mult, ALU.add)\
               .then_inc(ang_ok.sem, 1)
            rat(0)
            feed0()
            cross(0)
            mixture(0)
            rat(1)
            mixture(1)
            cross(1)
            feed3()

        @block.gpsimd
        def _(pool):
            def step(ins):
                link(pool, "pool", ins)

            def inverse_root(src, n, done):
                step(pool.tensor_scalar(ve[:, 0:n], mv[:, 0:n, 1], EPS, None, ALU.add))
                pool.tensor_tensor(rstd[:, 0:n], ve[:, 0:n], v("powc")[:, 0:n], ALU.pow).then_inc(done.sem, 1)

            def norm(n, scale=None):
                pool.wait_ge(*mv_ok(n, 1))
                if scale is None:
                    inverse_root(mv, NT, rstd_ok)
                    return
                step(pool.tensor_scalar(ve[:, 0:NT], mv[:, 0:NT, 1], EPS, None, ALU.add))
                step(pool.tensor_tensor(rstd[:, 0:NT], ve[:, 0:NT], v("powc")[:, 0:NT], ALU.pow))
                pool.tensor_scalar(rstd[:, 0:NT], rstd[:, 0:NT], scale, None, ALU.mult).then_inc(rstd_ok.sem, 1)

            def rat_read(k, half, nout):
                pool.wait_ge(*ymv_ok(2 * k + half, 1))
                inverse_root(mv, NT * nout, yrstd_ok)

            def rat_pads(k):
                qks, vs_ = v("qks%d" % k), v("vs%d" % k)
                if k:
                    pool.wait_ge(*x_ok(3, 1))
                pool.memset(qks[:, :, :, :, :], 0.0)
                step(pool.memset(vs_[:, :, :, :], 0.0))
                pool.memset(qks[:, :, 1, :, 3 * HD:3 * HD + 1], -1.0)
                pool.memset(vs_[:, :, :, HD:HD + 1], 1.0).then_inc(pads.sem, 1)

            def rat_attention(k):
                for i in range(B * NG):
                    pool.wait_ge(*p_ok(k, i + 1))
                    for c in (0, 2 * P):
                        m = v("p%d%d" % (k, i % 2))[:, :, c:c + P]
                        ins = pool.affine_select(out=m, in_=m, pattern=[[0, GH], [1, P]], compare_op=ALU.is_ge,
                                                 fill=0.0, base=0, channel_multiplier=-1)
                    ins.then_inc(pm_ok.sem, 1)

            def rat_write(k, half):
                i = 2 * k + half
                sp, ab, os_ = v("sp%d" % k), v("ab%d" % k), v("os%d" % k)
                pool.wait_ge(*sp_ok(i, 1))
                for t in range(NT):
                    delta = sp[:, t, AS:AS + H]
                    pool.tensor_tensor(
                        v("u%d" % k)[:, t, :, :].rearrange("p (s r) c -> p s r c", s=HS),
                        delta.rearrange("p (s r) -> p s r", s=HS).unsqueeze(3).broadcast_to([P, HS, RH, C3]),
                        sp[:, t, 0:AS].rearrange("p (r c) -> p r c", c=C3).unsqueeze(1)
                        .broadcast_to([P, HS, RH, C3]), ALU.mult).then_inc(u_ok.sem, 1)
                pool.wait_ge(*os_ok(i, 1))
                for t in range(NT):
                    delta = sp[:, t, AS:AS + H]
                    hs = xn[:, t, :].rearrange("p (h c) -> p h c", c=C)
                    skip = v("silu%d0" % k)[:, t * P:(t + 1) * P]
                    step(pool.tensor_tensor(
                        skip.rearrange("p (s r) -> p s r", s=HS), delta.rearrange("p (s r) -> p s r", s=HS),
                        ab[:, t, 2 * AS:NAB].unsqueeze(1).broadcast_to([P, HS, RH]), ALU.mult))
                    step(pool.tensor_tensor(skip, skip, os_[:, t, :], ALU.mult))
                    pool.tensor_tensor(hs[:, :, C3], hs[:, :, C3], skip, ALU.add)
                    pool.wait_ge(*abar_ok(i, t + 1))
                    pool.tensor_tensor(hs[:, :, 0:C3], hs[:, :, 0:C3], v("u%d" % k)[:, t, :, :], ALU.mult)\
                        .then_inc(ah_ok.sem, 1)

            def convert(m):
                src, dst = (("gq", "gi"), ("uq", "ui"), ("dq", "di"))[m]
                pool.wait_ge(*q_in[m](0, 16 * DC))
                pool.tensor_scalar(v(dst)[:, :, :], v(src)[:, :, :], -QZERO, None, ALU.add).then_inc(qi_ok.sem, 1)

            def rat(k):
                norm(RATN[k])
                rat_pads(k)
                rat_read(k, 0, 3)
                rat_attention(k)
                rat_write(k, 0)
                if k == 0:
                    convert(0)
                rat_read(k, 1, 2)
                if k == 0:
                    convert(1)
                rat_write(k, 1)
                if k == 0:
                    convert(2)

            def feed0():
                norm(1)
                pool.wait_ge(*ff_in(0, 16 * 8))
                last = slice(2 * R0, 3 * R0)
                pairs = [(v("gB"), v("gBraw")), (v("uB"), v("uBraw")), (v("dB"), v("dBraw"))]
                for dst, src in pairs:
                    ins = pool.tensor_copy(dst[:, :], src[:, :])
                for m in (v("gsc")[:, :, :], v("dsc")[:, :]):
                    pool.tensor_scalar(m, m, QSTEP, None, ALU.mult)
                dA = v("dA")
                step(pool.tensor_copy(dA[:, :, 0:R0], v("dAraw")[:, :, :]))
                for dst, src in pairs:
                    step(pool.tensor_tensor(dst[last, :], src[last, :], dst[last, :].bitcast(F32), ALU.subtract))
                pool.tensor_tensor(dA[:, :, R0:2 * R0], v("dAraw")[:, :, :], dA[:, :, 0:R0].bitcast(F32),
                                   ALU.subtract).then_inc(fb_ok.sem, 1)
                pool.wait_ge(*fb_ok(0, 1))
                for f in range(F0):
                    w = F0W[f]
                    pool.wait_ge(*hh_ok(0, f + 1))
                    pool.tensor_tensor(v("hl")[0:w, f, :], v("gp")[0:w, f % 2, :], v("hh")[0:w, f, :].bitcast(F32),
                                       ALU.subtract).then_inc(hl_ok.sem, 1)

            def context():
                kst, vx, ch, cx = v("kst"), v("vx"), v("ch"), v("ctx")
                pool.wait_ge(*d_ok(0, 1))
                pool.memset(kst[:, :, :, 3 * XD:XSLOT], 0.0)
                step(pool.tensor_copy(ch[:, :, :], cx[:, :, :]))
                hi = ch[:, :, :].rearrange("p j (g d) -> p j g d", d=XD)
                raw = cx[:, :, :].rearrange("p j (g d) -> p j g d", d=XD)
                hif = ch[:, :, :].bitcast(F32).rearrange("p j (g d) -> p j g d", d=XD)
                pool.memset(kst[:, :, :, 3 * XD:XK], -1.0)
                pool.tensor_copy(kst[:, :, :, 0:XD], hi)
                pool.tensor_copy(kst[:, :, :, 2 * XD:3 * XD], hi)
                pool.tensor_tensor(kst[:, :, :, XD:2 * XD], raw, hif, ALU.subtract).then_inc(kst_ok.sem, 1)
                pool.memset(vx[:, :, :, XV:SLOT], 0.0)
                pool.memset(vx[:, :, :, XD:XV], 1.0)
                pool.tensor_copy(vx[:, :, :, 0:XD], raw).then_inc(vx_ok.sem, 1)

            def cross(k):
                N = B * NPAIR
                norm([2, 6][k], scale=float(XD) ** -0.5)
                pool.memset(v("qst")[:, :, :, 3 * XD:XSLOT], 0.0)
                pool.wait_ge(*qh_ok(k, 1))
                for h in range(2):
                    ins = pool.tensor_copy(query_slots(v("qst"), h)[:, :, :, XD:2 * XD], query_heads(v("qh"), h))
                ins.then_inc(qst_ok.sem, 1)

                mh = v("mh")
                mask = v("mask_k")[:, 2:KT, :]
                step(pool.tensor_copy(v("mkh")[:, :, :], mask))
                pool.tensor_tensor(v("mkl")[:, :, :], mask, v("mkh")[:, :, :].bitcast(F32), ALU.subtract)\
                    .then_inc(mk_ok.sem, 1)

                def parts(n):
                    b, pr = n // NPAIR, n % NPAIR
                    top = v("qst")[:, b * QT:(b + 1) * QT, 2 * pr:2 * pr + 2, 3 * XD:XK]
                    pool.wait_ge(*xm_ok(k, 4 * n + 4))
                    if n:
                        pool.wait_ge(*ml_ok(k, n))
                    pool.tensor_copy(mh[:, :, :], top[:, :, :, 0]).then_inc(mh_ok.sem, 1)
                    pool.wait_ge(*mh_ok(k, n + 1))
                    pool.tensor_tensor(top[:, :, :, 1], top[:, :, :, 0], mh[:, :, :].bitcast(F32), ALU.subtract)\
                        .then_inc(ml_ok.sem, 1)

                def added(g):
                    b, gp = g // (XG // 2), g % (XG // 2)
                    pool.wait_ge(*on_ok(k, g + 1))
                    for qt in range(QT):
                        xv = x[:, b * QT + qt, gp * 2 * XR * XD:(gp + 1) * 2 * XR * XD]\
                            .rearrange("p (h m d) -> p m h d", h=2, m=2)
                        on = v("on")[:, :, :].rearrange("p (m q h e) d -> p m q h (e d)", m=2, q=QT, h=2)
                        ins = pool.tensor_tensor(xv, xv, on[:, :, qt, :, :], ALU.add)
                    ins.then_inc(xo_ok.sem, 1)

                for n in range(N):
                    parts(n)
                    if n > XR and n % XR == 2:
                        added(n // XR - 1)
                added(N // XR - 1)
                pool.wait_ge(*xo_ok(k, N // XR))
                pool.sem_inc(x_ok.sem, 1)

            def mixture(k):
                norm([3, 5][k])
                pool.wait_ge(*xn_ok([3, 5][k], NT))
                pool.wait_ge(*mix_in(k, 32))
                bias = v("mw")[:, MP["b"][0]:MP["b"][1]].unsqueeze(1).broadcast_to([P, NT, D])
                pool.tensor_tensor(x[:, :, :], x[:, :, :], bias, ALU.add).then_inc(xb_ok.sem, 1)

            def feed3():
                norm(7)
                for i, (m, at, n) in enumerate(ITEMS):
                    pool.wait_ge(*wc_ok(0, i + 1))
                    s = i % 3
                    pool.tensor_tensor(v("wlo%d" % s)[:, 0:n], v("wraw%d" % s)[:, 0:n],
                                       v("whi%d" % s)[:, 0:n].bitcast(F32), ALU.subtract).then_inc(wl_ok.sem, 1)

            c0, sel = v("causal0"), v("sel")
            pool.memset(ident[:, :], 0.0)
            pool.memset(c0[:, :], 0.0)
            pool.memset(sel[:, :], 1.0)
            pool.memset(v("powc")[:, 0:12], -0.5)
            pool.memset(v("powc")[:, 12:16], -1.0)
            step(pool.memset(v("dl")[:, :], 1.0))
            for c in (0, 2 * P):
                pool.affine_select(out=c0[:, c:c + P], in_=c0[:, c:c + P], pattern=[[-1, P]], compare_op=ALU.is_ge,
                                   fill=-1e30, base=0, channel_multiplier=1)
            pool.affine_select(out=ident[:, :], in_=ident[:, :], pattern=[[-1, P]], compare_op=ALU.not_equal,
                               fill=1.0, base=0, channel_multiplier=1).then_inc(ident_ok.sem, 1)
            pool.iota(v("iota8")[:, :], [[1, E]], base=-E, channel_multiplier=0,
                      allow_small_or_imprecise_dtypes=True)
            step(pool.affine_select(out=sel[:, :], in_=sel[:, :], pattern=[[-C, SLOT]], compare_op=ALU.is_ge,
                                    fill=0.0, base=0, channel_multiplier=1))
            pool.affine_select(out=sel[:, :], in_=sel[:, :], pattern=[[C, SLOT]], compare_op=ALU.is_ge,
                               fill=0.0, base=C - 1, channel_multiplier=-1).then_inc(const_ok.sem, 1)
            rat(0)
            feed0()
            context()
            cross(0)
            mixture(0)
            rat(1)
            mixture(1)
            cross(1)
            feed3()


def kernel(**inputs):
    import numpy as _np
    import concourse.bacc as _bacc
    from concourse import mybir as _mybir
    from concourse.bass_utils import run_bass_kernel_spmd as _run

    g = {n: _np.asarray(w) for n, w in inputs.items()}
    cat = _np.concatenate

    def tiles(m):
        n = m.shape[0] // P
        return m.reshape(n, P, -1).transpose(1, 0, 2).reshape(P, -1)

    def padded(m):
        return cat([m, _np.zeros((F0 * P - m.shape[0],) + m.shape[1:], m.dtype)])

    def thrice(m):
        return cat([m, m, m], axis=0)

    arrays = {
        "x": g["x"].reshape(T, D), "pos": tiles(g["pos_BxS"].reshape(T, 1)),
        "ctx": g["ctx_1024"].reshape(B * S2, CD), "mask": g["mask_SxS2_ff0"], "maskT": g["mask_SxS2_ff0"].T,
        "gq": g["L0_ffn_gate_q"].T, "uq": g["L0_ffn_up_q"].T, "dq": padded(g["L0_ffn_down_q"].T),
        "gA": tiles(cat([g["L0_ffn_gate_A"]] * 3, axis=1)).reshape(P, DC, 3 * R0),
        "uA": tiles(cat([g["L0_ffn_up_A"]] * 3, axis=1)).reshape(P, DC, 3 * R0),
        "gBraw": thrice(g["L0_ffn_gate_B"]), "uBraw": thrice(g["L0_ffn_up_B"]), "dBraw": thrice(g["L0_ffn_down_B"]),
        "dAraw": tiles(padded(g["L0_ffn_down_A"])).reshape(P, F0, R0),
        "gsc": cat([tiles(padded(g["L0_ffn_%s_scale" % n][:, None])) for n in ("gate", "up")], 1).reshape(P, 2, F0),
        "dsc": g["L0_ffn_down_scale"].reshape(1, D),
        "wg": g["L3_ffn_w_gate"].T, "wu": g["L3_ffn_w_up"].T, "wd": g["L3_ffn_w_down"].T,
    }
    for k, name in enumerate(("L0_xattn_", "L2_xattn_")):
        def w(n):
            return g[name + n]

        def read(half):
            return tiles(w(half + "_read_w").transpose(0, 2, 1).reshape(H * C, -1))

        def per_channel(n):
            return w(n).reshape(-1, H).T

        def both(half):
            return cat([w(half + "_wod_w"), w(half + "_wab_w")]).T

        arrays["rw%d" % k] = cat([
            read("attn"), per_channel("attn_read_g"), per_channel("attn_read_b"),
            w("qkv_w").transpose(2, 0, 1).reshape(H, 3 * H), both("attn"),
            read("mlp"), per_channel("mlp_read_g"), per_channel("mlp_read_b"), tiles(both("mlp"))], axis=1)
        arrays["rrow%d" % k] = _np.stack([w("attn_wab_b"), w("mlp_wab_b")])
        arrays["du%d" % k] = _np.stack([cat([w(h + "_du_w").T, w(h + "_du_b")[None]]) for h in ("attn", "mlp")], 1)
    for k, (pre, gate, low, up) in enumerate((("L1_ffn_", "W_gate", "A", "B"),
                                              ("L2_ffn_", "W_router", "lora_A", "lora_B"))):
        ag = cat([g[pre + low].reshape(ER, D), g[pre + gate]]).T
        arrays["mw%d" % k] = cat([tiles(g[pre + "W_base"].T), tiles(ag),
                                  _np.broadcast_to(g[pre + "b_base"], (P, D))], axis=1)
        arrays["mB%d" % k] = g[pre + up].transpose(0, 2, 1).reshape(ER, D)

    nc = _bacc.Bacc("TRN2", target_bir_lowering=False, num_devices=1)
    feeds, aps = {}, {}
    for name, m in arrays.items():
        m = _np.ascontiguousarray(m)
        feeds["in_" + name] = m
        aps[name] = nc.dram_tensor("in_" + name, m.shape, _mybir.dt.from_np(m.dtype), kind="ExternalInput").ap()
    out = nc.dram_tensor("out_0_dram", (T, D), F32, kind="ExternalOutput").ap()
    program(nc, aps, out)
    r = _run(nc, [feeds], core_ids=[0])
    return r.results[0]["out_0_dram"].reshape(B, S, D)
```

```python
from contextlib import ExitStack

import concourse.bass as bass
from concourse import mybir
import numpy as np

ALU = mybir.AluOpType
ACT = mybir.ActivationFunctionType
F32 = mybir.dt.float32
F32R = mybir.dt.float32r
I32 = mybir.dt.int32
AX = mybir.AxisListType

P = 128
B, S, D = 2, 256, 512
NT = B * S // P
QT = S // P
DC = D // P
T = B * S
S2, CD = 512, 128
KT = S2 // P
EPS = 1e-5

H, C, RH, DR, NH, HD = 128, 4, 16, 8, 16, 8
HS = H // RH
C3 = C - 1
AS = C3 * RH
NAB = 2 * AS + RH
NW = H + DR + NAB
MC = S2 // P
SLOT = 32
GH = P // SLOT
NG = NH // GH

XH, XG, XD = 32, 8, 16
XSLOT = 64
NPAIR = XH // 2
XK = 3 * XD + 2
XV = XD + 1
XR = XH // XG

I0, R0, QZERO, QSTEP, LRS = 1376, 32, 7.5, 0.005, 0.02
F0 = (I0 + P - 1) // P
F0W = [min(P, I0 - P * f) for f in range(F0)]

E, R = 8, 16
ER = E * R

I3 = 1792
NB3 = 4
W3 = I3 // NB3
WS = 4
F3 = I3 // P
QMAX, QEPS = 127.0, 1e-8
MAGIC = 1.5 * 2.0 ** 23

RP = {}
_at = 0
for _name, _n in (("rw", DC * 3), ("rg", 3), ("rb", 3), ("qkv", 3 * H), ("wcat", NW),
                  ("mw", DC * 2), ("mg", 2), ("mb", 2), ("mcat", MC * NW)):
    RP[_name] = (_at, _at + _n)
    _at += _n
RPN = _at
MP = {"base": (0, DC * D), "ag": (DC * D, DC * D + DC * (ER + E)), "b": (DC * D + DC * (ER + E), DC * D + DC * (ER + E) + D)}
MPN = MP["b"][1]


class Signal:

    def __init__(self, sem, per):
        self.sem, self.per = sem, per

    def __call__(self, k, n):
        assert 0 < n <= self.per, (self.sem, k, n)
        return self.sem, k * self.per + n


def sbuf_map(nc, first):
    buf, at = {}, {}

    def lay(end, *items):
        for name, shape, dt in items:
            buf[name] = nc.alloc_sbuf_tensor_at(name, shape, dt, offset=end)
            at[name] = end
            end += (int(np.prod(shape[1:])) * 4 + 31) // 32 * 32
        return end

    mix = lay(first,
              ("ident", [P, P], F32), ("identr", [P, P], F32R),
              ("causal0", [P, 3 * P], F32), ("causal", [P, 3 * P], F32R),
              ("sel", [P, SLOT], F32),
              ("iota8", [P, E], F32), ("powc", [P, 16], F32), ("tiny", [P, 2], F32),
              ("mask_q", [P, QT, S2], F32), ("mask_k", [P, KT, S], F32),
              ("x", [P, NT, D], F32), ("xn", [P, NT, D], F32), ("xnT", [P, DC, T], F32),
              ("ctx", [P, B * KT, CD], F32), ("ctxT", [P, B, S2], F32),
              ("rw", [P, RPN], F32), ("rrow", [P, 2, NAB], F32), ("du", [DR + 1, 2, H], F32),
              ("dl", [DR + 1, T], F32), ("wd", [P, DC, 3, SLOT], F32),
              ("pos", [P, NT], I32), ("ang", [P, NT, HD // 2], F32), ("turn", [P, NT, HD // 2], F32),
              ("cos", [P, NT, HD // 2], F32), ("sin", [P, NT, HD // 2], F32),
              ("stats", [P, 12, 6], F32), ("mv", [P, 12, 2], F32), ("ve", [P, 12], F32), ("rstd", [P, 12], F32),
              ("sc3", [P, 2, NT], F32), ("isc3", [P, 2, NT], F32), ("route", [P, 12, NT, E], F32))
    low = max(lay(mix, ("gA", [P, DC, 3 * R0], F32), ("uA", [P, DC, 3 * R0], F32),
                  ("gB", [3 * R0, I0], F32R), ("uB", [3 * R0, I0], F32R),
                  ("dA", [P, F0, 2 * R0], F32R), ("gsc", [P, 2, F0], F32), ("dsc", [P, D], F32),
                  ("dB", [3 * R0, D], F32R)),
              lay(mix, ("mw", [P, MPN], F32), ("mB", [P, D], F32), ("hs", [P, NT, ER], F32),
                  ("hsT", [P, T], F32)))

    def rat(k, start):
        qk = [P, NT, 2, H]
        a = lay(start, ("qks%d" % k, [P, NT, 2, NH, SLOT], F32))
        b = lay(a, ("vs%d" % k, [P, NT, NH, SLOT], F32), ("kT%d" % k, [P, NG, T], F32R))
        c = lay(b, ("yn%d" % k, [P, NT, 3, H], F32), ("ynT%d" % k, [P, 3, T], F32))
        lay(b, ("p%d0" % k, [P, GH, 3 * P], F32), ("p%d1" % k, [P, GH, 3 * P], F32))
        d = lay(c, ("qk%d" % k, qk, F32), ("qkr%d" % k, qk, F32))
        lay(c, ("qT%d" % k, [P, NG, T], F32R))
        e = lay(d, ("qkh%d" % k, qk, F32R))
        end = lay(e, ("oT%d0" % k, [P, S], F32), ("oT%d1" % k, [P, S], F32),
                  ("y%d" % k, [P, NT, H], F32), ("yT%d" % k, [P, 1, T], F32))
        assert lay(start, ("u%d" % k, [P, NT, H, C3], F32), ("t%d" % k, [P, NT, H, C3], F32),
                   ("os%d" % k, [P, NT, H], F32), ("ab%d" % k, [P, NT, NAB], F32)) <= a
        assert lay(a, ("sp%d" % k, [P, NT, AS + H], F32), ("gg%d" % k, [P, NT, AS], F32)) <= a + 8192
        lay(a + 8192, ("gT%d" % k, [P, MC, T], F32))
        lay(c, ("az%d" % k, [P, NT, AS + H], F32), ("ln%d" % k, [P, NT, AS + H], F32))
        lay(d, ("silu%d0" % k, [P, T], F32), ("silu%d1" % k, [P, T], F32))
        return end

    high = rat(0, low)
    high = max(high, lay(low, ("hh", [P, F0, T], F32R), ("hl", [P, F0, T], F32R),
                         ("xh", [P, DC, T], F32R), ("xl", [P, DC, T], F32R)))
    lay(low, ("gBraw", [3 * R0, I0], F32), ("uBraw", [3 * R0, I0], F32), ("dAraw", [P, F0, R0], F32),
        ("dBraw", [3 * R0, D], F32))
    lay(at["xn"], ("us", [3 * R0, 2, T], F32R), ("ug", [3 * R0, 2, T], F32))
    lay(at["xnT"], ("lg", [P, 2, T], F32), ("lu", [P, 2, T], F32))
    assert lay(at["rw"], ("gp", [P, 2, T], F32), ("up", [P, T], F32)) <= at["rrow"]
    lay(at["xn"], ("udh", [3 * R0, T], F32R), ("udf", [3 * R0, T], F32), ("ud2", [P, NT, 2 * R0], F32),
        ("ud3", [P, NT, 3, R0], F32))
    lay(low, ("dsum", [P, NT, D], F32))
    kv = lay(low, ("kx", [P, XG // 2, B * S2], F32R), ("vx", [P, B * KT, XG, SLOT], F32))
    lay(kv, ("kst", [P, B * KT, XG, XSLOT], F32), ("ch", [P, B * KT, CD], F32R))
    assert lay(kv, ("qt0", [P, S], F32R), ("qt1", [P, S], F32R), ("qm0", [P, S], F32R), ("qm1", [P, S], F32R),
               ("ox0", [P, 2, S], F32), ("ox1", [P, 2, S], F32), ("on", [P, QT * 2 * XR, XD], F32), ("rden", [P, QT * 2 * XR], F32)) <= high
    assert lay(high, ("qst", [P, NT, XH, XSLOT], F32), *[("px%d" % i, [P, 2, 2, S], F32) for i in range(4)],
               ("junk", [P, 2, S2], mybir.dt.bfloat16), ("mkh", [P, 2, S], F32R), ("mkl", [P, 2, S], F32R),
               ("mh", [P, QT, 2], F32R)) <= nc.sbuf_usable_end
    lay(at["xnT"], ("qh", [P, NT, D], F32R))
    assert lay(low, ("inter", [P, NT, I3], F32), ("iqT", [P, F3, T], F32R)) <= high
    lay(at["xnT"], ("xqT", [P, DC, T], F32R))
    assert lay(high, *[("w%s%d" % (n, i), [P, DC * W3], F32R) for n in ("hi", "lo") for i in range(WS)],
               ("sil0", [P, W3], F32), ("sil1", [P, W3], F32)) <= nc.sbuf_usable_end
    assert lay(mix, ("wraw0", [P, DC * W3], F32), ("wraw1", [P, DC * W3], F32)) <= low
    assert lay(at["ctx"], ("wraw2", [P, DC * W3], F32)) <= at["rw"]
    assert lay(at["rw"], ("wraw3", [P, DC * W3], F32)) <= at["dl"]
    ends = [lay(high, ("gi", [P, DC, I0], F32R), ("ui", [P, DC, I0], F32R), ("di", [P, F0, D], F32R)),
            lay(high, ("gq", [P, DC, I0], I32), ("uq", [P, DC, I0], I32), ("dq", [P, F0, D], I32)),
            rat(1, high)]
    assert max(ends) <= nc.sbuf_usable_end
    return buf


def program(nc, a, out):
    with ExitStack() as ctx:
        buf = sbuf_map(nc, (nc.sbuf_base + 31) // 32 * 32)
        ps = ctx.enter_context(nc.psum_tensor("ps", [P, 8, 512], F32))

        def v(name):
            return buf[name]

        def signal(name, per):
            return Signal(ctx.enter_context(nc.semaphore(name)), per)

        x, xn, xnT = v("x"), v("xn"), v("xnT")
        ident, identr = v("ident"), v("identr")
        stats, mv, ve, rstd = v("stats"), v("mv"), v("ve"), v("rstd")
        RATN = [0, 4]

        x_in = signal("x_in", 16)
        pos_in = signal("pos_in", 16)
        small_in = signal("small_in", 16 * 3)
        rat_in = signal("rat_in", 16 * 3)
        ff_in = signal("ff_in", 16 * 8)
        q_in = [signal("q_in%d" % i, 16 * DC) for i in range(3)]
        mix_in = signal("mix_in", 16 * 2)
        w_in = [signal("w_in%d" % i, 16) for i in range(WS)]
        stored = signal("stored", 16 * NT)
        ident_ok = signal("ident_ok", 1)
        const_ok = signal("const_ok", 1)
        constr = signal("constr", 2)
        rope_ok = signal("rope_ok", 1)
        ang_ok = signal("ang_ok", 1)
        ctxt_ok = signal("ctxt_ok", 1)
        ctxT_ok = signal("ctxT_ok", 1)
        mv_ok = signal("mv_ok", NT)
        rstd_ok = signal("rstd_ok", NT)
        xn_ok = signal("xn_ok", NT)
        xa_ok = signal("xa_ok", NT // 2)
        x_ok = signal("x_ok", 1)
        tr_ok = signal("tr_ok", NT)
        xnT_ok = signal("xnT_ok", NT)
        wd_ok = signal("wd_ok", 1)
        y_ok = signal("y_ok", NT)
        ymv_ok = signal("ymv_ok", NT)
        yrstd_ok = signal("yrstd_ok", NT)
        yn_ok = signal("yn_ok", NT)
        ynt_ok = signal("ynt_ok", 5)
        ynT_ok = signal("ynT_ok", 5)
        qkv_ok = signal("qkv_ok", NT)
        qk_sb = signal("qk_sb", 2 * NT)
        pads = signal("pads", 1)
        qkh_ok = signal("qkh_ok", 1)
        qks_ok = signal("qks_ok", 2)
        st_ok = signal("st_ok", 3 * NG)
        sT_ok = signal("sT_ok", 3 * NG)
        s_ok = signal("s_ok", B * NG)
        max_ok = signal("max_ok", B * NG)
        sk_ok = signal("sk_ok", 2 * B * NG)
        p_ok = signal("p_ok", 2 * B * NG)
        pm_ok = signal("pm_ok", 2 * B * NG)
        o_ok = signal("o_ok", 2 * B * NG)
        oT_ok = signal("oT_ok", B * NG)
        ot_ok = signal("ot_ok", B * NG)
        yy_ok = signal("yy_ok", B * NG)
        yt_ok = signal("yt_ok", 1)
        yT_ok = signal("yT_ok", 1)
        gate_ok = signal("gate_ok", MC)
        silu_ok = signal("silu_ok", MC)
        g_ok = signal("g_ok", MC)
        w1_ok = signal("w1_ok", 1)
        w2_ok = signal("w2_ok", 1)
        dl_ok = signal("dl_ok", 1)
        w3_ok = signal("w3_ok", 1)
        os_ok = signal("os_ok", 1)
        ab_ok = signal("ab_ok", 1)
        e_ok = signal("e_ok", 1)
        ln_ok = signal("ln_ok", 1)
        sp_ok = signal("sp_ok", 1)
        u_ok = signal("u_ok", NT)
        abar_ok = signal("abar_ok", NT)
        ah_ok = signal("ah_ok", NT)
        hid_ok = signal("hid_ok", 2 * NT)
        qi_ok = signal("qi_ok", 3)
        fh_ok = signal("fh_ok", 1)
        fb_ok = signal("fb_ok", 2)
        chi_ok = signal("chi_ok", 1)
        xhl_ok = signal("xhl_ok", 1)
        la_ok = signal("la_ok", 1)
        ug_ok = signal("ug_ok", 1)
        us_ok = signal("us_ok", 1)
        f_ok = signal("f_ok", F0)
        lc_ok = signal("lc_ok", F0)
        gp_ok = signal("gp_ok", F0)
        sg_ok = signal("sg_ok", F0)
        hp_ok = signal("hp_ok", F0)
        hh_ok = signal("hh_ok", F0)
        hl_ok = signal("hl_ok", F0)
        d_ok = signal("d_ok", 1)
        ud_ok = signal("ud_ok", 1)
        ud3_ok = signal("ud3_ok", 1)
        udt_ok = signal("udt_ok", 1)
        udf_ok = signal("udf_ok", 1)
        uds_ok = signal("uds_ok", 1)
        dlo_ok = signal("dlo_ok", 1)
        kst_ok = signal("kst_ok", 2)
        vx_ok = signal("vx_ok", 1)
        kt_ok = signal("kt_ok", XG)
        kx_ok = signal("kx_ok", XG)
        qh_ok = signal("qh_ok", 1)
        qst_ok = signal("qst_ok", 3)
        qt_ok = signal("qt_ok", B * NPAIR)
        qT_ok = signal("qT_ok", B * NPAIR)
        xs_ok = signal("xs_ok", 4 * B * NPAIR)
        xm_ok = signal("xm_ok", 4 * B * NPAIR)
        qm_ok = signal("qm_ok", B * NPAIR)
        qM_ok = signal("qM_ok", B * NPAIR)
        xk_ok = signal("xk_ok", 2 * B * NPAIR)
        ms_ok = signal("ms_ok", B * NPAIR)
        mk_ok = signal("mk_ok", 1)
        mh_ok = signal("mh_ok", B * NPAIR)
        ml_ok = signal("ml_ok", B * NPAIR)
        px_ok = signal("px_ok", 2 * B * NPAIR)
        pv_ok = signal("pv_ok", 2 * B * NPAIR)
        ox_ok = signal("ox_ok", B * NPAIR // 2)
        ot2_ok = signal("ot2_ok", B * NPAIR // XR)
        on_ok = signal("on_ok", B * NPAIR // XR)
        xo_ok = signal("xo_ok", B * NPAIR // XR)
        hl_ps = signal("hl_ps", 1)
        le_ok = signal("le_ok", 1)
        ee_ok = signal("ee_ok", 1)
        hw_ok = signal("hw_ok", 1)
        ht_ok = signal("ht_ok", 1)
        hT_ok = signal("hT_ok", 1)
        base_ok = signal("base_ok", NT)
        xb_ok = signal("xb_ok", 1)
        xq_ok = signal("xq_ok", NT)
        wc_ok = signal("wc_ok", 13)
        wl_ok = signal("wl_ok", 13)
        gu_ok = signal("gu_ok", NB3 * NT)
        si_ok = signal("si_ok", NB3 * NT)
        in_ok = signal("in_ok", NB3 * NT)
        iq_ok = signal("iq_ok", NT)
        it_ok = signal("it_ok", 4 * NT)
        iT_ok = signal("iT_ok", 4 * NT)
        dn_ok = signal("dn_ok", 5 * NT)
        result_ok = signal("result_ok", NT)
        step_done = {n: signal(n + "_step", 1 << 20) for n in ("dve", "pool", "act")}
        steps = {"dve": 0, "pool": 0, "act": 0}

        def link(e, name, ins):
            steps[name] += 1
            ins.then_inc(step_done[name].sem, 1)
            e.wait_ge(step_done[name].sem, steps[name])

        block = ctx.enter_context(nc.Block())

        ITEMS = [(m, blk, DC * W3) for blk in range(NB3) for m in ("wg", "wu")]
        DOWN = [(0, 3), (3, 3), (6, 3), (9, 3), (12, 2)]
        ITEMS += [("wd", f, n * D) for f, n in DOWN]
        GBANK = [0, 2, 6]
        DBANK = [0, 2, 1, 3]

        @block.sync
        def _(sp):
            sp.dma_start(x[:, :, :], a["x"].rearrange("(t p) d -> p t d", p=P)).then_inc(x_in.sem, 16)
            sp.dma_start(v("pos")[:, :], a["pos"]).then_inc(pos_in.sem, 16)

            def rat_weights(k):
                sp.dma_start(v("rw")[:, :], a["rw%d" % k]).then_inc(rat_in.sem, 16)
                sp.dma_start(v("rrow")[:, :, :], a["rrow%d" % k].partition_broadcast(P)).then_inc(rat_in.sem, 16)
                sp.dma_start(v("du")[:, :, :], a["du%d" % k]).then_inc(rat_in.sem, 16)

            rat_weights(0)
            sp.dma_start(v("ctx")[:, :, :], a["ctx"].rearrange("(j p) d -> p j d", p=P)).then_inc(small_in.sem, 16)
            sp.dma_start(v("mask_q")[:, :, :], a["mask"].rearrange("(t p) s -> p t s", p=P)).then_inc(small_in.sem, 16)
            sp.dma_start(v("mask_k")[:, :, :], a["maskT"].rearrange("(t p) s -> p t s", p=P)).then_inc(small_in.sem, 16)
            for m, name in enumerate(("gq", "uq")):
                for c in range(DC):
                    sp.dma_start(v(name)[:, c, :], a[name][c * P:(c + 1) * P, :]).then_inc(q_in[m].sem, 16)
            for c in range(DC):
                f0, f1 = 3 * c, min(F0, 3 * c + 3)
                sp.dma_start(v("dq")[:, f0:f1, :], a["dq"][f0 * P:f1 * P, :].rearrange("(f p) d -> p f d", p=P))\
                  .then_inc(q_in[2].sem, 16)
            for n in ("gA", "uA", "gsc"):
                sp.dma_start(v(n)[:, :, :], a[n]).then_inc(ff_in.sem, 16)
            sp.dma_start(v("dsc")[:, :], a["dsc"].partition_broadcast(P)).then_inc(ff_in.sem, 16)
            sp.wait_ge(*x_ok(0, 1))
            for n in ("gBraw", "uBraw", "dBraw"):
                sp.dma_start(v(n)[:, :], a[n]).then_inc(ff_in.sem, 16)
            sp.dma_start(v("dAraw")[:, :, :], a["dAraw"]).then_inc(ff_in.sem, 16)

            def mix_weights(k):
                sp.dma_start(v("mw")[:, :], a["mw%d" % k]).then_inc(mix_in.sem, 16)
                sp.dma_start(v("mB")[:, :], a["mB%d" % k]).then_inc(mix_in.sem, 16)

            sp.wait_ge(*x_ok(1, 1))
            mix_weights(0)
            rat_weights(1)
            sp.wait_ge(*x_ok(3, 1))
            mix_weights(1)
            sp.wait_ge(*x_ok(5, 1))
            for i, (m, at, n) in enumerate(ITEMS):
                if i >= WS:
                    sp.wait_ge(*wl_ok(0, i - WS + 1))
                dst = v("wraw%d" % (i % WS))[:, 0:n]
                if m == "wd":
                    f, c = at, n // D
                    sp.dma_start(dst.rearrange("p (f d) -> p f d", d=D),
                                 a["wd"][f * P:(f + c) * P, :].rearrange("(f p) d -> p f d", p=P))\
                      .then_inc(w_in[i % WS].sem, 16)
                else:
                    sp.dma_start(dst.rearrange("p (c i) -> p c i", c=DC),
                                 a[m][:, at * W3:(at + 1) * W3].rearrange("(c p) i -> p c i", p=P))\
                      .then_inc(w_in[i % WS].sem, 16)
            for t in range(NT):
                sp.wait_ge(*result_ok(0, t + 1))
                sp.dma_start(out[t * P:(t + 1) * P, :], x[:, t, :]).then_inc(stored.sem, 16)
            sp.wait_ge(*stored(0, 16 * NT))

        @block.tensor
        def _(pe):
            def turn_tile(src, t, ready, rk, off):
                pe.wait_ge(*ready(rk, off + t + 1))
                for c in range(DC):
                    mm = pe.transpose(ps[:, 4 + t, c * P:(c + 1) * P], src[:, t, c * P:(c + 1) * P], ident[:, :])
                mm.then_inc(tr_ok.sem, 1)

            def transposes(j, src, ready, rk, off=0):
                for t in range(NT):
                    turn_tile(src, t, ready, rk, off)

            def rat_read(k, half, nout):
                i, j = 2 * k + half, [[0, 1], [4, 5]][k][half]

                def product(t):
                    pe.wait_ge(*xnT_ok(j, t + 1))
                    for c in range(DC):
                        o = ps[:, t, 0:nout * H].rearrange("p (o h) -> p o h", o=nout)[:, :, c * SLOT:(c + 1) * SLOT]
                        mm = pe.matmul(o, xnT[:, c, t * P:(t + 1) * P], v("wd")[:, c, 0:nout, :],
                                       start=True, stop=True)
                    mm.then_inc(y_ok.sem, 1)

                ready, rk = (hid_ok, k) if half else (xn_ok, RATN[k])
                for t in range(NT):
                    turn_tile(xn, t, ready, rk, 0)
                    if t == 1:
                        pe.wait_ge(*wd_ok(i, 1))
                    if t:
                        product(t - 1)
                product(NT - 1)
                for o in range(nout):
                    for t in range(NT):
                        if o == 0:
                            pe.wait_ge(*yn_ok(i, t + 1))
                        mm = pe.transpose(ps[:, 4 + o, t * P:(t + 1) * P], v("yn%d" % k)[:, t, o, :], ident[:, :])
                    mm.then_inc(ynt_ok.sem, 1)

            def rat_attention(k):
                W0 = RP["qkv"][0]
                pe.wait_ge(*ynT_ok(k, 3))
                for t in range(NT):
                    for o in range(3):
                        mm = pe.matmul(ps[:, t, o * H:(o + 1) * H], v("ynT%d" % k)[:, o, t * P:(t + 1) * P],
                                       v("rw")[:, W0 + o * H:W0 + (o + 1) * H], start=True, stop=True)
                    mm.then_inc(qkv_ok.sem, 1)

                def turn(which, g, bank):
                    for t in range(NT):
                        src = v("qks%d" % k)[:, t, which, g * GH:(g + 1) * GH, :].rearrange("p h s -> p (h s)")
                        mm = pe.transpose(ps[:, bank, t * P:(t + 1) * P], src, ident[:, :])
                    mm.then_inc(st_ok.sem, 1)

                pe.wait_ge(*qks_ok(k, 2))
                for g in range(NG):
                    turn(1, g, 4 + g)
                for g in range(NG):
                    turn(0, g, g)
                kT, qT = v("kT%d" % k), v("qT%d" % k)
                pe.wait_ge(*sT_ok(k, 2 * NG))
                for i in range(B * NG):
                    b, g = i // NG, i % NG
                    bank = 4 * (i % 2)
                    if i >= 2:
                        pe.wait_ge(*max_ok(k, i - 1))
                    for r in range(GH):
                        pe.matmul(ps[:, bank + r, 0:3 * P], identr[:, :], v("causal")[:, :], start=True, stop=True)
                    for qt in range(QT):
                        for r in range(GH):
                            row = slice(SLOT * r, SLOT * r + 3 * HD + 1)
                            n = P * (qt + 1)
                            o = ps[:, bank + r, qt * P:qt * P + n]
                            mm = pe.matmul(o, qT[row, g, (b * QT + qt) * P:(b * QT + qt + 1) * P],
                                           kT[row, g, b * S:b * S + n], start=False, stop=True,
                                           skip_group_check=True)
                    mm.then_inc(s_ok.sem, 1)
                pe.wait_ge(*max_ok(k, B * NG))
                for g in range(NG):
                    turn(0, g, g)
                pe.wait_ge(*sT_ok(k, 3 * NG))

                def values(j):
                    i, half = j // 2, j % 2
                    b, g = i // NG, i % NG
                    pe.wait_ge(*pm_ok(k, j + 1))
                    if i >= 2 and half == 0:
                        pe.wait_ge(*oT_ok(k, i - 1))
                    for kt in range(QT):
                        for r in (2 * half, 2 * half + 1):
                            n = S - kt * P
                            pt = v("p%d%d" % (k, i % 2))[:, r, kt * S:kt * S + n]
                            mm = pe.matmul(ps[SLOT * r:SLOT * r + SLOT, 4 + i % 2, kt * P:S],
                                           v("vs%d" % k)[:, b * QT + kt, g * GH + r, :], pt,
                                           start=(kt == 0), stop=True, skip_group_check=True)
                    mm.then_inc(o_ok.sem, 1)

                def outputs(i):
                    pe.wait_ge(*oT_ok(k, i + 1))
                    if i >= 2:
                        pe.wait_ge(*yy_ok(k, i - 1))
                    for qt in range(QT):
                        mm = pe.transpose(ps[:, 6 + i % 2, qt * P:(qt + 1) * P],
                                          v("oT%d%d" % (k, i % 2))[:, qt * P:(qt + 1) * P], ident[:, :])
                    mm.then_inc(ot_ok.sem, 1)

                def scores_of_keys(j):
                    i, half = j // 2, j % 2
                    b, g = i // NG, i % NG
                    if j >= 2:
                        pe.wait_ge(*p_ok(k, j - 1))
                    for kt in range(QT):
                        for r in (2 * half, 2 * half + 1):
                            row = slice(SLOT * r, SLOT * r + 3 * HD + 1)
                            n = S - kt * P
                            mm = pe.matmul(ps[:, r, kt * S:kt * S + n],
                                           kT[row, g, b * S + kt * P:b * S + (kt + 1) * P],
                                           qT[row, g, b * S + kt * P:(b + 1) * S], start=True, stop=True)
                    mm.then_inc(sk_ok.sem, 1)

                scores_of_keys(0)
                scores_of_keys(1)
                for j in range(2 * B * NG):
                    if j + 2 < 2 * B * NG:
                        scores_of_keys(j + 2)
                    values(j)
                    if j % 2 and j >= 3:
                        outputs(j // 2 - 1)
                outputs(B * NG - 1)
                pe.wait_ge(*yy_ok(k, B * NG))
                for t in range(NT):
                    mm = pe.transpose(ps[:, 0, t * P:(t + 1) * P], v("y%d" % k)[:, t, :], ident[:, :])
                mm.then_inc(yt_ok.sem, 1)

            def rat_hidden(k):
                pe.wait_ge(*ynT_ok(k, 5))
                for m in range(MC):
                    if m >= len(GBANK):
                        pe.wait_ge(*g_ok(k, m - len(GBANK) + 1))
                    for o in range(2):
                        mm = pe.matmul(ps[:, GBANK[m % len(GBANK)] + o, :], v("ctxT")[:, o, m * P:(m + 1) * P],
                                       v("ynT%d" % k)[:, o, :], start=True, stop=True)
                    mm.then_inc(gate_ok.sem, 1)
                    if m >= 2:
                        pe.wait_ge(*g_ok(k, m - 1))
                        delta_low(k, 1, m - 2)

            def delta_low(k, half, c):
                w0 = RP["mcat" if half else "wcat"][0] + c * NW + H
                return pe.matmul(ps[0:DR, 4, :], v("rw")[:, w0:w0 + DR], v(("gT%d" if half else "yT%d") % k)[:, c, :],
                                 start=(c == 0), stop=(c == (MC - 1 if half else 0)))

            def rat_write(k, half):
                i = 2 * k + half
                n = MC if half else 1
                w0 = RP["mcat" if half else "wcat"][0]
                yt = v(("gT%d" if half else "yT%d") % k)
                if half:
                    pe.wait_ge(*g_ok(k, MC - 1))
                    delta_low(k, half, MC - 2)
                    pe.wait_ge(*g_ok(k, MC))
                else:
                    pe.wait_ge(*yT_ok(k, 1))
                delta_low(k, half, n - 1).then_inc(w2_ok.sem, 1)

                def products(t):
                    for c in range(n):
                        mm = pe.matmul(ps[:, t, 0:NW], yt[:, c, t * P:(t + 1) * P],
                                       v("rw")[:, w0 + c * NW:w0 + (c + 1) * NW], start=(c == 0), stop=(c == n - 1))
                    return mm

                products(0)
                pe.wait_ge(*dl_ok(i, 1))
                for t in range(NT):
                    mm = pe.matmul(ps[:, 5, t * P:(t + 1) * P], v("dl")[:, t * P:(t + 1) * P],
                                   v("du")[:, half, :], start=True, stop=True)
                mm.then_inc(w3_ok.sem, 1)
                for t in range(1, NT):
                    mm = products(t)
                mm.then_inc(w1_ok.sem, 1)

            def context_turned():
                pe.wait_ge(*small_in(0, 16 * 3))
                for j in range(B * KT):
                    mm = pe.transpose(ps[:, 6 + j // KT, (j % KT) * P:(j % KT + 1) * P], v("ctx")[:, j, :], ident[:, :])
                mm.then_inc(ctxt_ok.sem, 1)
                pe.wait_ge(*ctxT_ok(0, 1))

            def rat(k):
                rat_read(k, 0, 3)
                rat_attention(k)
                rat_write(k, 0)
                if k == 0:
                    context_turned()
                rat_read(k, 1, 2)
                rat_hidden(k)
                rat_write(k, 1)

            def feed0():
                transposes(2, xn, xn_ok, 1)
                pe.wait_ge(*xnT_ok(2, NT))
                pe.wait_ge(*ff_in(0, 16 * 8))
                for m, n in enumerate(("gA", "uA")):
                    for c in range(DC):
                        mm = pe.matmul(ps[0:3 * R0, 5 + 2 * m, :], v(n)[:, c, :], xnT[:, c, :], start=(c == 0),
                                       stop=(c == DC - 1))
                mm.then_inc(la_ok.sem, 1)
                pe.wait_ge(*xhl_ok(0, 1))
                for f in range(F0):
                    w = F0W[f]
                    fs = slice(f * P, f * P + w)
                    if f >= 2:
                        pe.wait_ge(*hp_ok(0, f - 1))
                    for m, n in enumerate(("gi", "ui")):
                        if f == 0:
                            pe.wait_ge(*qi_ok(0, m + 1))
                        for c in range(DC):
                            for p, part in enumerate(("xh", "xl")):
                                pe.matmul(ps[0:w, 2 * m + f % 2, :], v(n)[:, c, fs], v(part)[:, c, :],
                                          start=(c == 0 and p == 0), stop=(c == DC - 1 and p == 1))
                    if f == 0:
                        pe.wait_ge(*us_ok(0, 1))
                        pe.wait_ge(*fb_ok(0, 2))
                    for m, n in enumerate(("gB", "uB")):
                        mm = pe.matmul(ps[0:w, 4 + 2 * m + f % 2, :], v(n)[:, fs], v("us")[:, m, :],
                                       start=True, stop=True)
                    mm.then_inc(f_ok.sem, 1)
                pe.wait_ge(*qi_ok(0, 3))
                pe.wait_ge(*hp_ok(0, F0))
                for f in range(F0):
                    w = F0W[f]
                    pe.wait_ge(*hl_ok(0, f + 1))
                    for t in range(NT):
                        for p, part in enumerate(("hh", "hl")):
                            lhsT = v(part)[0:w, f, t * P:(t + 1) * P]
                            end = f == F0 - 1 and p == 1
                            pe.matmul(ps[:, t, :], lhsT, v("di")[0:w, f, :], start=(f == 0 and p == 0), stop=end)
                            mm = pe.matmul(ps[:, 4, t * P:t * P + 2 * R0], lhsT, v("dA")[0:w, f, :],
                                           start=(f == 0 and p == 0 and t == 0), stop=end,
                                           skip_group_check=True)
                mm.then_inc(d_ok.sem, 1)
                pe.wait_ge(*ud3_ok(0, 1))
                for t in range(NT):
                    mm = pe.transpose(ps[0:3 * R0, 5, t * P:(t + 1) * P],
                                      v("ud3")[:, t, :, :].rearrange("p c r -> p (c r)"), ident[:, :])
                mm.then_inc(udt_ok.sem, 1)
                pe.wait_ge(*uds_ok(0, 1))
                for t in range(NT):
                    mm = pe.matmul(ps[:, 4 + t, :], v("udh")[:, t * P:(t + 1) * P], v("dB")[:, :],
                                   start=True, stop=True)
                mm.then_inc(dlo_ok.sem, 1)

            def context():
                pe.wait_ge(*kst_ok(0, 2))
                pe.wait_ge(*x_ok(1, 1))
                for i in range(XG):
                    g, b = i // 2, i % 2
                    if i >= 2:
                        pe.wait_ge(*kx_ok(0, i - 1))
                    for kt in range(KT):
                        src = v("kst")[:, b * KT + kt, 2 * g:2 * g + 2, :].rearrange("p g s -> p (g s)")
                        mm = pe.transpose(ps[:, 4 + i % 2, kt * P:(kt + 1) * P], src, ident[:, :])
                    mm.then_inc(kt_ok.sem, 1)
                pe.wait_ge(*kx_ok(0, XG))
                pe.wait_ge(*vx_ok(0, 1))

            def cross(k):
                N = B * NPAIR
                kx, vx, qst = v("kx"), v("vx"), v("qst")

                def rows(i):
                    return slice(XSLOT * i, XSLOT * i + XK)

                def turn(n, col, done):
                    b, pr = n // NPAIR, n % NPAIR
                    for qt in range(QT):
                        src = qst[:, b * QT + qt, 2 * pr:2 * pr + 2, :].rearrange("p h s -> p (h s)")
                        mm = pe.transpose(ps[:, 7, col + qt * P:col + (qt + 1) * P], src, ident[:, :])
                    mm.then_inc(done.sem, 1)

                def turn_q(n):
                    if n >= 2:
                        pe.wait_ge(*qM_ok(k, n - 1))
                    elif n == 1:
                        pe.wait_ge(*qT_ok(k, 1))
                    turn(n, 0, qt_ok)

                def scores(n, qt):
                    b, g = n // NPAIR, n % NPAIR // 4
                    i = 4 * n + 2 * qt
                    pe.wait_ge(*qT_ok(k, n + 1))
                    for h in range(2):
                        if i >= 2:
                            pe.wait_ge(*xm_ok(k, i + h - 1))
                        pe.matmul(ps[:, 4 + h, :], v("qt%d" % (n % 2))[rows(h), qt * P:(qt + 1) * P],
                                  kx[rows(h), g, b * S2:(b + 1) * S2], start=True, stop=True)\
                          .then_inc(xs_ok.sem, 1)

                def key_masks(n):
                    if n >= 1:
                        pe.wait_ge(*px_ok(k, 2 * n))
                    else:
                        pe.wait_ge(*mk_ok(k, 1))
                    for h in range(2):
                        for m, part in enumerate(("mkh", "mkl")):
                            pe.matmul(ps[:, 2 + h, :], identr[:, :],
                                      v(part)[:, :, :].rearrange("p k q -> p (k q)"), start=(m == 0), stop=False,
                                      skip_group_check=True)

                def keys(n, u):
                    b, g = n // NPAIR, n % NPAIR // 4
                    if n >= 1 and u == 0:
                        pe.wait_ge(*ms_ok(k, n))
                    for kk in range(2):
                        c = b * S2 + (2 * u + kk) * P
                        for h in range(2):
                            mm = pe.matmul(ps[:, 2 * u + h, kk * S:(kk + 1) * S], kx[rows(h), g, c:c + P],
                                           v("qm%d" % (n % 2))[rows(h), :], start=(u == 0), stop=True,
                                           skip_group_check=True)
                    mm.then_inc(xk_ok.sem, 1)

                def values(n, u):
                    b, gp = n // NPAIR, n % NPAIR // XR
                    i = 2 * n + u
                    if n % 2 == 0 and u == 0 and n:
                        pe.wait_ge(*ox_ok(k, n // 2))
                    pe.wait_ge(*px_ok(k, i + 1))
                    for kk in range(2):
                        for h in range(2):
                            s0 = SLOT * (2 * h + n % 2)
                            mm = pe.matmul(ps[s0:s0 + SLOT, 6, 0:S], vx[:, b * KT + 2 * u + kk, 2 * gp + h, :],
                                           v("px%d" % (i % 4))[:, h, kk, :], start=(u + kk == 0),
                                           stop=(u + kk == 2), skip_group_check=True)
                    mm.then_inc(pv_ok.sem, 1)

                def outputs(g):
                    pe.wait_ge(*ox_ok(k, 2 * g + 2))
                    for dd in range(2):
                        for qt in range(QT):
                            c = (dd * QT + qt) * P
                            mm = pe.transpose(ps[:, 4, c:c + P], v("ox%d" % (g % 2))[:, dd, qt * P:(qt + 1) * P],
                                              ident[:, :])
                    mm.then_inc(ot2_ok.sem, 1)

                pe.wait_ge(*qst_ok(k, 3))
                turn_q(0)
                scores(0, 0)
                scores(0, 1)
                turn_q(1)
                scores(1, 0)
                for n in range(N):
                    pe.wait_ge(*ml_ok(k, n + 1))
                    if n + 2 <= N:
                        pe.wait_ge(*qT_ok(k, n + 2))
                    turn(n, 2 * P, qm_ok)
                    if n >= 1:
                        values(n - 1, 0)
                    if n + 1 < N:
                        scores(n + 1, 1)
                    pe.wait_ge(*qM_ok(k, n + 1))
                    keys(n, 0)
                    if n + 2 < N:
                        turn_q(n + 2)
                    key_masks(n)
                    keys(n, 1)
                    if n >= XR and n % XR == 1:
                        pe.wait_ge(*xm_ok(k, 4 * min(n + 2, N)))
                        outputs(n // XR - 1)
                        values(n - 1, 1)
                        pe.wait_ge(*on_ok(k, n // XR))
                        scores(n + 2, 0)
                    else:
                        if n + 2 < N:
                            scores(n + 2, 0)
                        if n >= 1:
                            values(n - 1, 1)
                values(N - 1, 0)
                values(N - 1, 1)
                outputs(N // XR - 1)

            def mixture(k):
                mw = v("mw")
                ag = mw[:, MP["ag"][0]:MP["ag"][1]].rearrange("p (c n) -> p c n", c=DC)
                base = mw[:, 0:DC * D].rearrange("p (c n) -> p c n", c=DC)
                j = [3, 6][k]
                transposes(j, xn, xn_ok, [3, 5][k])
                pe.wait_ge(*mix_in(k, 32))
                pe.wait_ge(*xnT_ok(j, NT))
                for t in range(NT):
                    for c in range(DC):
                        at = t % 2 * 2 * P
                        mm = pe.matmul(ps[:, 4 + t // 2, at:at + ER + E], xnT[:, c, t * P:(t + 1) * P], ag[:, c, :],
                                       start=(c == 0), stop=(c == DC - 1))
                mm.then_inc(hl_ps.sem, 1)
                for t in range(NT):
                    for c in range(DC):
                        pe.matmul(ps[:, t, :], xnT[:, c, t * P:(t + 1) * P], base[:, c, :], start=(c == 0), stop=False)
                pe.wait_ge(*hw_ok(k, 1))
                for t in range(NT):
                    mm = pe.transpose(ps[:, 6, t * P:(t + 1) * P], v("hs")[:, t, :], ident[:, :])
                mm.then_inc(ht_ok.sem, 1)
                pe.wait_ge(*hT_ok(k, 1))
                for t in range(NT):
                    pe.matmul(ps[:, t, :], v("hsT")[:, t * P:(t + 1) * P], v("mB")[:, :], start=False, stop=True)\
                      .then_inc(base_ok.sem, 1)

            def feed3():
                xqT, iqT = v("xqT"), v("iqT")
                transposes(7, xn, xq_ok, 0)
                pe.wait_ge(*xnT_ok(7, NT))

                def parts(i):
                    pe.wait_ge(*wl_ok(0, i + 1))
                    return [v("whi%d" % (i % WS)), v("wlo%d" % (i % WS))]

                for blk in range(NB3):
                    for t in range(NT):
                        i = blk * NT + t
                        if i >= 2:
                            pe.wait_ge(*in_ok(0, i - 1))
                        for m in range(2):
                            hi_lo = parts(2 * blk + m)
                            for c in range(DC):
                                for p, w in enumerate(hi_lo):
                                    mm = pe.matmul(ps[:, 2 * m + i % 2, 0:W3], xqT[:, c, t * P:(t + 1) * P],
                                                   w[:, c * W3:(c + 1) * W3], start=(c == 0 and p == 0),
                                                   stop=(c == DC - 1 and p == 1))
                        mm.then_inc(gu_ok.sem, 1)

                def turn_hidden(t):
                    pe.wait_ge(*iq_ok(0, t + 1))
                    for q in range(4):
                        i = 4 * t + q
                        if i >= 4:
                            pe.wait_ge(*iT_ok(0, i - 3))
                        fs = range(4 * q, min(F3, 4 * q + 4))
                        for f in fs:
                            mm = pe.transpose(ps[:, 4 + q, (f % 4) * P:(f % 4 + 1) * P],
                                              v("inter")[:, t, f * P:(f + 1) * P], ident[:, :])
                        mm.then_inc(it_ok.sem, 1)

                def down(t, n):
                    f0, cnt = DOWN[n]
                    hi_lo = parts(2 * NB3 + n)
                    for f in range(cnt):
                        for p, w in enumerate(hi_lo):
                            mm = pe.matmul(ps[:, DBANK[t], :], iqT[:, f0 + f, t * P:(t + 1) * P],
                                           w[:, f * D:(f + 1) * D], start=(f0 + f == 0 and p == 0),
                                           stop=(f0 + f == F3 - 1 and p == 1))
                    mm.then_inc(dn_ok.sem, 1)

                turn_hidden(0)
                for t in range(NT):
                    if t + 1 < NT:
                        turn_hidden(t + 1)
                    pe.wait_ge(*iT_ok(0, 4 * t + 4))
                    pe.wait_ge(*in_ok(0, NB3 * NT - 1 + t // 2))
                    for n in range(WS):
                        down(t, n)
                for t in range(NT):
                    down(t, WS)

            pe.wait_ge(*ident_ok(0, 1))
            pe.wait_ge(*constr(0, 2))
            pe.wait_ge(*const_ok(0, 1))
            rat(0)
            feed0()
            context()
            cross(0)
            mixture(0)
            rat(1)
            mixture(1)
            cross(1)
            feed3()

        def query_heads(m, h):
            return m[:, :, :].rearrange("p t (g h r d) -> p (t g) h r d", h=2, r=4, d=XD)[:, :, h, :, :]

        def query_slots(m, h):
            return m[:, :, :, :].rearrange("p t (g r h) s -> p (t g) r h s", r=4, h=2)[:, :, :, h, :]

        @block.scalar
        def _(act):
            def act_copy(dst, src, scale=1.0, bias=0.0):
                return act.activation(dst, src, ACT.Copy, bias=bias, scale=scale)

            def prepare_exp():
                link(act, "act", act.activation(v("tiny")[:, 1:2], v("tiny")[:, 0:1], ACT.Exp))

            def turned(j):
                for t in range(NT):
                    act.wait_ge(*tr_ok(j, t + 1))
                    act_copy(xnT[:, :, t * P:(t + 1) * P],
                             ps[:, 4 + t, :].rearrange("p (c q) -> p c q", c=DC)).then_inc(xnT_ok.sem, 1)

            def rat_read(k, half, nout):
                turned([[0, 1], [4, 5]][k][half])
                if k == 0 and half == 0:
                    act.wait_ge(*ang_ok(0, 1))
                    act.activation(v("sin")[:, :, :], v("ang")[:, :, :], ACT.Sin)
                    act.activation(v("cos")[:, :, :], v("turn")[:, :, :], ACT.Sin).then_inc(rope_ok.sem, 1)
                g0, b0 = RP["mg" if half else "rg"][0], RP["mb" if half else "rb"][0]
                for o in range(nout):
                    act.wait_ge(*ynt_ok(k, 3 * half + o + 1))
                    act.activation(v("ynT%d" % k)[:, o, :], ps[:, 4 + o, :], ACT.Identity,
                                   bias=v("rw")[:, b0 + o:b0 + o + 1], scale=v("rw")[:, g0 + o:g0 + o + 1])\
                       .then_inc(ynT_ok.sem, 1)

            def rat_attention(k):
                qk, qks, qkh = v("qk%d" % k), v("qks%d" % k), v("qkh%d" % k)
                act.wait_ge(*pads(k, 1))
                for t in range(NT):
                    act.wait_ge(*qkv_ok(k, t + 1))
                    act_copy(qk[:, t, :, :], ps[:, t, 0:2 * H].rearrange("p (w h) -> p w h", w=2))\
                        .then_inc(qk_sb.sem, 1)
                    act_copy(v("vs%d" % k)[:, t, :, 0:HD],
                             ps[:, t, 2 * H:3 * H].rearrange("p (h d) -> p h d", d=HD)).then_inc(qk_sb.sem, 1)
                act.wait_ge(*qkh_ok(k, 1))
                hi = [qkh[:, :, w, :].rearrange("p t (h d) -> p t h d", d=HD) for w in range(2)]
                for w, c in ((0, 0), (0, HD), (1, 0)):
                    act_copy(qks[:, :, w, :, c:c + HD], hi[w])
                act_copy(qks[:, :, 1, :, 2 * HD:3 * HD], hi[1]).then_inc(qks_ok.sem, 1)

                def turn(n, dst, g, bank):
                    act.wait_ge(*st_ok(k, n + 1))
                    act_copy(dst[:, g, :], ps[:, bank, :]).then_inc(sT_ok.sem, 1)

                for g in range(NG):
                    turn(g, v("kT%d" % k), g, 4 + g)
                for g in range(NG):
                    turn(NG + g, v("qT%d" % k), g, g)
                for g in range(NG):
                    turn(2 * NG + g, v("qT%d" % k), g, g)

                def output(i):
                    act.wait_ge(*o_ok(k, 2 * i + 2))
                    if i >= 2:
                        act.wait_ge(*ot_ok(k, i - 1))
                    act_copy(v("oT%d%d" % (k, i % 2))[:, :], ps[:, 4 + i % 2, 0:S]).then_inc(oT_ok.sem, 1)

                for j in range(2 * B * NG):
                    i, heads = j // 2, slice(2 * (j % 2), 2 * (j % 2) + 2)
                    act.wait_ge(*sk_ok(k, j + 1))
                    if j >= 4:
                        act.wait_ge(*o_ok(k, j - 3))
                    act.activation(v("p%d%d" % (k, i % 2))[:, heads, :], ps[:, heads, 0:3 * P], ACT.Exp,
                                   scale=float(1.0 / np.sqrt(np.float32(HD)))).then_inc(p_ok.sem, 1)
                    if j % 2 and i >= 1:
                        output(i - 1)
                output(B * NG - 1)
                act.wait_ge(*yt_ok(k, 1))
                act_copy(v("yT%d" % k)[:, 0, :], ps[:, 0, :]).then_inc(yT_ok.sem, 1)

            def rat_hidden(k):
                for m in range(MC):
                    act.wait_ge(*gate_ok(k, m + 1))
                    if m >= 2:
                        act.wait_ge(*g_ok(k, m - 1))
                    act.activation(v("silu%d%d" % (k, m % 2))[:, :], ps[:, GBANK[m % len(GBANK)], :], ACT.Silu)\
                       .then_inc(silu_ok.sem, 1)

            def rat_write(k, half):
                i = 2 * k + half
                az = v("az%d" % k)
                prepare_exp()
                act.wait_ge(*w3_ok(i, 1))
                act.activation(az[:, :, AS:AS + H], ps[:, 5, :].rearrange("p (t h) -> p t h", t=NT), ACT.Abs)
                act.wait_ge(*ab_ok(i, 1))
                link(act, "act", act.activation(az[:, :, 0:AS], v("ab%d" % k)[:, :, 0:AS], ACT.Abs))
                act.activation(az[:, :, :], az[:, :, :], ACT.Exp, scale=-1.0).then_inc(e_ok.sem, 1)
                act.wait_ge(*e_ok(i, 1))
                act.activation(v("ln%d" % k)[:, :, :], az[:, :, :], ACT.Ln, bias=1.0).then_inc(ln_ok.sem, 1)
                act_copy(v("os%d" % k)[:, :, :], ps[:, 0:NT, 0:H]).then_inc(os_ok.sem, 1)
                for t in range(NT):
                    act.wait_ge(*u_ok(i, t + 1))
                    u = v("u%d" % k)[:, t, :, :]
                    act.activation(u, u, ACT.Exp, scale=-1.0).then_inc(abar_ok.sem, 1)

            def rat(k):
                rat_read(k, 0, 3)
                rat_attention(k)
                rat_write(k, 0)
                if k == 0:
                    act.wait_ge(*ctxt_ok(0, 1))
                    act_copy(v("ctxT")[:, :, :], ps[:, 6:6 + B, :]).then_inc(ctxT_ok.sem, 1)
                rat_read(k, 1, 2)
                rat_hidden(k)
                rat_write(k, 1)

            def feed0():
                turned(2)
                act.wait_ge(*ff_in(0, 16 * 8))
                act_copy(v("dA")[:, :, 0:R0], v("dAraw")[:, :, :])
                for n in ("gB", "uB", "dB"):
                    ins = act_copy(v(n)[:, :], v(n + "raw")[:, :])
                ins.then_inc(fh_ok.sem, 1)
                act.wait_ge(*la_ok(0, 1))
                act_copy(v("ug")[:, :, :], ps[0:3 * R0, 5:8:2, :], scale=LRS).then_inc(ug_ok.sem, 1)

                def high(f):
                    act.wait_ge(*hp_ok(0, f + 1))
                    act_copy(v("hh")[0:F0W[f], f, :], v("gp")[0:F0W[f], f % 2, :]).then_inc(hh_ok.sem, 1)

                act.wait_ge(*fb_ok(0, 2))
                for f in range(F0):
                    w = F0W[f]
                    act.wait_ge(*f_ok(0, f + 1))
                    if f >= 2:
                        act.wait_ge(*hp_ok(0, f - 1))
                    act_copy(v("lg")[0:w, f % 2, :], ps[0:w, 4 + f % 2, :])
                    act_copy(v("lu")[0:w, f % 2, :], ps[0:w, 6 + f % 2, :]).then_inc(lc_ok.sem, 1)
                    if f >= 1:
                        high(f - 1)
                    act.wait_ge(*gp_ok(0, f + 1))
                    act.activation(v("gp")[0:w, f % 2, :], v("gp")[0:w, f % 2, :], ACT.Silu).then_inc(sg_ok.sem, 1)
                high(F0 - 1)
                act.wait_ge(*d_ok(0, 1))
                act_copy(v("ud2")[:, :, :], ps[:, 4, :].rearrange("p (t r) -> p t r", t=NT)[:, :, 0:2 * R0])\
                    .then_inc(ud_ok.sem, 1)
                act.wait_ge(*udt_ok(0, 1))
                act_copy(v("udf")[:, :], ps[0:3 * R0, 5, :], scale=LRS).then_inc(udf_ok.sem, 1)

            def context():
                act.wait_ge(*chi_ok(0, 1))
                hi = v("ch")[:, :, :].rearrange("p j (g d) -> p j g d", d=XD)
                act_copy(v("kst")[:, :, :, 0:XD], hi)
                act_copy(v("kst")[:, :, :, 2 * XD:3 * XD], hi).then_inc(kst_ok.sem, 1)
                act.wait_ge(*x_ok(1, 1))
                for i in range(XG):
                    act.wait_ge(*kt_ok(0, i + 1))
                    act_copy(v("kx")[:, i // 2, (i % 2) * S2:(i % 2 + 1) * S2], ps[:, 4 + i % 2, :])\
                        .then_inc(kx_ok.sem, 1)

            def cross(k):
                N = B * NPAIR
                prepare_exp()
                act.wait_ge(*qh_ok(k, 1))
                for h in range(2):
                    for c in (0, XD):
                        ins = act_copy(query_slots(v("qst"), h)[:, :, :, c:c + XD], query_heads(v("qh"), h))
                ins.then_inc(qst_ok.sem, 1)

                def turn_q(n):
                    act.wait_ge(*qt_ok(k, n + 1))
                    if n >= 2:
                        act.wait_ge(*xs_ok(k, 4 * n - 4))
                    act_copy(v("qt%d" % (n % 2))[:, :], ps[:, 7, 0:S]).then_inc(qT_ok.sem, 1)

                def exps(n, u):
                    i = 2 * n + u
                    px = v("px%d" % (i % 4))[:, :, :, :]
                    if u == 0:
                        act.wait_ge(*ms_ok(k, n + 1))
                        act.activation(px, px, ACT.Exp).then_inc(px_ok.sem, 1)
                        return
                    act.wait_ge(*xk_ok(k, i + 1))
                    if i >= 4:
                        act.wait_ge(*pv_ok(k, i - 3))
                    act.activation(px.rearrange("p h k q -> p h (k q)"), ps[:, 2:4, :], ACT.Exp)\
                       .then_inc(px_ok.sem, 1)

                def output(m):
                    act.wait_ge(*pv_ok(k, 4 * m + 4))
                    if m >= 4 and m % 2 == 0:
                        act.wait_ge(*ot2_ok(k, m // 2 - 1))
                    act_copy(v("ox%d" % (m // 2 % 2))[:, m % 2, :], ps[:, 6, 0:S]).then_inc(ox_ok.sem, 1)

                turn_q(0)
                turn_q(1)
                for n in range(N):
                    if n >= 1:
                        exps(n - 1, 1)
                    act.wait_ge(*qm_ok(k, n + 1))
                    if n >= 2:
                        act.wait_ge(*xk_ok(k, 2 * n - 2))
                    act_copy(v("qm%d" % (n % 2))[:, :], ps[:, 7, 2 * P:4 * P]).then_inc(qM_ok.sem, 1)
                    if n + 2 < N:
                        turn_q(n + 2)
                    exps(n, 0)
                    if n >= 2 and n % 2 == 0:
                        output(n // 2 - 1)
                exps(N - 1, 1)
                output(N // 2 - 1)

            def mixture(k):
                turned([3, 6][k])
                act.wait_ge(*le_ok(k, 1))
                act.activation(v("route")[:, 1, :, :], v("route")[:, 0, :, :], ACT.Exp).then_inc(ee_ok.sem, 1)
                act.wait_ge(*ht_ok(k, 1))
                act_copy(v("hsT")[:, :], ps[:, 6, :]).then_inc(hT_ok.sem, 1)

            def feed3():
                def split(i):
                    n = ITEMS[i][2]
                    act.wait_ge(*w_in[i % WS](i // WS, 16))
                    if WS <= i < 2 * NB3 + WS:
                        act.wait_ge(*gu_ok(0, NT * ((i - WS) // 2 + 1)))
                    elif i >= 2 * NB3 + WS:
                        act.wait_ge(*dn_ok(0, (NT - 1) * WS + i - WS - 2 * NB3 + 1))
                    act_copy(v("whi%d" % (i % WS))[:, 0:n], v("wraw%d" % (i % WS))[:, 0:n]).then_inc(wc_ok.sem, 1)

                act.wait_ge(*x_ok(6, 1))
                split(0)
                split(1)
                for t in range(NT):
                    act.wait_ge(*tr_ok(7, t + 1))
                    act_copy(v("xqT")[:, :, t * P:(t + 1) * P],
                             ps[:, 4 + t, :].rearrange("p (c q) -> p c q", c=DC), bias=-MAGIC)\
                        .then_inc(xnT_ok.sem, 1)

                for blk in range(NB3):
                    for t in range(NT):
                        i = blk * NT + t
                        act.wait_ge(*gu_ok(0, i + 1))
                        if i >= 2:
                            act.wait_ge(*in_ok(0, i - 1))
                        act.activation(v("sil%d" % (i % 2))[:, :], ps[:, i % 2, 0:W3], ACT.Silu,
                                       scale=v("sc3")[:, 0, t:t + 1]).then_inc(si_ok.sem, 1)
                        if t < 2:
                            split(2 * (blk + 1) + t)
                split(10)
                split(11)
                for t in range(NT):
                    for q in range(4):
                        n = min(4, F3 - 4 * q)
                        act.wait_ge(*it_ok(0, 4 * t + q + 1))
                        act_copy(v("iqT")[:, 4 * q:4 * q + n, t * P:(t + 1) * P],
                                 ps[:, 4 + q, 0:n * P].rearrange("p (f q) -> p f q", f=n), bias=-MAGIC)\
                            .then_inc(iT_ok.sem, 1)
                split(12)

            rat(0)
            feed0()
            context()
            cross(0)
            mixture(0)
            rat(1)
            mixture(1)
            cross(1)
            feed3()

        @block.vector
        def _(dve):
            def step(ins):
                link(dve, "dve", ins)

            def norm(n):
                if n:
                    dve.wait_ge(*x_ok(n - 1, 1))
                else:
                    dve.wait_ge(*x_in(0, 16))

                def normalised(t):
                    dve.wait_ge(*rstd_ok(n, t + 1))
                    dve.tensor_scalar(xn[:, t, :], x[:, t, :], mv[:, t, 0:1], rstd[:, t:t + 1],
                                      ALU.subtract, ALU.mult).then_inc(xn_ok.sem, 1)

                for t in range(NT):
                    step(dve.bn_stats(stats[:, t, :], x[:, t, :]))
                    dve.bn_aggr(mv[:, t, :], stats[:, t, :]).then_inc(mv_ok.sem, 1)
                    if t:
                        normalised(t - 1)
                normalised(NT - 1)

            def angles():
                dve.wait_ge(*pos_in(0, 16))
                ang, turn, cos = v("ang"), v("turn"), v("cos")
                for d in range(HD // 2):
                    inv = float(np.float32(1.0) / np.float32(10000.0) ** np.float32(d / (HD // 2)))
                    ins = dve.tensor_scalar(ang[:, :, d], v("pos")[:, :], inv, None, ALU.mult)
                step(ins)
                step(dve.tensor_scalar(turn[:, :, :], ang[:, :, :], 1.0 / (2.0 * np.pi), MAGIC, ALU.mult, ALU.add))
                step(dve.tensor_scalar(turn[:, :, :], turn[:, :, :], MAGIC, None, ALU.subtract))
                c1 = 6.28125
                c2 = float(np.round((2.0 * np.pi - c1) * 2 ** 20) / 2 ** 20)
                for c in (c1, c2, 2.0 * np.pi - c1 - c2):
                    step(dve.scalar_tensor_tensor(ang[:, :, :], turn[:, :, :], -c, ang[:, :, :], ALU.mult, ALU.add))
                step(dve.tensor_scalar(ang[:, :, :], ang[:, :, :], 3.1415925, -3.1415925, ALU.min, ALU.max))
                step(dve.scalar_tensor_tensor(turn[:, :, :], ang[:, :, :], -1.0, ang[:, :, :], ALU.mult, ALU.max))
                dve.tensor_scalar(turn[:, :, :], turn[:, :, :], -1.0, float(np.pi / 2), ALU.mult, ALU.add)\
                   .then_inc(ang_ok.sem, 1)

            def rat_read(k, half, nout):
                i = 2 * k + half
                c0, c1 = RP["mw" if half else "rw"]
                dve.wait_ge(*rat_in(k, 48))
                col = v("rw")[:, c0:c1].rearrange("p (c o) -> p c o", o=nout)
                for c in range(DC):
                    ins = dve.tensor_tensor(v("wd")[:, c, 0:nout, :],
                                            v("sel")[:, :].unsqueeze(1).broadcast_to([P, nout, SLOT]),
                                            col[:, c, :].unsqueeze(2).broadcast_to([P, nout, SLOT]), ALU.mult)
                ins.then_inc(wd_ok.sem, 1)
                if k == 0 and half == 0:
                    angles()

                def normalised(t):
                    dve.wait_ge(*yrstd_ok(i, t + 1))
                    for o in range(nout):
                        n = t * nout + o
                        ins = dve.tensor_scalar(v("yn%d" % k)[:, t, o, :], ps[:, t, o * H:(o + 1) * H],
                                                mv[:, n, 0:1], rstd[:, n:n + 1], ALU.subtract, ALU.mult)
                    ins.then_inc(yn_ok.sem, 1)

                for t in range(NT):
                    dve.wait_ge(*y_ok(i, t + 1))
                    for o in range(nout):
                        ins = dve.bn_stats(stats[:, t * nout + o, :], ps[:, t, o * H:(o + 1) * H])
                    step(ins)
                    for o in range(nout):
                        ins = dve.bn_aggr(mv[:, t * nout + o, :], stats[:, t * nout + o, :])
                    ins.then_inc(ymv_ok.sem, 1)
                    if t:
                        normalised(t - 1)
                normalised(NT - 1)

            def rat_attention(k):
                dve.wait_ge(*qk_sb(k, 2 * NT))
                dve.wait_ge(*rope_ok(0, 1))
                h2 = HD // 2
                view = [v("%s%d" % (n, k))[:, :, :, :].rearrange("p t w (h d) -> p t (w h) d", d=HD)
                        for n in ("qk", "qkr")]
                tmp = v("p%d0" % k)[:, :, :].rearrange("p h s -> p (h s)")[:, 0:NT * 2 * NH * h2]\
                    .rearrange("p (t h d) -> p t h d", t=NT, d=h2)
                cos, sin = [v(n)[:, :, :].unsqueeze(2).broadcast_to([P, NT, 2 * NH, h2]) for n in ("cos", "sin")]
                lo, hi = [w[:, :, :, 0:h2] for w in view], [w[:, :, :, h2:HD] for w in view]
                dve.tensor_tensor(lo[1], lo[0], cos, ALU.mult)
                dve.tensor_tensor(hi[1], hi[0], cos, ALU.mult)
                step(dve.tensor_tensor(tmp, hi[0], sin, ALU.mult))
                step(dve.tensor_tensor(lo[1], lo[1], tmp, ALU.subtract))
                step(dve.tensor_tensor(tmp, lo[0], sin, ALU.mult))
                step(dve.tensor_tensor(hi[1], hi[1], tmp, ALU.add))
                qkr, qkh, qks = v("qkr%d" % k), v("qkh%d" % k), v("qks%d" % k)
                dve.tensor_copy(qkh[:, :, :, :], qkr[:, :, :, :]).then_inc(qkh_ok.sem, 1)
                dve.wait_ge(*qkh_ok(k, 1))
                dve.wait_ge(*pads(k, 1))
                for w, c in ((0, 2 * HD), (1, HD)):
                    a3, b3 = [m[:, :, w, :].rearrange("p t (h d) -> p t h d", d=HD)
                              for m in (qkr, qkh[:, :, :, :].bitcast(F32))]
                    ins = dve.tensor_tensor(qks[:, :, w, :, c:c + HD], a3, b3, ALU.subtract)
                ins.then_inc(qks_ok.sem, 1)
                for i in range(B * NG):
                    b, g = i // NG, i % NG
                    bank = 4 * (i % 2)
                    dve.wait_ge(*s_ok(k, i + 1))
                    for qt in range(QT):
                        m = qks[:, b * QT + qt, 0, g * GH:(g + 1) * GH, 3 * HD:3 * HD + 1]
                        ins = dve.tensor_reduce(m, ps[:, bank:bank + GH, qt * P:P + 2 * qt * P], AX.X, ALU.max)
                    ins.then_inc(max_ok.sem, 1)
                for i in range(B * NG):
                    b, g = i // NG, i % NG
                    rc = v("route")[:, i % 2, 0:QT, 0:GH]
                    dve.wait_ge(*ot_ok(k, i + 1))
                    o = ps[:, 6 + i % 2, 0:S].rearrange("p (q h s) -> p q h s", q=QT, s=SLOT)
                    step(dve.reciprocal(rc, o[:, :, :, HD]))
                    y = v("y%d" % k)[:, b * QT:(b + 1) * QT, g * SLOT:(g + 1) * SLOT]\
                        .rearrange("p q (h d) -> p q h d", d=HD)
                    dve.tensor_tensor(y, o[:, :, :, 0:HD], rc.unsqueeze(3).broadcast_to([P, QT, GH, HD]), ALU.mult)\
                       .then_inc(yy_ok.sem, 1)

            def rat_hidden(k):
                for m in range(MC):
                    dve.wait_ge(*silu_ok(k, m + 1))
                    dve.tensor_tensor(v("gT%d" % k)[:, m, :], v("silu%d%d" % (k, m % 2))[:, :],
                                      ps[:, GBANK[m % len(GBANK)] + 1, :], ALU.mult).then_inc(g_ok.sem, 1)

            def rat_write(k, half):
                i = 2 * k + half
                ab, sp, gg, az, tt = [v(n % k) for n in ("ab%d", "sp%d", "gg%d", "az%d", "t%d")]
                dve.wait_ge(*w2_ok(i, 1))
                dve.tensor_copy(v("dl")[0:DR, :], ps[0:DR, 4, :]).then_inc(dl_ok.sem, 1)
                dve.wait_ge(*w1_ok(i, 1))
                dve.tensor_tensor(ab[:, :, :], ps[:, 0:NT, H + DR:NW],
                                  v("rrow")[:, half:half + 1, :].broadcast_to([P, NT, NAB]), ALU.add)\
                   .then_inc(ab_ok.sem, 1)
                dve.wait_ge(*ab_ok(i, 1))
                dve.wait_ge(*e_ok(i, 1))
                step(dve.tensor_scalar(sp[:, :, :], az[:, :, :], 1.0, None, ALU.add))
                step(dve.scalar_tensor_tensor(sp[:, :, :], sp[:, :, :], -1.0, az[:, :, :], ALU.add, ALU.subtract))
                dve.scalar_tensor_tensor(sp[:, :, 0:AS], ab[:, :, 0:AS], 0.0, sp[:, :, 0:AS], ALU.max, ALU.subtract)
                step(dve.scalar_tensor_tensor(sp[:, :, AS:AS + H], ps[:, 5, :].rearrange("p (t h) -> p t h", t=NT), 0.0,
                                              sp[:, :, AS:AS + H], ALU.max, ALU.subtract))
                dve.wait_ge(*ln_ok(i, 1))
                dve.tensor_tensor(sp[:, :, :], v("ln%d" % k)[:, :, :], sp[:, :, :], ALU.add).then_inc(sp_ok.sem, 1)
                dve.wait_ge(*sp_ok(i, 1))
                step(dve.tensor_scalar(gg[:, :, :], sp[:, :, 0:AS], -1.0, -EPS, ALU.mult, ALU.add))
                step(dve.reciprocal(gg[:, :, :], gg[:, :, :]))
                step(dve.tensor_tensor(gg[:, :, :], gg[:, :, :], ab[:, :, AS:2 * AS], ALU.mult))
                dve.wait_ge(*os_ok(i, 1))
                for n in range(2, NT + 1, 2):
                    ts = slice(n - 2, n)
                    dve.wait_ge(*abar_ok(i, n))
                    u, t2 = v("u%d" % k)[:, ts, :, :], tt[:, ts, :, :]
                    o3 = v("os%d" % k)[:, ts, :].unsqueeze(3).broadcast_to([P, 2, H, C3])
                    h3 = xn[:, ts, :].rearrange("p t (h c) -> p t h c", c=C)[:, :, :, 0:C3]
                    for t in (n - 2, n - 1):
                        u3, t3 = [m[:, t, :, :].rearrange("p (s r) c -> p s (r c)", s=HS)
                                  for m in (v("u%d" % k), tt)]
                        dve.scalar_tensor_tensor(t3, u3, -1.0, gg[:, t:t + 1, :].broadcast_to([P, HS, AS]),
                                                 ALU.add, ALU.mult)
                    step(dve.tensor_tensor(h3, h3, u, ALU.mult))
                    step(dve.tensor_tensor(t2, t2, o3, ALU.mult))
                    dve.wait_ge(*ah_ok(i, n))
                    dve.tensor_tensor(h3, h3, t2, ALU.add).then_inc(hid_ok.sem, 2)
                if half:
                    dve.wait_ge(*hid_ok(k, 2 * NT))
                    dve.wait_ge(*xa_ok(k, NT // 2))
                    ts = slice(NT // 2, NT)
                    dve.tensor_tensor(x[:, ts, :], x[:, ts, :], xn[:, ts, :], ALU.add).then_inc(x_ok.sem, 1)

            def rat(k):
                norm(RATN[k])
                rat_read(k, 0, 3)
                rat_attention(k)
                rat_write(k, 0)
                rat_read(k, 1, 2)
                rat_hidden(k)
                rat_write(k, 1)

            def feed0():
                norm(1)
                dve.wait_ge(*xnT_ok(2, NT))
                step(dve.tensor_copy(v("xh")[:, :, :], xnT[:, :, :]))
                dve.tensor_tensor(v("xl")[:, :, :], xnT[:, :, :], v("xh")[:, :, :].bitcast(F32), ALU.subtract)\
                   .then_inc(xhl_ok.sem, 1)
                dve.wait_ge(*fh_ok(0, 1))
                last = slice(2 * R0, 3 * R0)
                for n in ("gB", "uB"):
                    ins = dve.tensor_tensor(v(n)[last, :], v(n + "raw")[last, :], v(n)[last, :].bitcast(F32),
                                            ALU.subtract)
                ins.then_inc(fb_ok.sem, 1)
                dve.wait_ge(*ug_ok(0, 1))
                us, ug = v("us"), v("ug")
                mid = slice(R0, 2 * R0)
                step(dve.tensor_copy(us[:, :, :], ug[:, :, :]))
                dve.tensor_tensor(us[mid, :, :], ug[mid, :, :], us[mid, :, :].bitcast(F32), ALU.subtract)\
                   .then_inc(us_ok.sem, 1)
                for f in range(F0):
                    w = F0W[f]
                    gp, up = v("gp")[0:w, f % 2, :], v("up")[0:w, :]
                    dve.wait_ge(*lc_ok(0, f + 1))
                    if f >= 2:
                        dve.wait_ge(*hl_ok(0, f - 1))
                    dve.scalar_tensor_tensor(gp, ps[0:w, f % 2, :], v("gsc")[0:w, 0, f:f + 1],
                                             v("lg")[0:w, f % 2, :], ALU.mult, ALU.add).then_inc(gp_ok.sem, 1)
                    if f >= 1:
                        dve.wait_ge(*hp_ok(0, f))
                    step(dve.scalar_tensor_tensor(up, ps[0:w, 2 + f % 2, :], v("gsc")[0:w, 1, f:f + 1],
                                                  v("lu")[0:w, f % 2, :], ALU.mult, ALU.add))
                    dve.wait_ge(*sg_ok(0, f + 1))
                    dve.tensor_tensor(gp, gp, up, ALU.mult).then_inc(hp_ok.sem, 1)
                dve.wait_ge(*ud_ok(0, 1))
                ud2 = v("ud2")
                lo, hi = [ud2[:, :, n * R0:(n + 1) * R0].unsqueeze(2).broadcast_to([P, NT, 3, R0]) for n in range(2)]
                dve.tensor_tensor(v("ud3")[:, :, :, :], lo, hi, ALU.add).then_inc(ud3_ok.sem, 1)
                dsum = v("dsum")
                for t in range(NT):
                    dve.tensor_tensor(dsum[:, t, :], ps[:, t, :], v("dsc")[:, :], ALU.mult)
                dve.wait_ge(*udf_ok(0, 1))
                step(dve.tensor_copy(v("udh")[:, :], v("udf")[:, :]))
                dve.tensor_tensor(v("udh")[mid, :], v("udf")[mid, :], v("udh")[mid, :].bitcast(F32), ALU.subtract)\
                   .then_inc(uds_ok.sem, 1)
                for t in range(NT):
                    ins = dve.tensor_tensor(x[:, t, :], x[:, t, :], dsum[:, t, :], ALU.add)
                step(ins)
                dve.wait_ge(*dlo_ok(0, 1))
                for t in range(NT):
                    ins = dve.tensor_tensor(x[:, t, :], x[:, t, :], ps[:, 4 + t, :], ALU.add)
                ins.then_inc(x_ok.sem, 1)

            def cross(k):
                N = B * NPAIR
                norm([2, 6][k])
                dve.wait_ge(*xn_ok([2, 6][k], NT))
                qh, qst = v("qh"), v("qst")
                dve.tensor_copy(qh[:, :, :], xn[:, :, :]).then_inc(qh_ok.sem, 1)
                dve.wait_ge(*qh_ok(k, 1))
                for h in range(2):
                    ins = dve.tensor_tensor(query_slots(qst, h)[:, :, :, 2 * XD:3 * XD], query_heads(xn, h),
                                            query_heads(qh, h).bitcast(F32), ALU.subtract)
                ins.then_inc(qst_ok.sem, 1)

                def maxima(n, qt):
                    b, pr = n // NPAIR, n % NPAIR
                    i = 4 * n + 2 * qt
                    for h in range(2):
                        dve.wait_ge(*xs_ok(k, i + h + 1))
                        if i:
                            dve.wait_ge(*xm_ok(k, i + h - 1))
                        dve.tensor_tensor_reduce(v("junk")[:, h, :], ps[:, 4 + h, :], v("mask_q")[:, qt, :], 1.0,
                                                 -3.0e38, ALU.add, ALU.max,
                                                 qst[:, b * QT + qt, 2 * pr + h, 3 * XD:3 * XD + 1])\
                           .then_inc(xm_ok.sem, 1)

                def masked(n):
                    i = 2 * n
                    dve.wait_ge(*xk_ok(k, i + 1))
                    if i >= 4:
                        dve.wait_ge(*pv_ok(k, i - 3))
                    dve.tensor_tensor(v("px%d" % (i % 4))[:, :, :, :].rearrange("p h k q -> p h (k q)"),
                                      ps[:, 0:2, :],
                                      v("mask_k")[:, 0:2, :].rearrange("p k q -> p (k q)").unsqueeze(1)
                                      .broadcast_to([P, 2, 2 * S]), ALU.add).then_inc(ms_ok.sem, 1)

                def divided(g):
                    dve.wait_ge(*ot2_ok(k, g + 1))
                    o = ps[:, 4, :].rearrange("p (n v) -> p n v", v=SLOT)
                    if g:
                        dve.wait_ge(*xo_ok(k, g))
                    step(dve.reciprocal(v("rden")[:, :], o[:, :, XD]))
                    dve.tensor_tensor(v("on")[:, :, :], o[:, :, 0:XD],
                                      v("rden")[:, :].unsqueeze(2).broadcast_to([P, QT * 2 * XR, XD]),
                                      ALU.mult).then_inc(on_ok.sem, 1)

                maxima(0, 0)
                maxima(0, 1)
                maxima(1, 0)
                for n in range(N):
                    if n + 1 < N:
                        maxima(n + 1, 1)
                    masked(n)
                    if n >= XR and n % XR == 1:
                        divided(n // XR - 1)
                    if n + 2 < N:
                        maxima(n + 2, 0)
                divided(N // XR - 1)

            def mixture(k):
                rt = [v("route")[:, i, :, :] for i in range(12)]
                small = v("ve")

                def spread(ap):
                    return ap.unsqueeze(2).broadcast_to([P, NT, E])

                norm([3, 5][k])
                both = ps[:, 4:6, :].rearrange("p b (t n) -> p (b t) n", t=2)
                logits = both[:, :, ER:ER + E]
                iota = v("iota8")[:, :].unsqueeze(1).broadcast_to([P, NT, E])
                m0, m1, m2 = small[:, 0:4], small[:, 4:8], small[:, 8:12]
                dve.wait_ge(*hl_ps(k, 1))
                step(dve.tensor_reduce(m0, logits, AX.X, ALU.max))
                dve.tensor_tensor(rt[0], logits, spread(m0), ALU.subtract).then_inc(le_ok.sem, 1)
                dve.wait_ge(*ee_ok(k, 1))
                step(dve.tensor_reduce(m0, rt[1], AX.X, ALU.add))
                step(dve.reciprocal(m0, m0))
                step(dve.tensor_tensor(rt[2], rt[1], spread(m0), ALU.mult))

                def first_max(p, m, eq, cand, one):
                    step(dve.tensor_reduce(m, p, AX.X, ALU.max))
                    step(dve.tensor_tensor(eq, p, spread(m), ALU.is_equal))
                    step(dve.scalar_tensor_tensor(cand, eq, -float(E), iota, ALU.mult, ALU.add))
                    step(dve.tensor_reduce(m0, cand, AX.X, ALU.min))
                    step(dve.tensor_scalar(m0, m0, float(E), None, ALU.add))
                    step(dve.tensor_tensor(one, iota, spread(m0), ALU.is_equal))

                first_max(rt[2], m1, rt[3], rt[4], rt[5])
                step(dve.scalar_tensor_tensor(rt[6], rt[5], -4.0, rt[2], ALU.mult, ALU.add))
                first_max(rt[6], m2, rt[7], rt[8], rt[9])
                step(dve.tensor_tensor(rt[10], rt[5], rt[9], ALU.add))
                step(dve.tensor_tensor(rt[10], rt[10], rt[2], ALU.mult))
                step(dve.tensor_tensor(m1, m1, m2, ALU.add))
                step(dve.reciprocal(m1, m1))
                step(dve.tensor_scalar(m1, m1, float(k + 1), None, ALU.mult))
                step(dve.tensor_tensor(rt[11], rt[10], spread(m1), ALU.mult))
                w = rt[11].unsqueeze(3).broadcast_to([P, NT, E, R])
                dve.tensor_tensor(v("hs")[:, :, :].rearrange("p t (e r) -> p t e r", r=R),
                                  both[:, :, 0:ER].rearrange("p t (e r) -> p t e r", r=R), w, ALU.mult)\
                   .then_inc(hw_ok.sem, 1)
                dve.wait_ge(*xb_ok(k, 1))
                for t in range(NT):
                    dve.wait_ge(*base_ok(k, t + 1))
                    ins = dve.tensor_tensor(x[:, t, :], x[:, t, :], ps[:, t, :], ALU.add)
                ins.then_inc(x_ok.sem, 1)

            def feed3():
                sc, inv = v("sc3"), v("isc3")
                inter, tops = v("inter"), v("route")[:, 0, :, :]

                def quantise(m, t, src, done):
                    step(dve.tensor_reduce(sc[:, m, t:t + 1], tops[:, t, 0:NB3] if m else src, AX.X, ALU.max,
                                           apply_absolute_value=True))
                    step(dve.tensor_scalar(sc[:, m, t:t + 1], sc[:, m, t:t + 1], 1.0 / QMAX, QEPS,
                                           ALU.mult, ALU.max))
                    step(dve.reciprocal(inv[:, m, t:t + 1], sc[:, m, t:t + 1]))
                    step(dve.tensor_scalar(src, src, inv[:, m, t:t + 1], MAGIC, ALU.mult, ALU.add))
                    dve.tensor_scalar(src, src, MAGIC + QMAX, MAGIC - QMAX - 1, ALU.min, ALU.max)\
                       .then_inc(done.sem, 1)

                norm(7)
                for t in range(NT):
                    dve.wait_ge(*xn_ok(7, t + 1))
                    quantise(0, t, xn[:, t, :], xq_ok)
                for blk in range(NB3):
                    for t in range(NT):
                        i = blk * NT + t
                        dve.wait_ge(*si_ok(0, i + 1))
                        dve.scalar_tensor_tensor(inter[:, t, blk * W3:(blk + 1) * W3], ps[:, 2 + i % 2, 0:W3],
                                                 sc[:, 0, t:t + 1], v("sil%d" % (i % 2))[:, :], ALU.mult, ALU.mult)\
                           .then_inc(in_ok.sem, 1)
                        dve.wait_ge(*in_ok(0, i + 1))
                        step(dve.tensor_reduce(tops[:, t, blk:blk + 1], inter[:, t, blk * W3:(blk + 1) * W3], AX.X,
                                               ALU.max, apply_absolute_value=True))
                        if blk == NB3 - 1:
                            quantise(1, t, inter[:, t, :], iq_ok)
                for t in range(NT):
                    dve.wait_ge(*dn_ok(0, 4 * NT + t + 1))
                    dve.scalar_tensor_tensor(x[:, t, :], ps[:, DBANK[t], :], sc[:, 1, t:t + 1], x[:, t, :],
                                             ALU.mult, ALU.add).then_inc(result_ok.sem, 1)

            dve.wait_ge(*ident_ok(0, 1))
            dve.tensor_copy(identr[:, :], ident[:, :]).then_inc(constr.sem, 1)
            dve.tensor_copy(v("causal")[:, :], v("causal0")[:, :]).then_inc(constr.sem, 1)
            rat(0)
            feed0()
            cross(0)
            mixture(0)
            rat(1)
            mixture(1)
            cross(1)
            feed3()

        @block.gpsimd
        def _(pool):
            def step(ins):
                link(pool, "pool", ins)

            def inverse_root(a, b):
                step(pool.tensor_scalar(ve[:, a:b], mv[:, a:b, 1], EPS, None, ALU.add))
                return pool.tensor_tensor(rstd[:, a:b], ve[:, a:b], v("powc")[:, 0:b - a], ALU.pow)

            def norm(n, scale=None):
                for t in range(NT):
                    pool.wait_ge(*mv_ok(n, t + 1))
                    ins = inverse_root(t, t + 1)
                    if scale is not None:
                        step(ins)
                        ins = pool.tensor_scalar(rstd[:, t:t + 1], rstd[:, t:t + 1], scale, None, ALU.mult)
                    ins.then_inc(rstd_ok.sem, 1)

            def rat_read(k, half, nout):
                for t in range(NT):
                    pool.wait_ge(*ymv_ok(2 * k + half, t + 1))
                    inverse_root(t * nout, (t + 1) * nout).then_inc(yrstd_ok.sem, 1)

            def rat_pads(k):
                qks, vs_ = v("qks%d" % k), v("vs%d" % k)
                if k:
                    pool.wait_ge(*x_ok(3, 1))
                    pool.memset(qks[:, :, :, :, :], 0.0)
                step(pool.memset(vs_[:, :, :, :], 0.0))
                pool.memset(qks[:, :, 1, :, 3 * HD:3 * HD + 1], -1.0)
                pool.memset(vs_[:, :, :, HD:HD + 1], 1.0).then_inc(pads.sem, 1)

            def rat_attention(k):
                for j in range(2 * B * NG):
                    half = 2 * (j % 2)
                    pool.wait_ge(*p_ok(k, j + 1))
                    for c in (0, 2 * P):
                        m = v("p%d%d" % (k, j // 2 % 2))[:, half:half + 2, c:c + P]
                        ins = pool.affine_select(out=m, in_=m, pattern=[[0, 2], [1, P]], compare_op=ALU.is_ge,
                                                 fill=0.0, base=0, channel_multiplier=-1)
                    ins.then_inc(pm_ok.sem, 1)

            def rat_write(k, half):
                i = 2 * k + half
                sp, ab, os_ = v("sp%d" % k), v("ab%d" % k), v("os%d" % k)
                pool.wait_ge(*sp_ok(i, 1))
                for t in range(NT):
                    delta = sp[:, t, AS:AS + H]
                    pool.tensor_tensor(
                        v("u%d" % k)[:, t, :, :].rearrange("p (s r) c -> p s r c", s=HS),
                        delta.rearrange("p (s r) -> p s r", s=HS).unsqueeze(3).broadcast_to([P, HS, RH, C3]),
                        sp[:, t, 0:AS].rearrange("p (r c) -> p r c", c=C3).unsqueeze(1)
                        .broadcast_to([P, HS, RH, C3]), ALU.mult).then_inc(u_ok.sem, 1)
                pool.wait_ge(*os_ok(i, 1))
                for t in range(0, NT, 2):
                    ts = slice(t, t + 2)
                    last = xn[:, ts, :].rearrange("p t (h c) -> p t h c", c=C)[:, :, :, C3]
                    skip = v("silu%d0" % k)[:, t * P:(t + 2) * P].rearrange("p (t h) -> p t h", t=2)
                    step(pool.tensor_tensor(
                        skip.rearrange("p t (s r) -> p t s r", s=HS),
                        sp[:, ts, AS:AS + H].rearrange("p t (s r) -> p t s r", s=HS),
                        ab[:, ts, 2 * AS:NAB].unsqueeze(2).broadcast_to([P, 2, HS, RH]), ALU.mult))
                    step(pool.tensor_tensor(skip, skip, os_[:, ts, :], ALU.mult))
                    pool.tensor_tensor(last, last, skip, ALU.add).then_inc(ah_ok.sem, 2)
                if half:
                    for t in range(NT // 2):
                        pool.wait_ge(*hid_ok(k, NT + t + 1))
                        pool.tensor_tensor(x[:, t, :], x[:, t, :], xn[:, t, :], ALU.add).then_inc(xa_ok.sem, 1)

            def convert(m):
                src, dst = (("gq", "gi"), ("uq", "ui"), ("dq", "di"))[m]
                pool.wait_ge(*q_in[m](0, 16 * DC))
                pool.tensor_scalar(v(dst)[:, :, :], v(src)[:, :, :], -QZERO, None, ALU.add).then_inc(qi_ok.sem, 1)

            def rat(k):
                if k == 0:
                    pool.memset(v("qks0")[:, :, :, :, :], 0.0)
                norm(RATN[k])
                rat_read(k, 0, 3)
                rat_pads(k)
                if k == 0:
                    convert(0)
                    convert(1)
                rat_attention(k)
                rat_write(k, 0)
                rat_read(k, 1, 2)
                if k == 0:
                    convert(2)
                rat_write(k, 1)

            def feed0():
                norm(1)
                pool.wait_ge(*ff_in(0, 16 * 8))
                for m in (v("gsc")[:, :, :], v("dsc")[:, :]):
                    step(pool.tensor_scalar(m, m, QSTEP, None, ALU.mult))
                dA, dB, last = v("dA"), v("dB"), slice(2 * R0, 3 * R0)
                pool.wait_ge(*fh_ok(0, 1))
                step(pool.tensor_tensor(dB[last, :], v("dBraw")[last, :], dB[last, :].bitcast(F32), ALU.subtract))
                pool.tensor_tensor(dA[:, :, R0:2 * R0], v("dAraw")[:, :, :], dA[:, :, 0:R0].bitcast(F32),
                                   ALU.subtract).then_inc(fb_ok.sem, 1)
                pool.wait_ge(*fb_ok(0, 2))
                for f in range(F0):
                    w = F0W[f]
                    pool.wait_ge(*hh_ok(0, f + 1))
                    pool.tensor_tensor(v("hl")[0:w, f, :], v("gp")[0:w, f % 2, :], v("hh")[0:w, f, :].bitcast(F32),
                                       ALU.subtract).then_inc(hl_ok.sem, 1)

            def context():
                kst, vx, ch, cx = v("kst"), v("vx"), v("ch"), v("ctx")
                pool.wait_ge(*d_ok(0, 1))
                pool.tensor_copy(ch[:, :, :], cx[:, :, :]).then_inc(chi_ok.sem, 1)
                step(pool.memset(kst[:, :, :, 3 * XD:XSLOT], 0.0))
                hi = ch[:, :, :].rearrange("p j (g d) -> p j g d", d=XD)
                raw = cx[:, :, :].rearrange("p j (g d) -> p j g d", d=XD)
                hif = ch[:, :, :].bitcast(F32).rearrange("p j (g d) -> p j g d", d=XD)
                pool.memset(kst[:, :, :, 3 * XD:XK], -1.0)
                pool.wait_ge(*chi_ok(0, 1))
                pool.tensor_tensor(kst[:, :, :, XD:2 * XD], raw, hif, ALU.subtract).then_inc(kst_ok.sem, 1)
                pool.memset(vx[:, :, :, XV:SLOT], 0.0)
                pool.memset(vx[:, :, :, XD:XV], 1.0)
                pool.tensor_copy(vx[:, :, :, 0:XD], raw).then_inc(vx_ok.sem, 1)

            def cross(k):
                N = B * NPAIR
                norm([2, 6][k], scale=float(XD) ** -0.5)
                pool.memset(v("qst")[:, :, :, 3 * XD:XSLOT], 0.0).then_inc(qst_ok.sem, 1)
                mh = v("mh")
                mask = v("mask_k")[:, 2:KT, :]
                step(pool.tensor_copy(v("mkh")[:, :, :], mask))
                pool.tensor_tensor(v("mkl")[:, :, :], mask, v("mkh")[:, :, :].bitcast(F32), ALU.subtract)\
                    .then_inc(mk_ok.sem, 1)

                def parts(n):
                    b, pr = n // NPAIR, n % NPAIR
                    top = v("qst")[:, b * QT:(b + 1) * QT, 2 * pr:2 * pr + 2, 3 * XD:XK]
                    pool.wait_ge(*xm_ok(k, 4 * n + 4))
                    if n:
                        pool.wait_ge(*ml_ok(k, n))
                    pool.tensor_copy(mh[:, :, :], top[:, :, :, 0]).then_inc(mh_ok.sem, 1)
                    pool.wait_ge(*mh_ok(k, n + 1))
                    pool.tensor_tensor(top[:, :, :, 1], top[:, :, :, 0], mh[:, :, :].bitcast(F32), ALU.subtract)\
                        .then_inc(ml_ok.sem, 1)

                def added(g):
                    b, gp = g // (XG // 2), g % (XG // 2)
                    pool.wait_ge(*on_ok(k, g + 1))
                    for qt in range(QT):
                        xv = x[:, b * QT + qt, gp * 2 * XR * XD:(gp + 1) * 2 * XR * XD]\
                            .rearrange("p (h m d) -> p m h d", h=2, m=2)
                        on = v("on")[:, :, :].rearrange("p (m q h e) d -> p m q h (e d)", m=2, q=QT, h=2)
                        ins = pool.tensor_tensor(xv, xv, on[:, :, qt, :, :], ALU.add)
                    ins.then_inc(xo_ok.sem, 1)

                for n in range(N):
                    parts(n)
                    if n > XR and n % XR == 2:
                        added(n // XR - 1)
                added(N // XR - 1)
                pool.wait_ge(*xo_ok(k, N // XR))
                pool.sem_inc(x_ok.sem, 1)

            def mixture(k):
                norm([3, 5][k])
                pool.wait_ge(*xn_ok([3, 5][k], NT))
                pool.wait_ge(*mix_in(k, 32))
                bias = v("mw")[:, MP["b"][0]:MP["b"][1]].unsqueeze(1).broadcast_to([P, NT, D])
                pool.tensor_tensor(x[:, :, :], x[:, :, :], bias, ALU.add).then_inc(xb_ok.sem, 1)

            def feed3():
                norm(7)
                for i, (m, at, n) in enumerate(ITEMS):
                    pool.wait_ge(*wc_ok(0, i + 1))
                    s = i % WS
                    pool.tensor_tensor(v("wlo%d" % s)[:, 0:n], v("wraw%d" % s)[:, 0:n],
                                       v("whi%d" % s)[:, 0:n].bitcast(F32), ALU.subtract).then_inc(wl_ok.sem, 1)

            c0, sel = v("causal0"), v("sel")
            pool.memset(ident[:, :], 0.0)
            pool.memset(c0[:, :], 0.0)
            pool.memset(sel[:, :], 1.0)
            pool.memset(v("tiny")[:, :], 0.0)
            pool.memset(v("powc")[:, :], -0.5)
            step(pool.memset(v("dl")[:, :], 1.0))
            for c in (0, 2 * P):
                pool.affine_select(out=c0[:, c:c + P], in_=c0[:, c:c + P], pattern=[[-1, P]], compare_op=ALU.is_ge,
                                   fill=-1e30, base=0, channel_multiplier=1)
            pool.affine_select(out=ident[:, :], in_=ident[:, :], pattern=[[-1, P]], compare_op=ALU.not_equal,
                               fill=1.0, base=0, channel_multiplier=1).then_inc(ident_ok.sem, 1)
            pool.iota(v("iota8")[:, :], [[1, E]], base=-E, channel_multiplier=0,
                      allow_small_or_imprecise_dtypes=True)
            step(pool.affine_select(out=sel[:, :], in_=sel[:, :], pattern=[[-C, SLOT]], compare_op=ALU.is_ge,
                                    fill=0.0, base=0, channel_multiplier=1))
            pool.affine_select(out=sel[:, :], in_=sel[:, :], pattern=[[C, SLOT]], compare_op=ALU.is_ge,
                               fill=0.0, base=C - 1, channel_multiplier=-1).then_inc(const_ok.sem, 1)
            rat(0)
            feed0()
            context()
            cross(0)
            mixture(0)
            rat(1)
            mixture(1)
            cross(1)
            feed3()


def kernel(**inputs):
    import numpy as _np
    import concourse.bacc as _bacc
    from concourse import mybir as _mybir
    from concourse.bass_utils import run_bass_kernel_spmd as _run

    g = {n: _np.asarray(w) for n, w in inputs.items()}
    cat = _np.concatenate

    def tiles(m):
        n = m.shape[0] // P
        return m.reshape(n, P, -1).transpose(1, 0, 2).reshape(P, -1)

    def padded(m):
        return cat([m, _np.zeros((F0 * P - m.shape[0],) + m.shape[1:], m.dtype)])

    def thrice(m):
        return cat([m, m, m], axis=0)

    arrays = {
        "x": g["x"].reshape(T, D), "pos": tiles(g["pos_BxS"].reshape(T, 1)),
        "ctx": g["ctx_1024"].reshape(B * S2, CD), "mask": g["mask_SxS2_ff0"], "maskT": g["mask_SxS2_ff0"].T,
        "gq": g["L0_ffn_gate_q"].T, "uq": g["L0_ffn_up_q"].T, "dq": padded(g["L0_ffn_down_q"].T),
        "gA": tiles(cat([g["L0_ffn_gate_A"]] * 3, axis=1)).reshape(P, DC, 3 * R0),
        "uA": tiles(cat([g["L0_ffn_up_A"]] * 3, axis=1)).reshape(P, DC, 3 * R0),
        "gBraw": thrice(g["L0_ffn_gate_B"]), "uBraw": thrice(g["L0_ffn_up_B"]), "dBraw": thrice(g["L0_ffn_down_B"]),
        "dAraw": tiles(padded(g["L0_ffn_down_A"])).reshape(P, F0, R0),
        "gsc": cat([tiles(padded(g["L0_ffn_%s_scale" % n][:, None])) for n in ("gate", "up")], 1).reshape(P, 2, F0),
        "dsc": g["L0_ffn_down_scale"].reshape(1, D),
        "wg": g["L3_ffn_w_gate"].T, "wu": g["L3_ffn_w_up"].T, "wd": g["L3_ffn_w_down"].T,
    }
    for k, name in enumerate(("L0_xattn_", "L2_xattn_")):
        def w(n):
            return g[name + n]

        def read(half):
            return tiles(w(half + "_read_w").transpose(0, 2, 1).reshape(H * C, -1))

        def per_channel(n):
            return w(n).reshape(-1, H).T

        def both(half):
            return cat([w(half + "_wod_w"), w(half + "_wab_w")]).T

        arrays["rw%d" % k] = cat([
            read("attn"), per_channel("attn_read_g"), per_channel("attn_read_b"),
            w("qkv_w").transpose(2, 0, 1).reshape(H, 3 * H), both("attn"),
            read("mlp"), per_channel("mlp_read_g"), per_channel("mlp_read_b"), tiles(both("mlp"))], axis=1)
        arrays["rrow%d" % k] = _np.stack([w("attn_wab_b"), w("mlp_wab_b")])
        arrays["du%d" % k] = _np.stack([cat([w(h + "_du_w").T, w(h + "_du_b")[None]]) for h in ("attn", "mlp")], 1)
    for k, (pre, gate, low, up) in enumerate((("L1_ffn_", "W_gate", "A", "B"),
                                              ("L2_ffn_", "W_router", "lora_A", "lora_B"))):
        ag = cat([g[pre + low].reshape(ER, D), g[pre + gate]]).T
        arrays["mw%d" % k] = cat([tiles(g[pre + "W_base"].T), tiles(ag),
                                  _np.broadcast_to(g[pre + "b_base"], (P, D))], axis=1)
        arrays["mB%d" % k] = g[pre + up].transpose(0, 2, 1).reshape(ER, D)

    nc = _bacc.Bacc("TRN2", target_bir_lowering=False, num_devices=1)
    feeds, aps = {}, {}
    for name, m in arrays.items():
        m = _np.ascontiguousarray(m)
        feeds["in_" + name] = m
        aps[name] = nc.dram_tensor("in_" + name, m.shape, _mybir.dt.from_np(m.dtype), kind="ExternalInput").ap()
    out = nc.dram_tensor("out_0_dram", (T, D), F32, kind="ExternalOutput").ap()
    program(nc, aps, out)
    r = _run(nc, [feeds], core_ids=[0])
    return r.results[0]["out_0_dram"].reshape(B, S, D)
```
